# Optimizing a Trainium2 kernel written in Bass

```python
import numpy as np
import jax
import jax.numpy as jnp

def _softmax(x, axis=-1):
    return jax.nn.softmax(x, axis=axis)

def _gelu(x):
    return jax.nn.gelu(x, approximate=True)

def _silu(x):
    return jax.nn.silu(x)

def _sigmoid(x):
    return jax.nn.sigmoid(x)

def _layernorm(x, axis=-1, eps=1e-05):
    m = jnp.mean(x, axis=axis, keepdims=True)
    v = jnp.var(x, axis=axis, keepdims=True)
    return (x - m) / jnp.sqrt(v + eps)

def _scatter_add(tgt, idx, src, axis=0):
    return tgt.at[idx].add(src)

def _segment_sum(src, seg, n):
    return jax.ops.segment_sum(src, seg, n)
kernel_name = 'mk_adaln_d2_jaxref_r8_e8c1d2'

def setup_inputs(seed: int=0):
    np.random.seed(seed)
    _w = jnp.asarray

    def _L0_attn_setup():
        import jax, jax.numpy as jnp
        import numpy as np
        from jax import lax
        D_MODEL = 128
        D_STATE = 16
        D_CONV = 4
        EXPAND = 2
        D_INNER = D_MODEL * EXPAND
        BATCH = 2
        SEQ = 256

        def _forward(x, W_in, conv_w, conv_b, W_x, W_dt, b_dt, A_log, D_param, W_out):
            B, L, _ = x.shape
            xz = x @ W_in
            xc, z = jnp.split(xz, 2, axis=-1)
            xc_t = jnp.transpose(xc, (0, 2, 1))
            xc_t = lax.conv_general_dilated(xc_t, conv_w, window_strides=(1,), padding=[(D_CONV - 1, 0)], feature_group_count=D_INNER, dimension_numbers=('NCH', 'OIH', 'NCH'))
            xc_t = xc_t + conv_b[None, :, None]
            xc = jnp.transpose(xc_t, (0, 2, 1))
            xc = jax.nn.silu(xc)
            x_dbl = xc @ W_x
            dt_raw = x_dbl[..., :1]
            B_mat = x_dbl[..., 1:1 + D_STATE]
            C_mat = x_dbl[..., 1 + D_STATE:]
            dt = jax.nn.softplus(dt_raw @ W_dt + b_dt)
            A = -jnp.exp(A_log)

            def step(h, inp):
                x_t, dt_t, B_t, C_t = inp
                dA = jnp.exp(dt_t[..., None] * A)
                h = dA * h + dt_t[..., None] * B_t[:, None, :] * x_t[..., None]
                y = jnp.einsum('bds,bs->bd', h, C_t)
                return (h, y)
            xs = (jnp.moveaxis(xc, 1, 0), jnp.moveaxis(dt, 1, 0), jnp.moveaxis(B_mat, 1, 0), jnp.moveaxis(C_mat, 1, 0))
            h0 = jnp.zeros((B, D_INNER, D_STATE), dtype=x.dtype)
            _, ys = lax.scan(step, h0, xs)
            y = jnp.moveaxis(ys, 0, 1) + D_param * xc
            y = y * jax.nn.silu(z)
            return y @ W_out
        key = jax.random.key(seed)
        ks = jax.random.split(key, 9)
        s_in = 1.0 / np.sqrt(D_MODEL)
        s_x = 1.0 / np.sqrt(D_INNER)
        x = jax.random.normal(ks[0], (BATCH, SEQ, D_MODEL), dtype=jnp.float32)
        W_in = jax.random.normal(ks[1], (D_MODEL, 2 * D_INNER), dtype=jnp.float32) * s_in
        conv_w = jax.random.normal(ks[2], (D_INNER, 1, D_CONV), dtype=jnp.float32) * 0.5
        conv_b = jax.random.normal(ks[3], (D_INNER,), dtype=jnp.float32) * 0.1
        W_x = jax.random.normal(ks[4], (D_INNER, 2 * D_STATE + 1), dtype=jnp.float32) * s_x
        W_dt = jax.random.normal(ks[5], (1, D_INNER), dtype=jnp.float32)
        b_dt = jax.random.normal(ks[6], (D_INNER,), dtype=jnp.float32) * 0.1
        A_log = jnp.broadcast_to(jnp.log(jnp.arange(1, D_STATE + 1, dtype=jnp.float32)), (D_INNER, D_STATE))
        D_param = jnp.ones((D_INNER,), dtype=jnp.float32)
        W_out = jax.random.normal(ks[7], (D_INNER, D_MODEL), dtype=jnp.float32) * s_x
        return {'x': x, 'W_in': W_in, 'conv_w': conv_w, 'conv_b': conv_b, 'W_x': W_x, 'W_dt': W_dt, 'b_dt': b_dt, 'A_log': A_log, 'D_param': D_param, 'W_out': W_out}
    _L0_attn_in = _L0_attn_setup()

    def _L0_ffn_setup():
        import jax, jax.numpy as jnp
        import numpy as np
        D = 128
        F = 128
        E = 8
        K = 2
        B, T = (2, 256)

        def _moe_forward(x, router_w, w1, w2, shared_gate_up, shared_down, shared_gate_w):
            b, t, d = x.shape
            xf = x.reshape(-1, d)
            n = xf.shape[0]
            logits = xf @ router_w
            probs = jax.nn.softmax(logits, axis=-1)
            topw, topi = jax.lax.top_k(probs, K)
            combine = jnp.zeros((n, E), dtype=probs.dtype).at[jnp.arange(n)[:, None], topi].add(topw)
            h = jax.nn.silu(jnp.einsum('nd,edf->nef', xf, w1))
            ye = jnp.einsum('nef,efd->ned', h, w2)
            routed = jnp.einsum('ne,ned->nd', combine, ye)
            gu = xf @ shared_gate_up
            gate, up = (gu[:, :F], gu[:, F:])
            shared = jax.nn.silu(gate) * up @ shared_down
            shared = jax.nn.sigmoid(xf @ shared_gate_w) * shared
            return (routed + shared).reshape(b, t, d)
        key = jax.random.key(seed)
        ks = jax.random.split(key, 7)
        std = 0.02
        x = jax.random.normal(ks[0], (B, T, D), dtype=jnp.float32)
        router_w = jax.random.normal(ks[1], (D, E), dtype=jnp.float32) * std
        w1 = jax.random.normal(ks[2], (E, D, F), dtype=jnp.float32) * std
        w2 = jax.random.normal(ks[3], (E, F, D), dtype=jnp.float32) * std
        shared_gate_up = jax.random.normal(ks[4], (D, 2 * F), dtype=jnp.float32) * std
        shared_down = jax.random.normal(ks[5], (F, D), dtype=jnp.float32) * std
        shared_gate_w = jax.random.normal(ks[6], (D, 1), dtype=jnp.float32) * std
        return {'x': x, 'router_w': router_w, 'w1': w1, 'w2': w2, 'shared_gate_up': shared_gate_up, 'shared_down': shared_down, 'shared_gate_w': shared_gate_w}
    _L0_ffn_in = _L0_ffn_setup()
    _L0_c = _w((lambda *s: np.random.randn(*s).astype(np.float32) * 0.05)(8, 128))
    _L0_wmod = _w((lambda *s: np.random.randn(*s).astype(np.float32) * 0.05)(128, 6 * 128) * 128 ** (-0.5))

    def _L1_attn_setup():
        import jax, jax.numpy as jnp
        import numpy as np
        B, T, D, N, R = (2, 256, 128, 16, 64)
        key = jax.random.key(seed)
        ks = jax.random.split(key, 8)
        sc = 0.02
        return {'x': jax.random.normal(ks[0], (B, T, D), jnp.float32), 'W_in': jax.random.normal(ks[1], (2 * D, D), jnp.float32) * sc, 'conv_w': jax.random.normal(ks[2], (D, 3), jnp.float32) * sc, 'W_x': jax.random.normal(ks[3], (R + 2 * N, D), jnp.float32) * sc, 'W_dt': jax.random.normal(ks[4], (D, R), jnp.float32) * sc, 'b_dt': jnp.ones((D,), jnp.float32), 'A_log': jnp.full((D, N), -2.0, jnp.float32), 'D_param': jnp.ones((D,), jnp.float32), 'W_C': jax.random.normal(ks[5], (D, N), jnp.float32) * sc, 'W_out': jax.random.normal(ks[6], (D, D), jnp.float32) * sc}
    _L1_attn_in = _L1_attn_setup()

    def _L1_ffn_setup():
        import jax, jax.numpy as jnp
        import numpy as np
        TOP_K = 2
        key = jax.random.key(seed)
        k1, k2, k3 = jax.random.split(key, 3)
        B, S, H, E = (4, 256, 128, 8)
        x = jax.random.normal(k1, (B, S, H), dtype=jnp.float32)
        gate_w = jax.random.normal(k2, (E, H), dtype=jnp.float32) / np.sqrt(H)
        gate_b = jnp.zeros((E,), dtype=jnp.float32)
        expert_w = jax.random.normal(k3, (E, H, H), dtype=jnp.float32) / np.sqrt(H)
        expert_b = jnp.zeros((E, H), dtype=jnp.float32)
        return {'x': x, 'gate_w': gate_w, 'gate_b': gate_b, 'expert_w': expert_w, 'expert_b': expert_b}
    _L1_ffn_in = _L1_ffn_setup()
    _L1_c = _w((lambda *s: np.random.randn(*s).astype(np.float32) * 0.05)(8, 128))
    _L1_wmod = _w((lambda *s: np.random.randn(*s).astype(np.float32) * 0.05)(128, 6 * 128) * 128 ** (-0.5))
    _d = {'L0_attn_x': _L0_attn_in['x'], 'L0_attn_W_in': _L0_attn_in['W_in'], 'L0_attn_conv_w': _L0_attn_in['conv_w'], 'L0_attn_conv_b': _L0_attn_in['conv_b'], 'L0_attn_W_x': _L0_attn_in['W_x'], 'L0_attn_W_dt': _L0_attn_in['W_dt'], 'L0_attn_b_dt': _L0_attn_in['b_dt'], 'L0_attn_A_log': _L0_attn_in['A_log'], 'L0_attn_D_param': _L0_attn_in['D_param'], 'L0_attn_W_out': _L0_attn_in['W_out'], 'L0_ffn_router_w': _L0_ffn_in['router_w'], 'L0_ffn_w1': _L0_ffn_in['w1'], 'L0_ffn_w2': _L0_ffn_in['w2'], 'L0_ffn_shared_gate_up': _L0_ffn_in['shared_gate_up'], 'L0_ffn_shared_down': _L0_ffn_in['shared_down'], 'L0_ffn_shared_gate_w': _L0_ffn_in['shared_gate_w'], 'L0_c': _L0_c, 'L0_wmod': _L0_wmod, 'L1_attn_W_in': _L1_attn_in['W_in'], 'L1_attn_conv_w': _L1_attn_in['conv_w'], 'L1_attn_W_x': _L1_attn_in['W_x'], 'L1_attn_W_dt': _L1_attn_in['W_dt'], 'L1_attn_b_dt': _L1_attn_in['b_dt'], 'L1_attn_A_log': _L1_attn_in['A_log'], 'L1_attn_D_param': _L1_attn_in['D_param'], 'L1_attn_W_C': _L1_attn_in['W_C'], 'L1_attn_W_out': _L1_attn_in['W_out'], 'L1_ffn_gate_w': _L1_ffn_in['gate_w'], 'L1_ffn_gate_b': _L1_ffn_in['gate_b'], 'L1_ffn_expert_w': _L1_ffn_in['expert_w'], 'L1_ffn_expert_b': _L1_ffn_in['expert_b'], 'L1_c': _L1_c, 'L1_wmod': _L1_wmod}
    _x0 = _d['L0_attn_x']
    _d['L0_attn_x'] = jax.random.normal(jax.random.fold_in(jax.random.key(seed), 1), (8, 1024, 128), dtype=_x0.dtype)
    del _x0
    return _d

def reference(L0_attn_x, L0_attn_W_in, L0_attn_conv_w, L0_attn_conv_b, L0_attn_W_x, L0_attn_W_dt, L0_attn_b_dt, L0_attn_A_log, L0_attn_D_param, L0_attn_W_out, L0_ffn_router_w, L0_ffn_w1, L0_ffn_w2, L0_ffn_shared_gate_up, L0_ffn_shared_down, L0_ffn_shared_gate_w, L0_c, L0_wmod, L1_attn_W_in, L1_attn_conv_w, L1_attn_W_x, L1_attn_W_dt, L1_attn_b_dt, L1_attn_A_log, L1_attn_D_param, L1_attn_W_C, L1_attn_W_out, L1_ffn_gate_w, L1_ffn_gate_b, L1_ffn_expert_w, L1_ffn_expert_b, L1_c, L1_wmod):

    def _L0_attn_ref(x, W_in, conv_w, conv_b, W_x, W_dt, b_dt, A_log, D_param, W_out):
        import jax, jax.numpy as jnp
        import numpy as np
        from jax import lax
        D_MODEL = 128
        D_STATE = 16
        D_CONV = 4
        EXPAND = 2
        D_INNER = D_MODEL * EXPAND
        BATCH = 2
        SEQ = 256

        def _forward(x, W_in, conv_w, conv_b, W_x, W_dt, b_dt, A_log, D_param, W_out):
            B, L, _ = x.shape
            xz = x @ W_in
            xc, z = jnp.split(xz, 2, axis=-1)
            xc_t = jnp.transpose(xc, (0, 2, 1))
            xc_t = lax.conv_general_dilated(xc_t, conv_w, window_strides=(1,), padding=[(D_CONV - 1, 0)], feature_group_count=D_INNER, dimension_numbers=('NCH', 'OIH', 'NCH'))
            xc_t = xc_t + conv_b[None, :, None]
            xc = jnp.transpose(xc_t, (0, 2, 1))
            xc = jax.nn.silu(xc)
            x_dbl = xc @ W_x
            dt_raw = x_dbl[..., :1]
            B_mat = x_dbl[..., 1:1 + D_STATE]
            C_mat = x_dbl[..., 1 + D_STATE:]
            dt = jax.nn.softplus(dt_raw @ W_dt + b_dt)
            A = -jnp.exp(A_log)

            def step(h, inp):
                x_t, dt_t, B_t, C_t = inp
                dA = jnp.exp(dt_t[..., None] * A)
                h = dA * h + dt_t[..., None] * B_t[:, None, :] * x_t[..., None]
                y = jnp.einsum('bds,bs->bd', h, C_t)
                return (h, y)
            xs = (jnp.moveaxis(xc, 1, 0), jnp.moveaxis(dt, 1, 0), jnp.moveaxis(B_mat, 1, 0), jnp.moveaxis(C_mat, 1, 0))
            h0 = jnp.zeros((B, D_INNER, D_STATE), dtype=x.dtype)
            _, ys = lax.scan(step, h0, xs)
            y = jnp.moveaxis(ys, 0, 1) + D_param * xc
            y = y * jax.nn.silu(z)
            return y @ W_out
        return _forward(x, W_in, conv_w, conv_b, W_x, W_dt, b_dt, A_log, D_param, W_out)

    def _L0_ffn_ref(x, router_w, w1, w2, shared_gate_up, shared_down, shared_gate_w):
        import jax, jax.numpy as jnp
        import numpy as np
        D = 128
        F = 128
        E = 8
        K = 2
        B, T = (2, 256)

        def _moe_forward(x, router_w, w1, w2, shared_gate_up, shared_down, shared_gate_w):
            b, t, d = x.shape
            xf = x.reshape(-1, d)
            n = xf.shape[0]
            logits = xf @ router_w
            probs = jax.nn.softmax(logits, axis=-1)
            topw, topi = jax.lax.top_k(probs, K)
            combine = jnp.zeros((n, E), dtype=probs.dtype).at[jnp.arange(n)[:, None], topi].add(topw)
            h = jax.nn.silu(jnp.einsum('nd,edf->nef', xf, w1))
            ye = jnp.einsum('nef,efd->ned', h, w2)
            routed = jnp.einsum('ne,ned->nd', combine, ye)
            gu = xf @ shared_gate_up
            gate, up = (gu[:, :F], gu[:, F:])
            shared = jax.nn.silu(gate) * up @ shared_down
            shared = jax.nn.sigmoid(xf @ shared_gate_w) * shared
            return (routed + shared).reshape(b, t, d)
        return _moe_forward(x, router_w, w1, w2, shared_gate_up, shared_down, shared_gate_w)

    def _L1_attn_ref(x, W_in, conv_w, W_x, W_dt, b_dt, A_log, D_param, W_C, W_out):
        import jax, jax.numpy as jnp
        import numpy as np
        B, T, D, N, R = (2, 256, 128, 16, 64)
        xz = jnp.einsum('btd,ed->bte', x, W_in)
        xc, z = jnp.split(xz, 2, axis=-1)
        xp = jnp.pad(xc, ((0, 0), (1, 1), (0, 0)))
        xconv = xp[:, :-2] * conv_w[:, 0] + xp[:, 1:-1] * conv_w[:, 1] + xp[:, 2:] * conv_w[:, 2]
        xs = jax.nn.silu(xconv)
        x_dbl = jnp.einsum('btd,ed->bte', xs, W_x)
        dt_param = x_dbl[..., :R]
        Bp = x_dbl[..., R:R + N]
        Cp = x_dbl[..., R + N:]
        dt = jax.nn.softplus(dt_param @ W_dt.T + b_dt) + 1e-05
        A_disc = jnp.exp(-jnp.exp(A_log)[None, None] * dt[..., None])
        Bx = Bp[:, :, None, :] * dt[..., None] * xs[..., None]
        C = Cp @ W_C.T

        def step(s, inp):
            A_t, Bx_t = inp
            s = A_t * s + Bx_t
            return (s, s.sum(-1))
        s0 = jnp.zeros((x.shape[0], D, N), x.dtype)
        _, ssum = jax.lax.scan(step, s0, (A_disc.transpose(1, 0, 2, 3), Bx.transpose(1, 0, 2, 3)))
        ssum = ssum.transpose(1, 0, 2)
        y = C * ssum + D_param * xs
        return jnp.einsum('btd,ed->bte', y, W_out) * jax.nn.silu(z)

    def _L1_ffn_ref(x, gate_w, gate_b, expert_w, expert_b):
        import jax, jax.numpy as jnp
        import numpy as np
        TOP_K = 2
        gates = jax.nn.softmax(jnp.einsum('bsh,eh->bse', x, gate_w) + gate_b, axis=-1)
        top_gates, top_idx = jax.lax.top_k(gates, TOP_K)
        expert_out = jnp.einsum('bsh,eoh->bseo', x, expert_w) + expert_b
        selected = jnp.take_along_axis(expert_out, top_idx[..., None], axis=2)
        return (selected * top_gates[..., None]).sum(axis=2)
    x = L0_attn_x
    mod = (_silu(L0_c) @ L0_wmod).reshape(L0_c.shape[0], 6, 1, -1)
    sa, ca, ga, sb, cb, gb = (mod[:, 0], mod[:, 1], mod[:, 2], mod[:, 3], mod[:, 4], mod[:, 5])
    ga = (2 * (ga >= 0) - 1) * jnp.maximum(jnp.abs(ga), 0.25)
    gb = (2 * (gb >= 0) - 1) * jnp.maximum(jnp.abs(gb), 0.25)
    h = _layernorm(x, axis=-1) * (1 + ca) + sa
    x = x + ga * _L0_attn_ref(h, L0_attn_W_in, L0_attn_conv_w, L0_attn_conv_b, L0_attn_W_x, L0_attn_W_dt, L0_attn_b_dt, L0_attn_A_log, L0_attn_D_param, L0_attn_W_out)
    h = _layernorm(x, axis=-1) * (1 + cb) + sb
    x = x + gb * _L0_ffn_ref(h, L0_ffn_router_w, L0_ffn_w1, L0_ffn_w2, L0_ffn_shared_gate_up, L0_ffn_shared_down, L0_ffn_shared_gate_w)
    mod = (_silu(L1_c) @ L1_wmod).reshape(L1_c.shape[0], 6, 1, -1)
    sa, ca, ga, sb, cb, gb = (mod[:, 0], mod[:, 1], mod[:, 2], mod[:, 3], mod[:, 4], mod[:, 5])
    ga = (2 * (ga >= 0) - 1) * jnp.maximum(jnp.abs(ga), 0.25)
    gb = (2 * (gb >= 0) - 1) * jnp.maximum(jnp.abs(gb), 0.25)
    h = _layernorm(x, axis=-1) * (1 + ca) + sa
    x = x + ga * _L1_attn_ref(h, L1_attn_W_in, L1_attn_conv_w, L1_attn_W_x, L1_attn_W_dt, L1_attn_b_dt, L1_attn_A_log, L1_attn_D_param, L1_attn_W_C, L1_attn_W_out)
    h = _layernorm(x, axis=-1) * (1 + cb) + sb
    x = x + gb * _L1_ffn_ref(h, L1_ffn_gate_w, L1_ffn_gate_b, L1_ffn_expert_w, L1_ffn_expert_b)
    return x

_drawn_inputs = setup_inputs


def setup_inputs(seed=0):
    import zlib

    import numpy as np

    out = dict(_drawn_inputs(seed))
    spreads = {'L0_attn_D_param': (1.0, 0.6),
     'L1_attn_b_dt': (1.0, 0.2),
     'L1_attn_A_log': (-2.0, 0.6),
     'L1_attn_D_param': (1.0, 0.6),
     'L1_ffn_gate_b': (0.0, 1.187),
     'L1_ffn_expert_b': (0.0, 0.738)}
    factors = {'L0_attn_b_dt': 5.891,
     'L0_ffn_router_w': 8.0,
     'L0_ffn_w1': 8.0,
     'L0_ffn_w2': 8.0,
     'L0_ffn_shared_gate_up': 8.0,
     'L0_ffn_shared_down': 8.0,
     'L0_ffn_shared_gate_w': 8.0,
     'L1_attn_W_in': 8.0,
     'L1_attn_conv_w': 8.0,
     'L1_attn_W_x': 8.0,
     'L1_attn_W_C': 8.0,
     'L1_attn_W_out': 8.0}
    for name, (base, spread) in spreads.items():
        noise = np.random.default_rng([zlib.crc32(name.encode()), seed]).standard_normal(out[name].shape)
        drawn = base * np.exp(spread * noise) if base else spread * noise
        out[name] = jnp.asarray(drawn.astype(out[name].dtype))
    for name, factor in factors.items():
        out[name] = (out[name] * factor).astype(out[name].dtype)
    return out
```

```python
from contextlib import ExitStack

import concourse.bass as bass
from concourse import mybir

F32 = mybir.dt.float32
ALU = mybir.AluOpType
ACT = mybir.ActivationFunctionType
AX = mybir.AxisListType

P = 128
NB = 8
T = 1024
D = 128
DI = 256
NS = 16
NE = 8
R1 = 64
TILES = T // P
CH = 512
NC = T // CH
TPC = CH // P
H0 = DI // P
SHI = 4
SLO = NS // SHI
R = P // SLO
KPH = P // R
TAPS0 = 4
TAPS1 = 3
GATE_MIN = 0.25
EPS = 1e-5
MB = 3
HALF = KPH * SHI
LAG_Y = 4
LAG_GATE = 3
LAG_OUT = 4
LAG_RES = 8
LAG1 = (3, 2, 6, 6, 9)
HR = 4
CR = 4


def adaln_blocks(nc, x_in, w, rows_dram, comb_dram, out):
    with ExitStack() as ctx:
        def sb(name, shape):
            return ctx.enter_context(nc.sbuf_tensor(name, shape, F32))

        def ps(name, shape):
            return ctx.enter_context(nc.psum_tensor(name, shape, F32))

        per = {}
        counted = []

        def sem(name, per_sequence):
            s = ctx.enter_context(nc.semaphore(name))
            per[s.name] = per_sequence
            if per_sequence:
                counted.append(s)
            return s

        def at(s, b, n):
            return b * per[s.name] + n + 1

        w_in0 = sb("w_in0", [P, 2 * DI])
        conv_b0 = sb("conv_b0", [P, H0])
        w_x0 = sb("w_x0", [P, H0, 1 + 2 * NS])
        w_dt0 = sb("w_dt0", [1, DI])
        b_dt0 = sb("b_dt0", [P, H0])
        a_log0 = sb("a_log0", [P, H0 * KPH, SHI])
        d0 = sb("d0", [P, H0])
        w_out0 = sb("w_out0", [P, H0, D])
        router = sb("router", [P, NE + 1])
        w1 = sb("w1", [P, NE + 2, P])
        w2 = sb("w2", [P, NE + 1, D])
        w_in1 = sb("w_in1", [P, 2 * D])
        w_x1dt = sb("w_x1dt", [R1, D])
        w_x1b = sb("w_x1b", [P, NS])
        w_x1c = sb("w_x1c", [NS, D])
        w_dt1 = sb("w_dt1", [R1, D])
        w_c1 = sb("w_c1", [NS, D])
        b_dt1 = sb("b_dt1", [P, 1])
        a_log1 = sb("a_log1", [P, KPH, SHI])
        d1 = sb("d1", [P, 1])
        w_out1 = sb("w_out1", [P, D])
        gate_w1 = sb("gate_w1", [P, NE])
        gate_b1 = sb("gate_b1", [P, NE])
        w_e1 = sb("w_e1", [P, NE, D])
        b_e1 = sb("b_e1", [NE, D])
        c_t = sb("c_t", [P, 2, NB])
        w_mod = sb("w_mod", [P, 2, 6 * D])

        ident = sb("ident", [P, P])
        rep = sb("rep", [P, KPH, P])
        state_sum = sb("state_sum", [P, R])
        rev = sb("rev", [P, NE])
        w_conv0 = sb("w_conv0", [P, TAPS0, DI])
        w_conv1 = sb("w_conv1", [P, TAPS1, D])
        neg_a0 = sb("neg_a0", [P, H0 * KPH, SHI])
        neg_a1 = sb("neg_a1", [P, KPH, SHI])
        w_dtx1 = sb("w_dtx1", [P, D])
        w_cx1 = sb("w_cx1", [P, D])
        silu_c = sb("silu_c", [P, 2, NB])
        mods = sb("mods", [P, 2, 6, NB])
        gates = sb("gates", [P, 3, NB, D])
        eps_col = sb("eps_col", [P, 1])

        xa = sb("xa", [P, TILES, D])
        xr = sb("xr", [P, TILES, D])
        xo = sb("xo", [P, TILES, D])
        stats = sb("stats", [P, TILES, 6])
        mean_var = sb("mean_var", [P, TILES, 2])
        log_var = sb("log_var", [P, TILES])
        rstd = sb("rstd", [P, TILES])
        xn = sb("xn", [P, TILES, D])
        hT = sb("hT", [P, T + 4])
        xs = sb("xs", [P, H0, T])
        zs = sb("zs", [P, H0, T])
        conv0_bc = zs[:, 0, :].rearrange("p (k d) -> p k d", k=TAPS0)
        conv1_bc = zs[:, 1, 0:TAPS1 * D].rearrange("p (k d) -> p k d", k=TAPS1)
        xdbl = sb("xdbl", [1 + 2 * NS, T])
        sp = sb("sp", [P, 2, CH])
        dt = sb("dt", [P, H0, T])
        dtx = sb("dtx", [P, H0, T])
        gate_tmp = dtx[:, 0, :]
        b_rep = sb("b_rep", [P, SHI, T])
        c_rep = sb("c_rep", [P, SHI, T])
        dt_rep = sb("dt_rep", [P, 2, CH])
        carry = sb("carry", [P, H0 * KPH, SHI])
        u = sb("u", [P, 2, CH])
        h = sb("h", [P, HR, CH])
        hc = sb("hc", [P, CR, CH])
        y1 = sb("y1", [P, CH])
        y2 = sb("y2", [P, H0, CH])
        w_out0g = sb("w_out0g", [P, H0, D])
        c_mat = sb("c_mat", [P, T])
        mx = sb("mx", [P, TILES])
        lg = sb("lg", [P, TILES, NE])
        ex = sb("ex", [P, TILES, NE])
        sg = sb("sg", [P, TILES])
        pr = sb("pr", [P, TILES, NE])
        key = sb("key", [P, TILES, NE])
        pick1 = sb("pick1", [P, TILES, NE])
        pick2 = sb("pick2", [P, TILES, NE])
        comb = sb("comb", [P, TILES, NE + 1])
        combT = sb("combT", [NE + 1, T])
        comb_rep = sb("comb_rep", [P, 3, CH])
        hw = sb("hw", [P, 2, CH])
        gate_act = sb("gate_act", [P, CH])
        shared = sb("shared", [P, CH])
        ffn = sb("ffn", [P, TPC, D])

        da = ps("da", [P, 2, CH])
        dtx_rep = ps("dtx_rep", [P, 2, CH])
        ysum = ps("ysum", [P, CH])
        mm = ps("mm", [P, MB, CH])

        s_load = sem("s_load", 0)
        s_const = sem("s_const", 0)
        s_setup_pe = sem("s_setup_pe", 0)
        s_setup_act = sem("s_setup_act", 0)
        s_setup = sem("s_setup", 0)
        s_x = sem("s_x", 16)
        s_stats = sem("s_stats", 2 * 4)
        s_logvar = sem("s_logvar", 4)
        s_rstd = sem("s_rstd", 4)
        s_xn = sem("s_xn", 4)
        s_xnT = sem("s_xnT", 4 * NC)
        s_hT = sem("s_hT", 4 * NC)
        N_IN = NC * (2 * H0) + NC * 2
        s_in = sem("s_in", N_IN)
        s_in_act = sem("s_in_act", N_IN)
        s_xdbl = sem("s_xdbl", 2 * NC)
        s_xdbl_act = sem("s_xdbl_act", 2 * NC)
        s_cpe = sem("s_cpe", NC)
        s_cmat = sem("s_cmat", NC)
        N_DT = NC * H0 + NC
        s_dtpre = sem("s_dtpre", N_DT)
        s_sp1 = sem("s_sp1", 3 * N_DT)
        s_relu = sem("s_relu", N_DT)
        s_dt = sem("s_dt", N_DT)
        s_dtx = sem("s_dtx", N_DT)
        s_brep = sem("s_brep", 2 * SLO * 16)
        s_crep = sem("s_crep", SLO * 16)
        s_rows = sem("s_rows", 2 * 16)
        s_comb_row = sem("s_comb_row", NC * 16)
        KS0 = NC * H0 * KPH
        KS1 = NC * KPH
        s_dtrep = [sem(f"s_dtrep{i}", (KS0 + KS1) // 2 * SLO * 16) for i in range(2)]
        s_dtxrep = sem("s_dtxrep", KS0 + KS1)
        NSC = (KS0 + KS1) * SHI
        s_da = sem("s_da", NSC)
        s_u = sem("s_u", NSC)
        s_scan = sem("s_scan", NSC)
        s_carry = sem("s_carry", NSC // 2)
        s_hc = sem("s_hc", KS0 * SHI)
        s_hsum = sem("s_hsum", NSC)
        NY = NC * H0 + NC
        s_y1 = sem("s_y1", NY)
        s_y2 = sem("s_y2", NC * H0)
        s_wg = sem("s_wg", 1)
        s_out0 = sem("s_out0", NC)
        s_xr0 = sem("s_xr0", NC)
        s_cy = sem("s_cy", NC)
        s_out1 = sem("s_out1", NC)
        s_o1 = sem("s_o1", NC)
        s_o1T = sem("s_o1T", NC)
        s_xr2 = sem("s_xr2", NC)
        s_lg = sem("s_lg", 2)
        N_ROUTE = (21, 19)
        s_route = sem("s_route", sum(N_ROUTE))
        s_ex = sem("s_ex", 2)
        s_sg = sem("s_sg", 1)
        s_combT = sem("s_combT", 2 * NC)
        s_combT_act = sem("s_combT_act", 2 * NC)
        s_crow = [sem(f"s_crow{i}", NC * (NE + 1) // 3 * 16) for i in range(3)]
        s_h1 = sem("s_h1", NC * (NE + 2))
        s_h1a = sem("s_h1a", NC * (NE + 1))
        s_sh = sem("s_sh", NC)
        s_hw = sem("s_hw", NC * (2 * NE))
        s_hws = sem("s_hws", NC)
        s_hwu = sem("s_hwu", NC * (2 * NE + 1))
        s_erep = sem("s_erep", NC * NE)
        s_ffn = sem("s_ffn", 2 * NC)
        s_xr1 = sem("s_xr1", NC)
        s_xo = sem("s_xo", NC)
        s_store = sem("s_store", 16)

        N_CONST = 5 + NE + 1 + KPH + SLO + TAPS0 + TAPS1
        N_COPIED = 6
        N_MODS = N_COPIED + 4 + 4
        N_SETUP = N_MODS + 3 * 2 + 3 * 4
        XS0 = [c * 2 * H0 + m + 1 for c in range(NC) for m in range(H0)]
        ZS0 = [c * 2 * H0 + H0 + m + 1 for c in range(NC) for m in range(H0)]
        XS1 = [NC * 2 * H0 + 2 * c + 1 for c in range(NC)]

        def kept(n):
            n0 = min(max(n, 0), H0 * KPH * SHI)
            n1 = min(max(n - KS0 * SHI, 0), KPH * SHI)
            return n0 + n1

        uses = []
        place = {}

        def use(what, freed_by, n):
            place[what] = len(uses)
            uses.append((freed_by, n))

        def use_norm(l):
            for c in range(NC):
                use(("norm", l, c), s_hT, NC * l + c + 1)

        use_norm(0)
        for c in range(NC):
            for j in range(2 * H0):
                use(("in", c * 2 * H0 + j), s_in_act, c * 2 * H0 + j + 1)
        for c in range(NC):
            use(("xdbl", c), s_xdbl_act, c + 1)
        for i in range(NC * H0):
            use(("dtpre", i), s_dt, i + 1)
        for c in range(NC):
            use(("out0", c), s_xr0, c + 1)
        use_norm(1)
        use(("lg", 0), s_route, 3)
        for c in range(NC):
            use(("combT", c), s_combT_act, c + 1)
        for c in range(NC):
            use(("acc", c), s_ffn, c + 1)
            for e in range(NE + 2):
                if e < NE:
                    use(("h1", c, e), s_hw, NE * c + e + 1)
                elif e == NE:
                    use(("h1", c, e), s_h1a, (NE + 1) * (c + 1))
                else:
                    use(("h1", c, e), s_sh, c + 1)
        use_norm(2)
        for i in range(NC * 2):
            use(("in", NC * 2 * H0 + i), s_in_act, NC * 2 * H0 + i + 1)
        for i in range(NC):
            use(("xdbl", NC + i), s_xdbl_act, NC + i + 1)
        for i in range(NC):
            use(("cmat", i), s_cmat, i + 1)
        for i in range(NC):
            use(("dtpre", NC * H0 + i), s_dt, NC * H0 + i + 1)
        for c in range(NC):
            use(("out1", c), s_o1, c + 1)
            use(("o1T", c), s_xr2, c + 1)
        use_norm(3)
        use(("lg", 1), s_route, N_ROUTE[0] + 1)
        for c in range(NC):
            use(("combT", NC + c), s_combT_act, NC + c + 1)
        for c in range(NC):
            use(("acc", NC + c), s_ffn, NC + c + 1)
            for e in range(NE):
                use(("erep", c, e), s_hw, NC * NE + NE * c + e + 1)

        bank = {}
        waits = {}
        holder = [None] * MB
        order = [0] * MB
        names = sorted(place, key=place.get)
        ends = {}
        for c in range(NC):
            ends[("acc", c)] = place[("h1", c, NE + 1)]
            ends[("acc", NC + c)] = place[("erep", c, NE - 1)]
        for n, name in enumerate(names):
            free = [i for i in range(MB) if holder[i] is None or n > ends.get(holder[i], -1)]
            i = min(free, key=lambda k: order[k])
            bank[name] = i
            waits[name] = None if holder[i] is None else uses[place[holder[i]]]
            holder[i], order[i] = name, n

        def claim(pe, b, name):
            if waits[name] is None:
                pe.wait_ge(s_ffn, at(s_ffn, b, 0))
                pe.wait_ge(s_hw, at(s_hw, b, 0))
            else:
                pe.wait_ge(waits[name][0], at(waits[name][0], b, waits[name][1]))
            return mm[:, bank[name], :]

        def bank_of(name):
            return mm[:, bank[name], :]

        block = ctx.enter_context(nc.Block())

        loads = [
            (w_in0[:], w["w_in0"]), (conv0_bc, w["conv0"].partition_broadcast(P)), (conv_b0[:], w["conv_b0"]),
            (w_x0[:], w["w_x0"]), (w_dt0[:], w["w_dt0"]), (b_dt0[:], w["b_dt0"]), (a_log0[:], w["a_log0"]),
            (d0[:], w["d0"]), (w_out0[:], w["w_out0"]), (router[:], w["router"]), (w1[:], w["w1"]),
            (w2[:], w["w2"]), (w_in1[:], w["w_in1"]), (conv1_bc, w["conv1"].partition_broadcast(P)),
            (w_x1dt[:], w["w_x1dt"]), (w_x1b[:], w["w_x1b"]), (w_x1c[:], w["w_x1c"]), (w_dt1[:], w["w_dt1"]),
            (w_c1[:], w["w_c1"]), (b_dt1[:], w["b_dt1"]), (a_log1[:], w["a_log1"]), (d1[:], w["d1"]),
            (w_out1[:], w["w_out1"]), (gate_w1[:], w["gate_w1"]), (gate_b1[:], w["gate_b1"].partition_broadcast(P)),
            (w_e1[:], w["w_e1"]), (b_e1[:], w["b_e1"]), (c_t[:], w["c_t"]), (w_mod[:], w["w_mod"]),
        ]
        N_LOAD = 16 * len(loads)

        @block.sync
        def _(sp_):
            for dst, src in loads:
                sp_.dma_start(dst, src).then_inc(s_load, 16)

            def rep_dt(b, j):
                lay1 = j >= KS0
                jj = j - KS0 if lay1 else j
                kn = KPH if lay1 else H0 * KPH
                c, k = jj // kn, jj % kn
                m, kk = k // KPH, k % KPH
                there = sp_.compute_val(at(s_dt, b, NC * H0 + c + 1 if lay1 else c * H0 + m + 1))
                free = sp_.compute_val(at(s_da, b, SHI * max(j - 1, 0)))
                sp_.wait_ge(s_dt, there)
                sp_.wait_ge(s_da, free)
                for a in range(SLO):
                    sp_.dma_start(dt_rep[R * a:R * a + R, j % 2, :],
                                  dt[R * kk:R * kk + R, m, CH * c:CH * c + CH]).then_inc(s_dtrep[j % 2], 16)

            def rep_rows(dst, row0, s_done):
                for a in range(SLO):
                    sp_.dma_start(dst[R * a:R * a + R, :, :],
                                  rows_dram[row0 + SHI * a:row0 + SHI * a + SHI, :].partition_broadcast(R)
                                  ).then_inc(s_done, 16)

            def spill_rows(b, n, rows):
                sp_.dma_start(rows_dram[0:rows, :], xdbl[0:rows, :]).then_inc(s_rows, 16)
                sp_.wait_ge(s_rows, at(s_rows, b, 16 * n))

            def rep_comb(b, c, e):
                n = c * (NE + 1) + e
                if n < 3 or (n - 3) % (NE + 1) == NE:
                    used, value = s_hws, max(n - 3, -1) // (NE + 1) + 1
                else:
                    used, value = s_hw, (n - 3) // (NE + 1) * NE + (n - 3) % (NE + 1) + 1
                free = sp_.compute_val(at(used, b, value))
                if e == 0:
                    there, stored = sp_.compute_val(at(s_combT_act, b, c + 1)), sp_.compute_val(at(s_comb_row, b, 16 * (c + 1)))
                    sp_.wait_ge(s_combT_act, there)
                    cols = slice(CH * c, CH * c + CH)
                    sp_.dma_start(comb_dram[:, cols], combT[:, cols]).then_inc(s_comb_row, 16)
                    sp_.wait_ge(s_comb_row, stored)
                sp_.wait_ge(used, free)
                sp_.dma_start(comb_rep[:, n % 3:n % 3 + 1, :],
                              comb_dram[e:e + 1, CH * c:CH * c + CH].partition_broadcast(P)).then_inc(s_crow[n % 3], 16)

            with sp_.Fori(0, NB) as b:
                sp_.wait_ge(s_load, N_LOAD)
                sp_.wait_ge(s_xr0, at(s_xr0, b, 0))
                sp_.dma_start(xa[:], x_in[bass.ds(b, 1), :, :].rearrange("o (i p) d -> (o p) i d", p=P)).then_inc(s_x, 16)
                there, scanned, summed = (sp_.compute_val(v) for v in (at(s_xdbl_act, b, NC), at(s_u, b, 0), at(s_hc, b, 0)))
                sp_.wait_ge(s_xdbl_act, there)
                sp_.wait_ge(s_u, scanned)
                sp_.wait_ge(s_hc, summed)
                spill_rows(b, 1, 1 + 2 * NS)
                rep_rows(b_rep, 1, s_brep)
                rep_rows(c_rep, 1 + NS, s_crep)
                for j in range(KS0):
                    rep_dt(b, j)
                for c in range(NC):
                    for e in range(NE + 1):
                        rep_comb(b, c, e)
                there, scanned = (sp_.compute_val(v) for v in (at(s_xdbl_act, b, 2 * NC), at(s_u, b, KS0 * SHI)))
                sp_.wait_ge(s_xdbl_act, there)
                sp_.wait_ge(s_u, scanned)
                spill_rows(b, 2, NS)
                rep_rows(b_rep, 0, s_brep)
                for j in range(KS0, KS0 + KS1):
                    rep_dt(b, j)
                sp_.wait_ge(s_load, N_LOAD)
                sp_.wait_ge(s_xo, at(s_xo, b, NC))
                sp_.dma_start(out[bass.ds(b, 1), :, :].rearrange("o (i p) d -> (o p) i d", p=P), xo[:]).then_inc(s_store, 16)
            sp_.wait_ge(s_store, 16 * NB + 1)

        @block.gpsimd
        def _(pool):
            for s in counted:
                pool.sem_inc(s, 1)
            pool.memset(ident[:], 0.0).then_inc(s_const, 1)
            pool.memset(rep[:], 0.0).then_inc(s_const, 1)
            pool.memset(state_sum[:], 0.0).then_inc(s_const, 1)
            pool.memset(eps_col[:], EPS).then_inc(s_const, 1)
            pool.memset(hT[:], 0.0).then_inc(s_const, 1)
            for e in range(NE):
                pool.memset(rev[:, e:e + 1], float(NE - e)).then_inc(s_const, 1)
            n = 5 + NE
            pool.wait_ge(s_const, n)
            pool.affine_select(out=ident[:], in_=ident[:], compare_op=ALU.not_equal, fill=1.0, base=0,
                               pattern=[[-1, P]], channel_multiplier=1).then_inc(s_const, 1)
            n += 1
            for k in range(KPH):
                v = rep[:, k, :].rearrange("p (a r) -> p a r", a=SLO)
                pool.affine_select(out=v, in_=v, compare_op=ALU.not_equal, fill=1.0, base=-R * k,
                                   pattern=[[0, SLO], [-1, R]], channel_multiplier=1).then_inc(s_const, 1)
            n += KPH
            for a in range(SLO):
                pool.wait_ge(s_const, n)
                pool.affine_select(out=state_sum[:], in_=state_sum[:], compare_op=ALU.not_equal, fill=1.0,
                                   base=-R * a, pattern=[[-1, R]], channel_multiplier=1).then_inc(s_const, 1)
                n += 1
            pool.wait_ge(s_load, N_LOAD)
            for k in range(TAPS0):
                pool.tensor_tensor(w_conv0[:, k, :], w_in0[:, 0:DI], conv0_bc[:, k, :], ALU.mult).then_inc(s_const, 1)
            for k in range(TAPS1):
                pool.tensor_tensor(w_conv1[:, k, :], w_in1[:, 0:D], conv1_bc[:, k, :], ALU.mult).then_inc(s_const, 1)

            def normalise(b, l, src):
                there = pool.compute_val(at(s_rstd, b, l + 1))
                free = pool.compute_val(at(s_xnT, b, NC * l))
                pool.wait_ge(s_setup, N_SETUP)
                pool.wait_ge(s_rstd, there)
                pool.wait_ge(s_xnT, free)
                for i in range(TILES):
                    ins = pool.tensor_scalar(xn[:, i, :], src[:, i, :], mean_var[:, i, 0:1], rstd[:, i:i + 1],
                                             ALU.subtract, ALU.mult)
                ins.then_inc(s_xn, 1)

            with pool.Fori(0, NB) as b:
                pool.wait_ge(s_setup, N_SETUP)
                pool.wait_ge(s_out0, at(s_out0, b, 0))
                for m in range(H0):
                    ins = pool.tensor_tensor(w_out0g[:, m:m + 1, :], w_out0[:, m:m + 1, :], gates[:, 0, bass.ds(b, 1), :], ALU.mult)
                ins.then_inc(s_wg, 1)
                normalise(b, 0, xa)
                for c in range(NC):
                    for m in range(H0):
                        i = c * H0 + m
                        pool.wait_ge(s_dt, at(s_dt, b, i + 1))
                        pool.wait_ge(s_in_act, at(s_in_act, b, XS0[i]))
                        pool.wait_ge(s_dtxrep, at(s_dtxrep, b, 0))
                        pool.tensor_tensor(dtx[:, m, CH * c:CH * c + CH], dt[:, m, CH * c:CH * c + CH],
                                           xs[:, m, CH * c:CH * c + CH], ALU.mult).then_inc(s_dtx, 1)
                def y_gated(c, m):
                    i = c * H0 + m
                    pool.wait_ge(s_y1, at(s_y1, b, i + 1))
                    pool.wait_ge(s_in_act, at(s_in_act, b, ZS0[i]))
                    if c:
                        pool.wait_ge(s_out0, at(s_out0, b, c))
                    pool.tensor_tensor(y2[:, m, :], y1[:], zs[:, m, CH * c:CH * c + CH], ALU.mult).then_inc(s_y2, 1)

                pool.wait_ge(s_crep, at(s_crep, b, SLO * 16))
                for n in range(KS0 * SHI):
                    c, i = n // (H0 * KPH * SHI), n % SHI
                    pool.wait_ge(s_scan, at(s_scan, b, n + 1))
                    pool.wait_ge(s_hsum, at(s_hsum, b, max(n - CR + 1, 0)))
                    pool.tensor_tensor(hc[:, n % CR, :], h[:, n % HR, :], c_rep[:, i, CH * c:CH * c + CH],
                                       ALU.mult).then_inc(s_hc, 1)
                    half, past = (n + 1 - LAG_GATE) // HALF, (n + 1 - LAG_GATE) % HALF
                    if past == 0 and half >= 1:
                        y_gated((half - 1) // H0, (half - 1) % H0)
                y_gated(NC - 1, H0 - 1)
                normalise(b, 1, xr)
                for c in range(NC):
                    n = c * (NE + 1) + NE
                    pool.wait_ge(s_crow[n % 3], at(s_crow[n % 3], b, 16 * (n // 3 + 1)))
                    pool.wait_ge(s_sh, at(s_sh, b, c + 1))
                    pool.wait_ge(s_hwu, at(s_hwu, b, n - 1))
                    pool.tensor_tensor(hw[:, NE % 2, :], shared[:], comb_rep[:, n % 3, :], ALU.mult).then_inc(s_hws, 1)
                    pool.wait_ge(s_ffn, at(s_ffn, b, c + 1))
                    pool.wait_ge(s_xr0, at(s_xr0, b, c + 1))
                    v = xr[:, TPC * c:TPC * c + TPC, :]
                    pool.tensor_tensor(v, v, ffn[:], ALU.add).then_inc(s_xr1, 1)
                pool.wait_ge(s_xr1, at(s_xr1, b, NC))
                normalise(b, 2, xr)
                for c in range(NC):
                    pool.wait_ge(s_dt, at(s_dt, b, NC * H0 + c + 1))
                    pool.wait_ge(s_in_act, at(s_in_act, b, XS1[c]))
                    pool.wait_ge(s_dtxrep, at(s_dtxrep, b, KS0))
                    pool.tensor_tensor(dtx[:, 0, CH * c:CH * c + CH], dt[:, 0, CH * c:CH * c + CH],
                                       xs[:, 0, CH * c:CH * c + CH], ALU.mult).then_inc(s_dtx, 1)
                normalise(b, 3, xr)
                for c in range(NC):
                    pool.wait_ge(s_ffn, at(s_ffn, b, NC + c + 1))
                    pool.wait_ge(s_store, at(s_store, b, 0))
                    v = xr[:, TPC * c:TPC * c + TPC, :]
                    pool.tensor_tensor(xo[:, TPC * c:TPC * c + TPC, :], v, ffn[:], ALU.add).then_inc(s_xo, 1)

        @block.scalar
        def _(act):
            act.wait_ge(s_load, N_LOAD)
            act.activation(silu_c[:], c_t[:], ACT.Silu).then_inc(s_setup_act, 1)
            act.activation(neg_a0[:], a_log0[:], ACT.Exp).then_inc(s_setup_act, 1)
            act.activation(neg_a1[:], a_log1[:], ACT.Exp).then_inc(s_setup_act, 1)
            act.wait_ge(s_setup, N_SETUP)
            act.wait_ge(s_const, N_CONST)

            def norm_scale(b, l):
                act.wait_ge(s_stats, at(s_stats, b, 2 * l + 2))
                act.wait_ge(s_rstd, at(s_rstd, b, l))
                act.activation(log_var[:], mean_var[:, :, 1], ACT.Ln, bias=eps_col[:, 0:1]).then_inc(s_logvar, 1)
                act.wait_ge(s_logvar, at(s_logvar, b, l + 1))
                act.wait_ge(s_xn, at(s_xn, b, l))
                act.activation(rstd[:], log_var[:], ACT.Exp, scale=-0.5).then_inc(s_rstd, 1)
                for c in range(NC):
                    act.wait_ge(s_setup, N_SETUP)
                    act.wait_ge(s_xnT, at(s_xnT, b, NC * l + c + 1))
                    lay, j = l // 2, 3 * (l % 2)
                    act.activation(hT[:, 3 + CH * c:3 + CH * c + CH], bank_of(("norm", l, c)), ACT.Identity,
                                   bias=mods[:, lay, j, bass.ds(b, 1)], scale=mods[:, lay, j + 1, bass.ds(b, 1)]
                                   ).then_inc(s_hT, 1)

            def silu_in(b, n, dst, bias):
                act.wait_ge(s_in, at(s_in, b, n + 1))
                act.activation(dst, bank_of(("in", n)), ACT.Silu, bias=bias).then_inc(s_in_act, 1)

            def softplus(b, i, bias):
                act.wait_ge(s_dtpre, at(s_dtpre, b, i + 1))
                if i >= 2:
                    act.wait_ge(s_dt, at(s_dt, b, i - 1))
                else:
                    act.wait_ge(s_dt, at(s_dt, b, 0))
                v = sp[:, i % 2, :]
                act.activation(v, bank_of(("dtpre", i)), ACT.Abs, bias=bias).then_inc(s_sp1, 1)
                act.wait_ge(s_sp1, at(s_sp1, b, 3 * i + 1))
                act.activation(v, v, ACT.Exp, scale=-1.0).then_inc(s_sp1, 1)
                act.wait_ge(s_sp1, at(s_sp1, b, 3 * i + 2))
                act.activation(v, v, ACT.Ln, bias=1.0).then_inc(s_sp1, 1)

            def decays(b, lay):
                base = KS0 if lay else 0
                kn = KPH if lay else H0 * KPH
                neg_a = neg_a1 if lay else neg_a0

                def save_last(n, k, i):
                    act.wait_ge(s_scan, at(s_scan, b, n + 1))
                    act.copy(carry[:, k, i:i + 1], h[:, n % HR, CH - 1:CH]).then_inc(s_carry, 1)

                pending = []
                for c in range(NC):
                    for k in range(kn):
                        j = base + c * kn + k
                        act.wait_ge(s_dtrep[j % 2], at(s_dtrep[j % 2], b, (j // 2 + 1) * SLO * 16))
                        for i in range(SHI):
                            n = SHI * j + i
                            act.wait_ge(s_scan, at(s_scan, b, max(n - 1, 0)))
                            act.activation(da[:, n % 2, :], dt_rep[:, j % 2, :], ACT.Exp,
                                           scale=neg_a[:, k, i:i + 1]).then_inc(s_da, 1)
                            if pending:
                                save_last(*pending.pop(0))
                            if c == 0:
                                pending.append((n, k, i))
                for p in pending:
                    save_last(*p)

            with act.Fori(0, NB) as b:
                norm_scale(b, 0)
                for c in range(NC):
                    for m in range(H0):
                        silu_in(b, c * 2 * H0 + m, xs[:, m, CH * c:CH * c + CH], conv_b0[:, m:m + 1])
                    for m in range(H0):
                        silu_in(b, c * 2 * H0 + H0 + m, zs[:, m, CH * c:CH * c + CH], 0.0)
                for c in range(NC):
                    act.wait_ge(s_xdbl, at(s_xdbl, b, c + 1))
                    act.wait_ge(s_crep, at(s_crep, b, 0))
                    act.wait_ge(s_brep, at(s_brep, b, 0))
                    act.copy(xdbl[:, CH * c:CH * c + CH], bank_of(("xdbl", c))[0:1 + 2 * NS, :]).then_inc(s_xdbl_act, 1)
                for i in range(NC * H0):
                    softplus(b, i, b_dt0[:, i % H0:i % H0 + 1])
                decays(b, 0)
                norm_scale(b, 1)
                act.wait_ge(s_route, at(s_route, b, 2))
                act.activation(ex[:], lg[:], ACT.Exp).then_inc(s_ex, 1)
                act.wait_ge(s_route, at(s_route, b, 3))
                act.activation(sg[:], sg[:], ACT.Exp, scale=-1.0).then_inc(s_sg, 1)
                for c in range(NC):
                    act.wait_ge(s_combT, at(s_combT, b, c + 1))
                    act.wait_ge(s_hwu, at(s_hwu, b, 0))
                    act.copy(combT[:, CH * c:CH * c + CH], bank_of(("combT", c))[0:NE + 1, :]).then_inc(s_combT_act, 1)
                for c in range(NC):
                    for e in range(NE + 1):
                        act.wait_ge(s_h1, at(s_h1, b, c * (NE + 2) + e + 1))
                        v = bank_of(("h1", c, e))
                        if e == NE:
                            act.wait_ge(s_sh, at(s_sh, b, c))
                        act.activation(v if e < NE else gate_act[:], v, ACT.Silu).then_inc(s_h1a, 1)
                norm_scale(b, 2)
                for c in range(NC):
                    silu_in(b, NC * 2 * H0 + 2 * c, xs[:, 0, CH * c:CH * c + CH], 0.0)
                    silu_in(b, NC * 2 * H0 + 2 * c + 1, zs[:, 0, CH * c:CH * c + CH], 0.0)
                for c in range(NC):
                    act.wait_ge(s_xdbl, at(s_xdbl, b, NC + c + 1))
                    act.wait_ge(s_brep, at(s_brep, b, SLO * 16))
                    act.wait_ge(s_crep, at(s_crep, b, SLO * 16))
                    act.copy(xdbl[0:NS, CH * c:CH * c + CH], bank_of(("xdbl", NC + c))[0:NS, :]).then_inc(s_xdbl_act, 1)
                for c in range(NC):
                    act.wait_ge(s_cpe, at(s_cpe, b, c + 1))
                    act.copy(c_mat[:, CH * c:CH * c + CH], bank_of(("cmat", c))).then_inc(s_cmat, 1)
                for i in range(NC * H0, N_DT):
                    softplus(b, i, b_dt1[:, 0:1])
                decays(b, 1)
                norm_scale(b, 3)
                act.wait_ge(s_route, at(s_route, b, N_ROUTE[0] + 3))
                act.activation(ex[:], lg[:], ACT.Exp).then_inc(s_ex, 1)
                for c in range(NC):
                    act.wait_ge(s_combT, at(s_combT, b, NC + c + 1))
                    act.wait_ge(s_hw, at(s_hw, b, NC * NE))
                    act.wait_ge(s_hws, at(s_hws, b, NC))
                    act.copy(combT[0:NE, CH * c:CH * c + CH], bank_of(("combT", NC + c))[0:NE, :]).then_inc(s_combT_act, 1)

        @block.vector
        def _(dve):
            dve.wait_ge(s_setup_act, 3)
            dve.wait_ge(s_const, N_CONST)
            dve.tensor_scalar(neg_a0[:], neg_a0[:], -1.0, None, ALU.mult).then_inc(s_setup, 1)
            dve.tensor_scalar(neg_a1[:], neg_a1[:], -1.0, None, ALU.mult).then_inc(s_setup, 1)
            n = 2
            dve.wait_ge(s_setup_pe, 3)
            for lay in range(2):
                v = mods[:, lay, :, :].rearrange("p j b -> p (j b)")
                dve.tensor_copy(v, mm[:, lay, 0:6 * NB]).then_inc(s_setup, 1)
            dve.tensor_copy(w_dtx1[:], mm[:, 2, 0:D]).then_inc(s_setup, 1)
            dve.tensor_copy(w_cx1[:], mm[:, 2, D:2 * D]).then_inc(s_setup, 1)
            n += 4
            dve.wait_ge(s_setup, n)
            for lay in range(2):
                for j in (1, 4):
                    dve.tensor_scalar(mods[:, lay, j, :], mods[:, lay, j, :], 1.0, None, ALU.add).then_inc(s_setup, 1)
                    n += 1

            def gated(v, tmp):
                nonlocal n
                dve.wait_ge(s_setup, n)
                dve.tensor_scalar(tmp, v, 0.0, 2.0, ALU.is_ge, ALU.mult).then_inc(s_setup, 1)
                dve.wait_ge(s_setup, n + 1)
                dve.scalar_tensor_tensor(out=v, in0=tmp, scalar=-1.0, in1=v, op0=ALU.add, op1=ALU.mult).then_inc(s_setup, 1)
                dve.wait_ge(s_setup, n + 2)
                dve.tensor_scalar(v, v, GATE_MIN, None, ALU.max).then_inc(s_setup, 1)
                dve.wait_ge(s_setup, n + 3)
                dve.scalar_tensor_tensor(out=v, in0=tmp, scalar=-1.0, in1=v, op0=ALU.add, op1=ALU.mult).then_inc(s_setup, 1)
                n += 4

            gated(mods[:, 1, 2, :], gate_tmp[:, 0:NB])
            for g in range(3):
                for q in range(2):
                    dve.wait_ge(s_setup_pe, 4 + 2 * g + q)
                    dve.tensor_copy(gates[:, g, NB // 2 * q:NB // 2 * q + NB // 2, :].rearrange("p b d -> p (b d)"),
                                    mm[:, q, :]).then_inc(s_setup, 1)
                    n += 1
            for g in range(3):
                gated(gates[:, g, :, :].rearrange("p b d -> p (b d)"), gate_tmp)
            assert n == N_SETUP

            def norm_stats(b, l, src):
                dve.wait_ge(s_xn, at(s_xn, b, l))
                for i in range(TILES):
                    ins = dve.bn_stats(stats[:, i, :], src[:, i, :])
                ins.then_inc(s_stats, 1)
                stats_there = dve.compute_val(at(s_stats, b, 2 * l + 1))
                dve.wait_ge(s_setup, N_SETUP)
                dve.wait_ge(s_stats, stats_there)
                for i in range(TILES):
                    ins = dve.bn_aggr(mean_var[:, i, :], stats[:, i, :])
                ins.then_inc(s_stats, 1)

            def time_step(b, i, bias, floor, m, c):
                v = bank_of(("dtpre", i))
                dve.wait_ge(s_sp1, at(s_sp1, b, 3 * i + 1))
                dve.tensor_scalar(v, v, bias, 0.0, ALU.add, ALU.max).then_inc(s_relu, 1)
                dve.wait_ge(s_relu, at(s_relu, b, i + 1))
                dve.wait_ge(s_sp1, at(s_sp1, b, 3 * i + 3))
                dve.scalar_tensor_tensor(out=dt[:, m, CH * c:CH * c + CH], in0=sp[:, i % 2, :], scalar=floor, in1=v,
                                         op0=ALU.add, op1=ALU.add).then_inc(s_dt, 1)

            def scans(b, lay, after):
                base = KS0 * SHI if lay else 0
                count = KS1 * SHI if lay else KS0 * SHI
                kn = KPH if lay else H0 * KPH

                def product(n):
                    j, i = n // SHI, n % SHI
                    c = (n - base) // (kn * SHI)
                    if i == 0:
                        dve.wait_ge(s_dtxrep, at(s_dtxrep, b, j + 1))
                    dve.wait_ge(s_scan, at(s_scan, b, max(n - 1, 0)))
                    dve.tensor_tensor(u[:, n % 2, :], dtx_rep[:, j % 2, :], b_rep[:, i, CH * c:CH * c + CH],
                                      ALU.mult).then_inc(s_u, 1)

                dve.wait_ge(s_brep, at(s_brep, b, SLO * 16 * (lay + 1)))
                product(base)
                for n in range(base, base + count):
                    c, k, i = (n - base) // (kn * SHI), (n - base) // SHI % kn, n % SHI
                    if n + 1 < base + count:
                        product(n + 1)
                    dve.wait_ge(s_u, at(s_u, b, n + 1))
                    dve.wait_ge(s_da, at(s_da, b, n + 1))
                    dve.wait_ge(s_hc, at(s_hc, b, min(max(n - HR + 1, 0), KS0 * SHI)))
                    dve.wait_ge(s_hsum, at(s_hsum, b, n - HR + 1 if lay else 0))
                    dve.wait_ge(s_carry, at(s_carry, b, kept(n - HR + 1)))
                    dve.tensor_tensor_scan(h[:, n % HR, :], da[:, n % 2, :], u[:, n % 2, :],
                                           0.0 if c == 0 else carry[:, k, i:i + 1], ALU.mult, ALU.add
                                           ).then_inc(s_scan, 1)
                    after(n - base + 1)
                after(None)

            def y0(b):
                def y_sum(c, m):
                    i = c * H0 + m
                    dve.wait_ge(s_hsum, at(s_hsum, b, HALF * (i + 1)))
                    dve.wait_ge(s_y2, at(s_y2, b, i))
                    dve.scalar_tensor_tensor(out=y1[:], in0=xs[:, m, CH * c:CH * c + CH], scalar=d0[:, m:m + 1],
                                             in1=ysum[:], op0=ALU.mult, op1=ALU.add).then_inc(s_y1, 1)

                def residual(c):
                    dve.wait_ge(s_out0, at(s_out0, b, c + 1))
                    dve.wait_ge(s_xo, at(s_xo, b, 0))
                    v = slice(TPC * c, TPC * c + TPC)
                    dve.tensor_tensor(xr[:, v, :], xa[:, v, :],
                                      bank_of(("out0", c)).rearrange("p (i d) -> p i d", i=TPC), ALU.add
                                      ).then_inc(s_xr0, 1)

                def after(n):
                    if n is None:
                        y_sum(NC - 1, H0 - 1)
                        residual(NC - 1)
                    elif n > HALF and (n - LAG_Y) % HALF == 0:
                        i = (n - LAG_Y) // HALF - 1
                        y_sum(i // H0, i % H0)
                    elif n > H0 * HALF and (n - LAG_RES) % (H0 * HALF) == 0:
                        residual((n - LAG_RES) // (H0 * HALF) - 1)
                return after

            def y1_(b):
                def y_sum(c):
                    dve.wait_ge(s_hsum, at(s_hsum, b, SHI * KS0 + HALF * (c + 1)))
                    dve.wait_ge(s_cmat, at(s_cmat, b, c + 1))
                    dve.tensor_tensor(ysum[:], ysum[:], c_mat[:, CH * c:CH * c + CH], ALU.mult).then_inc(s_cy, 1)
                    dve.wait_ge(s_cy, at(s_cy, b, c + 1))
                    dve.wait_ge(s_out1, at(s_out1, b, c))
                    dve.wait_ge(s_y2, at(s_y2, b, NC * H0))
                    dve.scalar_tensor_tensor(out=y1[:], in0=xs[:, 0, CH * c:CH * c + CH], scalar=d1[:, 0:1],
                                             in1=ysum[:], op0=ALU.mult, op1=ALU.add).then_inc(s_y1, 1)

                def gate(c):
                    dve.wait_ge(s_out1, at(s_out1, b, c + 1))
                    dve.wait_ge(s_o1T, at(s_o1T, b, c))
                    dve.scalar_tensor_tensor(out=y2[:, 0, :], in0=bank_of(("out1", c)), scalar=mods[:, 1, 2, bass.ds(b, 1)],
                                             in1=zs[:, 0, CH * c:CH * c + CH], op0=ALU.mult, op1=ALU.mult
                                             ).then_inc(s_o1, 1)

                def residual(c):
                    dve.wait_ge(s_o1T, at(s_o1T, b, c + 1))
                    v = xr[:, TPC * c:TPC * c + TPC, :]
                    dve.tensor_tensor(v, v, bank_of(("o1T", c)).rearrange("p (i d) -> p i d", i=TPC), ALU.add
                                      ).then_inc(s_xr2, 1)

                def after(n):
                    for lag, step in ((LAG1[0], y_sum), (LAG1[2], gate), (LAG1[4], residual)):
                        if n is None:
                            step(NC - 1)
                        elif n > HALF and (n - lag) % HALF == 0:
                            step((n - lag) // HALF - 1)
                return after

            def route(b, f):
                base = sum(N_ROUTE[:f])
                steps = [base]

                def done(ins):
                    ins.then_inc(s_route, 1)
                    steps[0] += 1

                def need():
                    dve.wait_ge(s_route, at(s_route, b, steps[0]))

                def bc(v):
                    return v.unsqueeze(2).to_broadcast([P, TILES, NE])

                dve.wait_ge(s_lg, at(s_lg, b, f + 1))
                width = NE + 1 if f == 0 else NE
                v = bank_of(("lg", f))[:, 0:TILES * width].rearrange("p (i e) -> p i e", i=TILES)
                dve.wait_ge(s_combT, at(s_combT, b, NC * f))
                dve.wait_ge(s_erep, at(s_erep, b, 0))
                need()
                if f == 0:
                    done(dve.tensor_reduce(mx[:], v[:, :, 0:NE], AX.X, ALU.max))
                    need()
                    done(dve.tensor_tensor(lg[:], v[:, :, 0:NE], bc(mx[:]), ALU.subtract))
                    done(dve.tensor_copy(sg[:], v[:, :, NE]))
                else:
                    done(dve.tensor_tensor(lg[:], v, gate_b1[:].unsqueeze(1).to_broadcast([P, TILES, NE]), ALU.add))
                    need()
                    done(dve.tensor_reduce(mx[:], lg[:], AX.X, ALU.max))
                    need()
                    done(dve.tensor_tensor(lg[:], lg[:], bc(mx[:]), ALU.subtract))
                need()
                dve.wait_ge(s_ex, at(s_ex, b, f + 1))
                done(dve.tensor_reduce(mx[:], ex[:], AX.X, ALU.add))
                need()
                done(dve.reciprocal(mx[:], mx[:]))
                need()
                done(dve.tensor_tensor(pr[:], ex[:], bc(mx[:]), ALU.mult))
                rv = rev[:].unsqueeze(1).to_broadcast([P, TILES, NE])

                def largest(dst):
                    need()
                    done(dve.tensor_reduce(mx[:], ex[:], AX.X, ALU.max))
                    need()
                    done(dve.tensor_tensor(key[:], ex[:], bc(mx[:]), ALU.is_equal))
                    need()
                    done(dve.tensor_tensor(key[:], key[:], rv, ALU.mult))
                    need()
                    done(dve.tensor_reduce(mx[:], key[:], AX.X, ALU.max))
                    need()
                    done(dve.tensor_tensor(dst[:], key[:], bc(mx[:]), ALU.is_equal))

                largest(pick1)
                need()
                done(dve.scalar_tensor_tensor(out=ex[:], in0=pick1[:], scalar=-4.0, in1=ex[:], op0=ALU.mult, op1=ALU.add))
                largest(pick2)
                need()
                done(dve.tensor_tensor(pick1[:], pick1[:], pick2[:], ALU.add))
                need()
                done(dve.tensor_tensor(comb[:, :, 0:NE], pick1[:], pr[:], ALU.mult))
                if f == 0:
                    dve.wait_ge(s_sg, at(s_sg, b, 1))
                    done(dve.tensor_scalar(sg[:], sg[:], 1.0, None, ALU.add))
                    need()
                    done(dve.reciprocal(comb[:, :, NE], sg[:]))
                assert steps[0] == base + N_ROUTE[f], steps

            def ffn_scale(b, f, c):
                dve.wait_ge(s_hwu, at(s_hwu, b, NE * c + NE + (NC * (NE + 1) if f else c + 1)))
                dve.wait_ge(s_xr1, at(s_xr1, b, c if f == 0 else NC))
                if f:
                    dve.wait_ge(s_xo, at(s_xo, b, c))
                else:
                    dve.wait_ge(s_xo, at(s_xo, b, 0))
                dve.tensor_tensor(ffn[:], bank_of(("acc", NC * f + c)).rearrange("p (i d) -> p i d", i=TPC),
                                  gates[:, 1 + f, bass.ds(b, 1), :].to_broadcast([P, TPC, D]), ALU.mult).then_inc(s_ffn, 1)

            with dve.Fori(0, NB) as b:
                dve.wait_ge(s_x, at(s_x, b, 16))
                norm_stats(b, 0, xa)
                for c in range(NC):
                    for m in range(H0):
                        time_step(b, c * H0 + m, b_dt0[:, m:m + 1], 0.0, m, c)
                scans(b, 0, y0(b))
                dve.wait_ge(s_xr0, at(s_xr0, b, NC))
                norm_stats(b, 1, xr)
                route(b, 0)
                for c in range(NC):
                    for e in range(NE):
                        n = c * (NE + 1) + e
                        dve.wait_ge(s_h1a, at(s_h1a, b, n + 1))
                        dve.wait_ge(s_crow[n % 3], at(s_crow[n % 3], b, 16 * (n // 3 + 1)))
                        dve.wait_ge(s_hwu, at(s_hwu, b, n - (e > 0)))
                        dve.tensor_tensor(hw[:, e % 2, :], bank_of(("h1", c, e)), comb_rep[:, n % 3, :], ALU.mult
                                          ).then_inc(s_hw, 1)
                    dve.wait_ge(s_h1, at(s_h1, b, (NE + 2) * (c + 1)))
                    dve.wait_ge(s_h1a, at(s_h1a, b, (NE + 1) * (c + 1)))
                    dve.wait_ge(s_hws, at(s_hws, b, c))
                    dve.tensor_tensor(shared[:], bank_of(("h1", c, NE + 1)), gate_act[:], ALU.mult).then_inc(s_sh, 1)
                    ffn_scale(b, 0, c)
                dve.wait_ge(s_xr1, at(s_xr1, b, NC))
                norm_stats(b, 2, xr)
                for c in range(NC):
                    time_step(b, NC * H0 + c, b_dt1[:, 0:1], EPS, 0, c)
                scans(b, 1, y1_(b))
                dve.wait_ge(s_xr2, at(s_xr2, b, NC))
                norm_stats(b, 3, xr)
                route(b, 1)
                for c in range(NC):
                    for e in range(NE):
                        dve.wait_ge(s_erep, at(s_erep, b, NE * c + e + 1))
                        dve.wait_ge(s_hwu, at(s_hwu, b, NC * (NE + 1) + NE * c + e - (e > 0)))
                        dve.tensor_tensor(hw[:, e % 2, :], bank_of(("erep", c, e)), hT[:, 3 + CH * c:3 + CH * c + CH],
                                          ALU.mult).then_inc(s_hw, 1)
                    ffn_scale(b, 1, c)

        @block.tensor
        def _(pe):
            pe.wait_ge(s_load, N_LOAD)
            pe.wait_ge(s_setup_act, 1)
            for lay in range(2):
                for j in range(6):
                    ins = pe.matmul(mm[:, lay, NB * j:NB * j + NB], w_mod[:, lay, D * j:D * j + D], silu_c[:, lay, :],
                                    start=True, stop=True)
                ins.then_inc(s_setup_pe, 1)
            pe.matmul(mm[:, 2, 0:D], w_x1dt[:], w_dt1[:], start=True, stop=True)
            pe.matmul(mm[:, 2, D:2 * D], w_x1c[:], w_c1[:], start=True, stop=True).then_inc(s_setup_pe, 1)
            for g, (lay, j) in enumerate(((0, 2), (0, 5), (1, 5))):
                for q in range(2):
                    pe.wait_ge(s_setup, N_MODS + 2 * (g - 1) + q + 1 if g else N_COPIED)
                    for i in range(NB // 2):
                        bb = NB // 2 * q + i
                        ins = pe.matmul(mm[:, q, D * i:D * i + D], silu_c[:, lay, bb:bb + 1].to_broadcast([P, P]),
                                        w_mod[:, lay, D * j:D * j + D], start=True, stop=True)
                    ins.then_inc(s_setup_pe, 1)
            pe.wait_ge(s_setup, N_SETUP)
            pe.wait_ge(s_const, N_CONST)

            def norm_T(b, l):
                pe.wait_ge(s_xn, at(s_xn, b, l + 1))
                for c in range(NC):
                    v = claim(pe, b, ("norm", l, c))
                    for i in range(TPC):
                        ins = pe.transpose(v[:, P * i:P * i + P], xn[:, TPC * c + i, :], ident[:])
                    ins.then_inc(s_xnT, 1)

            def conv(v, w_taps, taps, first, c, m):
                for k in range(taps):
                    o = 3 + CH * c + k - first
                    ins = pe.matmul(v, w_taps[:, k, P * m:P * m + P], hT[:, o:o + CH], start=(k == 0), stop=(k == taps - 1))
                return ins

            def scan_sums(b, lay):
                base = KS0 if lay else 0
                kn = KPH if lay else H0 * KPH

                def replicate(j):
                    c, k = (j - base) // kn, (j - base) % kn
                    m = k // KPH
                    pe.wait_ge(s_dtx, at(s_dtx, b, NC * H0 + c + 1 if lay else c * H0 + m + 1))
                    if j >= 2:
                        pe.wait_ge(s_u, at(s_u, b, SHI * (j - 1)))
                    else:
                        pe.wait_ge(s_u, at(s_u, b, 0))
                    pe.matmul(dtx_rep[:, j % 2, :], rep[:, k % KPH, :], dtx[:, m, CH * c:CH * c + CH],
                              start=True, stop=True).then_inc(s_dtxrep, 1)

                def out0(c):
                    pe.wait_ge(s_wg, at(s_wg, b, 1))
                    pe.wait_ge(s_y2, at(s_y2, b, H0 * (c + 1)))
                    v = claim(pe, b, ("out0", c))
                    for i in range(TPC):
                        for m in range(H0):
                            ins = pe.matmul(v[:, D * i:D * i + D], y2[:, m, P * i:P * i + P], w_out0g[:, m, :],
                                            start=(m == 0), stop=(m == H0 - 1))
                    ins.then_inc(s_out0, 1)

                def out1(c):
                    pe.wait_ge(s_y1, at(s_y1, b, NC * H0 + c + 1))
                    v = claim(pe, b, ("out1", c))
                    pe.matmul(v, w_out1[:], y1[:], start=True, stop=True).then_inc(s_out1, 1)

                def out1_T(c):
                    pe.wait_ge(s_o1, at(s_o1, b, c + 1))
                    v = claim(pe, b, ("o1T", c))
                    for i in range(TPC):
                        ins = pe.transpose(v[:, D * i:D * i + D], y2[:, 0, P * i:P * i + P], ident[:])
                    ins.then_inc(s_o1T, 1)

                steps = ((LAG1[1], out1), (LAG1[3], out1_T)) if lay else ((LAG_OUT, out0),)

                replicate(base)
                for j in range(base, base + NC * kn):
                    if j + 1 < base + NC * kn:
                        replicate(j + 1)
                    kk, half = j % KPH, j // KPH
                    for i in range(SHI):
                        n = SHI * j + i
                        if lay == 0:
                            pe.wait_ge(s_hc, at(s_hc, b, n + 1))
                        else:
                            pe.wait_ge(s_scan, at(s_scan, b, n + 1))
                        if kk == 0 and i == 0:
                            pe.wait_ge(s_y1, at(s_y1, b, half))
                        src = hc[:, n % CR, :] if lay == 0 else h[:, n % HR, :]
                        pe.matmul(ysum[R * kk:R * kk + R, :], state_sum[:], src, start=(i == 0), stop=(i == SHI - 1)
                                  ).then_inc(s_hsum, 1)
                        done, chunk = n + 1 - SHI * base, SHI * kn
                        for lag, step in steps:
                            if done > chunk and (done - lag) % chunk == 0:
                                step((done - lag) // chunk - 1)
                for _, step in steps:
                    step(NC - 1)

            def router_T(b, f, width):
                for c in range(NC):
                    v = claim(pe, b, ("combT", NC * f + c))
                    for i in range(TPC):
                        ins = pe.transpose(v[0:width, P * i:P * i + P], comb[:, TPC * c + i, 0:width], ident[:])
                    ins.then_inc(s_combT, 1)

            with pe.Fori(0, NB) as b:
                norm_T(b, 0)
                for c in range(NC):
                    pe.wait_ge(s_hT, at(s_hT, b, NC))
                    for m in range(H0):
                        v = claim(pe, b, ("in", c * 2 * H0 + m))
                        conv(v, w_conv0, TAPS0, TAPS0 - 1, c, m).then_inc(s_in, 1)
                    for m in range(H0):
                        v = claim(pe, b, ("in", c * 2 * H0 + H0 + m))
                        pe.matmul(v, w_in0[:, DI + P * m:DI + P * m + P], hT[:, 3 + CH * c:3 + CH * c + CH],
                                  start=True, stop=True).then_inc(s_in, 1)
                for c in range(NC):
                    pe.wait_ge(s_in_act, at(s_in_act, b, XS0[c * H0 + H0 - 1]))
                    v = claim(pe, b, ("xdbl", c))
                    for m in range(H0):
                        ins = pe.matmul(v[0:1 + 2 * NS, :], w_x0[:, m, :], xs[:, m, CH * c:CH * c + CH],
                                        start=(m == 0), stop=(m == H0 - 1))
                    ins.then_inc(s_xdbl, 1)
                for c in range(NC):
                    pe.wait_ge(s_xdbl_act, at(s_xdbl_act, b, c + 1))
                    for m in range(H0):
                        v = claim(pe, b, ("dtpre", c * H0 + m))
                        pe.matmul(v, w_dt0[0:1, P * m:P * m + P], xdbl[0:1, CH * c:CH * c + CH],
                                  start=True, stop=True).then_inc(s_dtpre, 1)
                scan_sums(b, 0)
                norm_T(b, 1)
                pe.wait_ge(s_hT, at(s_hT, b, 2 * NC))
                v = claim(pe, b, ("lg", 0))
                for i in range(TILES):
                    ins = pe.matmul(v[:, (NE + 1) * i:(NE + 1) * (i + 1)], hT[:, 3 + P * i:3 + P * i + P], router[:],
                                    start=True, stop=True)
                ins.then_inc(s_lg, 1)
                pe.wait_ge(s_route, at(s_route, b, N_ROUTE[0]))
                router_T(b, 0, NE + 1)
                for c in range(NC):
                    acc = claim(pe, b, ("acc", c))

                    def second(e):
                        n = c * (NE + 1) + e
                        if e < NE:
                            pe.wait_ge(s_hw, at(s_hw, b, NE * c + e + 1))
                        else:
                            pe.wait_ge(s_hws, at(s_hws, b, c + 1))
                        for i in range(TPC):
                            ins = pe.matmul(acc[:, D * i:D * i + D], hw[:, e % 2, P * i:P * i + P], w2[:, e, :],
                                            start=(e == 0 and i == 0), stop=(e == NE), skip_group_check=True)
                        ins.then_inc(s_hwu, 1)

                    for e in range(NE + 2):
                        v = claim(pe, b, ("h1", c, e))
                        pe.matmul(v, w1[:, e, :], hT[:, 3 + CH * c:3 + CH * c + CH], start=True, stop=True).then_inc(s_h1, 1)
                        if e >= 1 and e <= NE:
                            second(e - 1)
                    second(NE)
                norm_T(b, 2)
                for c in range(NC):
                    pe.wait_ge(s_hT, at(s_hT, b, 3 * NC))
                    v = claim(pe, b, ("in", NC * 2 * H0 + 2 * c))
                    conv(v, w_conv1, TAPS1, TAPS1 // 2, c, 0).then_inc(s_in, 1)
                    v = claim(pe, b, ("in", NC * 2 * H0 + 2 * c + 1))
                    pe.matmul(v, w_in1[:, D:2 * D], hT[:, 3 + CH * c:3 + CH * c + CH], start=True, stop=True).then_inc(s_in, 1)
                for c in range(NC):
                    pe.wait_ge(s_in_act, at(s_in_act, b, XS1[c]))
                    v = claim(pe, b, ("xdbl", NC + c))
                    pe.matmul(v[0:NS, :], w_x1b[:], xs[:, 0, CH * c:CH * c + CH], start=True, stop=True).then_inc(s_xdbl, 1)
                for c in range(NC):
                    v = claim(pe, b, ("cmat", c))
                    pe.matmul(v, w_cx1[:], xs[:, 0, CH * c:CH * c + CH], start=True, stop=True).then_inc(s_cpe, 1)
                for c in range(NC):
                    v = claim(pe, b, ("dtpre", NC * H0 + c))
                    pe.matmul(v, w_dtx1[:], xs[:, 0, CH * c:CH * c + CH], start=True, stop=True).then_inc(s_dtpre, 1)
                scan_sums(b, 1)
                norm_T(b, 3)
                pe.wait_ge(s_hT, at(s_hT, b, 4 * NC))
                v = claim(pe, b, ("lg", 1))
                for i in range(TILES):
                    ins = pe.matmul(v[:, NE * i:NE * (i + 1)], hT[:, 3 + P * i:3 + P * i + P], gate_w1[:],
                                    start=True, stop=True)
                ins.then_inc(s_lg, 1)
                pe.wait_ge(s_route, at(s_route, b, sum(N_ROUTE)))
                router_T(b, 1, NE)
                for c in range(NC):
                    acc = claim(pe, b, ("acc", NC + c))
                    pe.wait_ge(s_combT_act, at(s_combT_act, b, NC + c + 1))
                    for i in range(TPC):
                        pe.matmul(acc[:, D * i:D * i + D], combT[0:NE, CH * c + P * i:CH * c + P * i + P], b_e1[:],
                                  start=(i == 0), stop=False, skip_group_check=True)

                    def second1(e):
                        pe.wait_ge(s_hw, at(s_hw, b, NC * NE + NE * c + e + 1))
                        for i in range(TPC):
                            ins = pe.matmul(acc[:, D * i:D * i + D], hw[:, e % 2, P * i:P * i + P], w_e1[:, e, :],
                                            start=False, stop=(e == NE - 1), skip_group_check=True)
                        ins.then_inc(s_hwu, 1)

                    for e in range(NE):
                        v = claim(pe, b, ("erep", c, e))
                        for i in range(TPC):
                            ins = pe.transpose(v[:, P * i:P * i + P], comb[:, TPC * c + i, e:e + 1].to_broadcast([P, P]), ident[:])
                        ins.then_inc(s_erep, 1)
                        if e:
                            second1(e - 1)
                    second1(NE - 1)


_NAMES = ["w_in0", "conv0", "conv_b0", "w_x0", "w_dt0", "b_dt0", "a_log0", "d0", "w_out0", "router", "w1", "w2", "w_in1",
          "conv1", "w_x1dt", "w_x1b", "w_x1c", "w_dt1", "w_c1", "b_dt1", "a_log1", "d1", "w_out1", "gate_w1", "gate_b1",
          "w_e1", "b_e1", "c_t", "w_mod"]


def kernel(**inputs):
    import numpy as _np
    import concourse.bacc as _bacc
    from concourse.bass_utils import run_bass_kernel_spmd as _run

    g = {k: _np.asarray(v) for k, v in inputs.items()}

    def halves(a):
        return a.reshape((H0, P) + a.shape[1:]).swapaxes(0, 1)

    def blocks(a):
        return a.reshape(-1, R, SLO, SHI).transpose(2, 1, 0, 3).reshape(P, -1, SHI)

    wx1 = g["L1_attn_W_x"]
    sgu = g["L0_ffn_shared_gate_up"].reshape(D, 2, P)
    laid = {
        "w_in0": g["L0_attn_W_in"],
        "conv0": g["L0_attn_conv_w"].reshape(DI, TAPS0).T,
        "conv_b0": g["L0_attn_conv_b"].reshape(H0, P).T,
        "w_x0": halves(g["L0_attn_W_x"]),
        "w_dt0": g["L0_attn_W_dt"],
        "b_dt0": g["L0_attn_b_dt"].reshape(H0, P).T,
        "a_log0": blocks(g["L0_attn_A_log"]),
        "d0": g["L0_attn_D_param"].reshape(H0, P).T,
        "w_out0": halves(g["L0_attn_W_out"]),
        "router": _np.concatenate([g["L0_ffn_router_w"], g["L0_ffn_shared_gate_w"]], axis=1),
        "w1": _np.concatenate([g["L0_ffn_w1"].transpose(1, 0, 2), sgu], axis=1),
        "w2": _np.concatenate([g["L0_ffn_w2"].transpose(1, 0, 2), g["L0_ffn_shared_down"][:, None, :]], axis=1),
        "w_in1": g["L1_attn_W_in"].T,
        "conv1": g["L1_attn_conv_w"].T,
        "w_x1dt": wx1[:R1],
        "w_x1b": wx1[R1:R1 + NS].T,
        "w_x1c": wx1[R1 + NS:],
        "w_dt1": g["L1_attn_W_dt"].T,
        "w_c1": g["L1_attn_W_C"].T,
        "b_dt1": g["L1_attn_b_dt"].reshape(P, 1),
        "a_log1": blocks(g["L1_attn_A_log"]),
        "d1": g["L1_attn_D_param"].reshape(P, 1),
        "w_out1": g["L1_attn_W_out"].T,
        "gate_w1": g["L1_ffn_gate_w"].T,
        "gate_b1": g["L1_ffn_gate_b"],
        "w_e1": g["L1_ffn_expert_w"].transpose(2, 0, 1),
        "b_e1": g["L1_ffn_expert_b"],
        "c_t": _np.stack([g["L0_c"].T, g["L1_c"].T], axis=1),
        "w_mod": _np.stack([g["L0_wmod"], g["L1_wmod"]], axis=1),
    }
    nc = _bacc.Bacc("TRN2", target_bir_lowering=False, num_devices=1)
    arrays, w = {}, {}
    for name in _NAMES:
        a = _np.ascontiguousarray(laid[name])
        arrays[f"in_{name}"] = a
        w[name] = nc.dram_tensor(f"in_{name}", a.shape, mybir.dt.from_np(a.dtype), kind="ExternalInput").ap()
    x = _np.ascontiguousarray(g["L0_attn_x"])
    arrays["in_x"] = x
    x_ap = nc.dram_tensor("in_x", x.shape, F32, kind="ExternalInput").ap()
    out = nc.dram_tensor("out_0", (NB, T, D), F32, kind="ExternalOutput").ap()
    rows = nc.dram_tensor("rows", (1 + 2 * NS, T), F32, kind="Internal").ap()
    comb = nc.dram_tensor("comb_rows", (NE + 1, T), F32, kind="Internal").ap()
    adaln_blocks(nc, x_ap, w, rows, comb, out)
    r = _run(nc, [arrays], core_ids=[0])
    return r.results[0]["out_0"]
```

```python
from contextlib import ExitStack

import concourse.bass as bass
from concourse import mybir

F32 = mybir.dt.float32
ALU = mybir.AluOpType
ACT = mybir.ActivationFunctionType
AX = mybir.AxisListType

P = 128
NB = 8
T = 1024
D = 128
DI = 256
NS = 16
NE = 8
R1 = 64
TILES = T // P
CH = 512
NC = T // CH
TPC = CH // P
H0 = DI // P
SHI = 4
SLO = NS // SHI
R = P // SLO
KPH = P // R
TAPS0 = 4
TAPS1 = 3
GATE_MIN = 0.25
EPS = 1e-5
MB = 3
HALF = KPH * SHI
S0 = KPH * H0 * NC * SHI
S1 = KPH * NC * SHI
KS0 = S0 // SHI
KS1 = S1 // SHI
HR = 4
CR = 3
DR = 4


def adaln_blocks(nc, x_in, w, rows0_dram, rows1_dram, comb0_dram, comb1_dram, gates_dram, out):
    with ExitStack() as ctx:
        def sb(name, shape):
            return ctx.enter_context(nc.sbuf_tensor(name, shape, F32))

        def ps(name, shape):
            return ctx.enter_context(nc.psum_tensor(name, shape, F32))

        per = {}
        counted = []

        def sem(name, per_pass=True):
            s = ctx.enter_context(nc.semaphore(name))
            per[s.name] = 0
            if per_pass:
                counted.append(s)
            return s

        def at(s, t, n):
            return t * per[s.name] + n + 1

        w_in0 = sb("w_in0", [P, 2 * DI])
        conv_b0 = sb("conv_b0", [P, H0])
        w_x0 = sb("w_x0", [P, H0, 1 + 2 * NS])
        w_dt0 = sb("w_dt0", [1, DI])
        b_dt0 = sb("b_dt0", [P, H0])
        a_log0 = sb("a_log0", [P, H0 * KPH, SHI])
        d0 = sb("d0", [P, H0])
        w_out0 = sb("w_out0", [P, H0, D])
        router = sb("router", [P, NE + 1])
        w1 = sb("w1", [P, NE + 2, P])
        w2 = sb("w2", [P, NE + 1, D])
        w_in1 = sb("w_in1", [P, 2 * D])
        w_x1dt = sb("w_x1dt", [R1, D])
        w_x1b = sb("w_x1b", [P, NS])
        w_x1c = sb("w_x1c", [NS, D])
        w_dt1 = sb("w_dt1", [R1, D])
        w_c1 = sb("w_c1", [NS, D])
        b_dt1 = sb("b_dt1", [P, 1])
        a_log1 = sb("a_log1", [P, KPH, SHI])
        d1 = sb("d1", [P, 1])
        w_out1 = sb("w_out1", [P, D])
        gate_w1 = sb("gate_w1", [P, NE])
        gate_b1 = sb("gate_b1", [P, NE])
        w_e1 = sb("w_e1", [P, NE, D])
        b_e1 = sb("b_e1", [NE, D])
        c_t = sb("c_t", [P, 2, NB])

        ident = sb("ident", [P, P])
        rep = sb("rep", [P, KPH, P])
        state_sum = sb("state_sum", [P, R])
        rev = sb("rev", [P, NE])
        w_conv0 = sb("w_conv0", [P, TAPS0, DI])
        w_conv1 = sb("w_conv1", [P, TAPS1, D])
        neg_a0 = sb("neg_a0", [P, H0 * KPH, SHI])
        neg_a1 = sb("neg_a1", [P, KPH, SHI])
        w_dtx1 = sb("w_dtx1", [P, D])
        w_cx1 = sb("w_cx1", [P, D])
        silu_c = sb("silu_c", [P, 2, NB])
        mods = sb("mods", [P, 2, 6, NB])
        gate_a = sb("gate_a", [P, 1, D])
        gate_b = sb("gate_b", [P, 2, D])
        eps8 = sb("eps8", [P, TILES])
        neg_half = sb("neg_half", [P, TILES])
        neg_one = sb("neg_one", [P, TILES])

        xa = sb("xa", [P, TILES, D])
        xr0 = sb("xr0", [P, TILES, D])
        xr1 = sb("xr1", [P, TILES, D])
        xr2 = sb("xr2", [P, TILES, D])
        stats = sb("stats", [P, TILES, 6])
        mean_var = sb("mean_var", [P, TILES, 2])
        var_eps = sb("var_eps", [P, TILES])
        rstd = sb("rstd", [P, TILES])
        shift = sb("shift", [P, TILES])
        xn = sb("xn", [P, TILES, D])
        hTa = sb("hTa", [P, T + 4])
        hTb = sb("hTb", [P, T + 4])
        xs = sb("xs", [P, H0, T])
        zs = sb("zs", [P, H0, T])
        xs1 = sb("xs1", [P, T])
        zs1 = sb("zs1", [P, T])
        conv0_bc = zs[:, 0, :].rearrange("p (k d) -> p k d", k=TAPS0)
        conv1_bc = zs[:, 1, 0:TAPS1 * D].rearrange("p (k d) -> p k d", k=TAPS1)
        xdbl = sb("xdbl", [1 + 2 * NS, T])
        dt = sb("dt", [P, H0, T])
        dtx = sb("dtx", [P, H0, T])
        dt1 = sb("dt1", [P, T])
        dtx1 = sb("dtx1", [P, T])
        gate_tmp = dtx[:, 0, :]
        b_rep = sb("b_rep", [P, NC, SHI, CH])
        c_rep = sb("c_rep", [P, SHI, T])
        w_mod = b_rep[:].rearrange("p c s t -> p (c s t)")[:, 0:2 * 6 * D].rearrange("p (l d) -> p l d", l=2)
        gates = c_rep[:].rearrange("p s t -> p (s t)")[:, 0:3 * NB * D].rearrange("p (g b d) -> p g b d", g=3, b=NB)
        dt_rep = sb("dt_rep", [P, 2, CH])
        carry = sb("carry", [P, H0 * KPH, SHI])
        da = sb("da", [P, DR, CH])
        h = sb("h", [P, HR, CH])
        hc = sb("hc", [P, CR, CH])
        y1 = sb("y1", [P, CH])
        y2 = sb("y2", [P, H0, CH])
        w_out0g = sb("w_out0g", [P, H0, D])
        c_mat = sb("c_mat", [P, T])
        mx = sb("mx", [P, TILES])
        lg = sb("lg", [P, TILES, NE])
        ex = sb("ex", [P, TILES, NE])
        sg = sb("sg", [P, TILES])
        pr = sb("pr", [P, TILES, NE])
        key = sb("key", [P, TILES, NE])
        pick1 = sb("pick1", [P, TILES, NE])
        pick2 = sb("pick2", [P, TILES, NE])
        comb0 = sb("comb0", [P, TILES, NE + 1])
        comb1 = sb("comb1", [P, TILES, NE])
        combT = sb("combT", [NE + 1, T])
        comb_rep = sb("comb_rep", [P, 3, CH])
        hw = sb("hw", [P, 2, CH])
        gate_act = sb("gate_act", [P, CH])
        shared = sb("shared", [P, CH])
        ffn = sb("ffn", [P, TPC, D])

        u = ps("u", [P, 2, CH])
        dtx_rep = ps("dtx_rep", [P, 2, CH])
        ysum = ps("ysum", [P, CH])
        mm = ps("mm", [P, MB, CH])

        s_load = sem("s_load", False)
        s_const = sem("s_const", False)
        s_setup_pe = sem("s_setup_pe", False)
        s_setup_act = sem("s_setup_act", False)
        s_setup = sem("s_setup", False)
        s_gstore = sem("s_gstore", False)
        s_x = sem("s_x")
        s_keep = [sem(f"s_keep{c}") for c in range(NC)]
        s_stats = sem("s_stats")
        s_rstd = sem("s_rstd")
        s_xn = sem("s_xn")
        s_xnT = sem("s_xnT")
        s_hT = sem("s_hT")
        s_in = sem("s_in")
        s_in_act = sem("s_in_act")
        s_xdbl = sem("s_xdbl")
        s_xdbl_act = sem("s_xdbl_act")
        s_cpe = sem("s_cpe")
        s_cmat = sem("s_cmat")
        s_dtpre = sem("s_dtpre")
        s_pre = sem("s_pre")
        s_soft = sem("s_soft")
        s_dt = sem("s_dt")
        s_dtx = sem("s_dtx")
        s_brep = [[sem(f"s_brep{lay}{c}") for c in range(NC)] for lay in range(2)]
        s_crep = sem("s_crep")
        s_rows = [sem(f"s_rows{lay}") for lay in range(2)]
        s_comb_row = [[sem(f"s_comb_row{f}{c}") for c in range(NC)] for f in range(2)]
        s_gate = [sem(f"s_gate{g}") for g in range(3)]
        s_dtrep = [sem(f"s_dtrep{i}") for i in range(2)]
        s_dtxrep = sem("s_dtxrep")
        s_da = sem("s_da")
        s_u = sem("s_u")
        s_scan = sem("s_scan")
        s_carry = sem("s_carry")
        s_hc = sem("s_hc")
        s_hsum = sem("s_hsum")
        s_y1 = sem("s_y1")
        s_y2 = sem("s_y2")
        s_wg = sem("s_wg")
        s_out0 = sem("s_out0")
        s_xr0 = sem("s_xr0")
        s_cy = sem("s_cy")
        s_out1 = sem("s_out1")
        s_o1 = sem("s_o1")
        s_o1T = sem("s_o1T")
        s_xr2 = sem("s_xr2")
        s_lg = sem("s_lg")
        s_route = sem("s_route")
        s_ex = sem("s_ex")
        s_sg = sem("s_sg")
        s_combT = sem("s_combT")
        s_combT_act = sem("s_combT_act")
        s_crow = [sem(f"s_crow{i}") for i in range(3)]
        s_h1 = sem("s_h1")
        s_h1a = sem("s_h1a")
        s_sh = sem("s_sh")
        s_hw = sem("s_hw")
        s_hws = sem("s_hws")
        s_hwu = sem("s_hwu")
        s_hw1 = sem("s_hw1")
        s_ffn = sem("s_ffn")
        s_xr1 = sem("s_xr1")
        s_xo = sem("s_xo")
        s_store = [sem(f"s_store{c}") for c in range(NC)]
        N_CONST = 8 + NE + 1 + KPH + SLO + TAPS0 + TAPS1
        N_COPIED = 6
        N_MODS = N_COPIED + 4 + 4
        N_SETUP = N_MODS + 3 * 2 + 3 * 4
        IN0, SCAN0, MOE0, IN1, SCAN1, MOE1 = "in0", "scan0", "moe0", "in1", "scan1", "moe1"
        LAG = {IN0: 0, SCAN0: 1, MOE0: 2, IN1: 2, SCAN1: 2, MOE1: 3}
        STEPS = S0 + S1
        N_MOE0, N_MOE1, N_IN1, N_IN0 = range(4)
        NORM_MODS = {N_MOE0: (0, 3, MOE0), N_MOE1: (1, 3, MOE1), N_IN1: (1, 0, IN1), N_IN0: (0, 0, IN0)}
        IN_1 = {("xs", c): c for c in range(NC)} | {("zs", c): NC + c for c in range(NC)}
        IN_0 = {("xs", c, m): 2 * NC + 2 * H0 * c + m for c in range(NC) for m in range(H0)} | \
               {("zs", c, m): 2 * NC + 2 * H0 * c + H0 + m for c in range(NC) for m in range(H0)}
        N_ROUTE = (21, 19)
        EXP0 = NE + 1

        def pair_step(k):
            return 13 + 3 * k + (k >= 1) + 2 * (k >= 8)

        PLAN = []

        def plan(stage, engine, step, piece, *args):
            PLAN.append((step, stage, engine, piece, args))

        def plan_norm(stage, pos, at_step):
            plan(stage, "dve", at_step, "stats", pos)
            plan(stage, "pool", at_step + 1, "rstd", pos)
            for c in range(NC):
                plan(stage, "act", at_step + 3, "norm", pos, c)
                plan(stage, "pe", at_step + 4, "xnT", pos, c)
                plan(stage, "act", at_step + 5, "hT", pos, c)

        def plan_router(stage, f, at_step):
            plan(stage, "pe", at_step, "lg", f)
            plan(stage, "dve", at_step + 1, "route_max", f)
            plan(stage, "act", at_step + 2, "ex", f)
            plan(stage, "dve", at_step + 3, "route_first", f)
            plan(stage, "dve", at_step + 4, "route_second", f)
            for c in range(NC):
                plan(stage, "pe", at_step + 5, "combT", f, c)
                plan(stage, "act", at_step + 5, "combT", f, c)

        plan(SCAN0, "sp", 0, "gate_load", 0)
        plan(SCAN0, "sp", 0, "fill_b", 0, 1)
        plan(MOE0, "sp", 0, "gate_load", 1)
        plan(MOE1, "sp", 0, "gate_load", 2)
        plan_norm(MOE0, N_MOE0, 0)
        plan(SCAN0, "pool", 4, "w_gate")
        plan_norm(MOE1, N_MOE1, 2)
        plan_router(MOE0, 0, 6)
        plan_router(MOE1, 1, 11)
        for c in range(NC):
            plan(MOE1, "sp", 17, "comb_store", 1, c)
        for c in range(NC):
            plan(MOE0, "sp", 11, "comb_store", 0, c)
        for c in range(NC):
            for p in range((NE + 2) // 2):
                s = pair_step(c * (NE + 2) // 2 + p)
                for e in (2 * p, 2 * p + 1):
                    plan(MOE0, "pe", s, "h1", c, e)
                    if e < EXP0:
                        plan(MOE0, "act", s + 1, "silu_h", c, e)
                    if e < NE:
                        plan(MOE0, "dve", s + 2, "hw0", c, e)
                        plan(MOE0, "pe", s + 3, "second0", c, e)
                    if e < EXP0:
                        n = c * EXP0 + e - 3
                        cc, ee = n // EXP0, n % EXP0
                        r = 11 if n < 0 else pair_step(cc * (NE + 2) // 2 + ee // 2) + 2 + (ee == NE)
                        plan(MOE0, "sp", r, "comb_rep", c * EXP0 + e)
            plan(MOE0, "dve", s + 2, "shared", c)
            plan(MOE0, "pool", s + 3, "hws", c)
            plan(MOE0, "pe", s + 4, "second0", c, NE)
            plan(MOE0, "dve", s + 5, "scale", 0, c)
            plan(MOE0, "pool", s + 6, "moe_sum", 0, c)
            plan(SCAN0, "sp", s + 6, "keep_x", c)
        plan(IN0, "sp", s + 7, "load_x")

        plan_norm(IN1, N_IN1, s + 7)
        o = s + 13
        for c in range(NC):
            plan(IN1, "pe", o, "in1", "xs", c)
            plan(IN1, "act", o + 1, "silu1", "xs", c)
        for c in range(NC):
            plan(IN1, "pe", o + 2, "in1", "zs", c)
            plan(IN1, "act", o + 2, "silu1", "zs", c)
        for c in range(NC):
            plan(IN1, "pe", o + 3, "xdbl1", c)
            plan(IN1, "act", o + 3, "xdbl1", c)
        for c in range(NC):
            plan(IN1, "pe", o + 4, "dtpre1", c)
            plan(IN1, "act", o + 4, "relu_abs1", c)
        plan(IN1, "act", o + 5, "soft", 1)
        for c in range(NC):
            plan(IN1, "pe", o + 5, "cmat", c)
            plan(IN1, "act", o + 5, "cmat", c)
            plan(IN1, "dve", o + 6, "step1", c)
            plan(IN1, "pool", o + 7, "dtx1", c)
        plan(IN1, "sp", o, "rows", 1)
        plan(IN1, "sp", o, "fill_b", 1, 0)
        plan(SCAN1, "sp", S0, "fill_b", 1, 1)

        plan_norm(IN0, N_IN0, S0 - 5)
        for c in range(NC):
            o = S0 + 1 + 7 * c
            for m in range(H0):
                plan(IN0, "pe", o, "in0", "xs", c, m)
                plan(IN0, "act", o + 2, "silu0", "xs", c, m)
            for m in range(H0):
                plan(IN0, "pe", o + 3, "in0", "zs", c, m)
                plan(IN0, "act", o + 4, "silu0", "zs", c, m)
        o = S0 + 13
        for c in range(NC):
            plan(IN0, "pe", o, "xdbl0", c)
            plan(IN0, "act", o + 1, "xdbl0", c)
        for c in range(NC):
            for m in range(H0):
                plan(IN0, "pe", o + 2 + 2 * c, "dtpre0", c, m)
                plan(IN0, "act", o + 3 + 2 * c, "relu_abs0", c, m)
        plan(IN0, "act", o + 6, "soft", 0)
        for c in range(NC):
            for m in range(H0):
                plan(IN0, "dve", o + 7 + 2 * c + m, "step0", c, m)
                plan(IN0, "pool", o + 8 + 2 * c + m, "dtx0", c, m)
        plan(IN0, "sp", o + 2, "rows", 0)
        plan(IN0, "sp", o + 2, "fill_c")
        plan(IN0, "sp", S0 + HALF + 4, "fill_b", 0, 0)

        for c in range(NC):
            s = S0 + 12 * c
            plan(MOE1, "pe", s + 1, "bias1", c)
            for e in range(NE):
                r = s + 1 + (5 * e) // 4
                plan(MOE1, "pool", r, "hw1", c, e)
                plan(MOE1, "pe", r + 1, "second1", c, e)
                plan(MOE1, "sp", r - 4 if c or e > 2 else s - 8, "comb_rep", NC * EXP0 + c * NE + e)
            plan(MOE1, "dve", s + 12, "scale", 1, c)
            plan(MOE1, "pool", s + 13, "moe_sum", 1, c)
            plan(MOE1, "sp", s + 13, "store", c)

        for i in range(NC * H0):
            plan(SCAN0, "dve", HALF * (i + 1) + 3, "y_sum0", i)
            plan(SCAN0, "pool", HALF * (i + 1) + 4, "y_gated", i)
        for c in range(NC):
            plan(SCAN0, "pe", H0 * HALF * (c + 1) + 6, "out0", c)
            plan(SCAN0, "dve", H0 * HALF * (c + 1) + 7, "residual0", c)
            o = S0 + HALF * (c + 1)
            plan(SCAN1, "dve", o + 2, "y_sum1", c)
            plan(SCAN1, "pe", o + 3, "out1", c)
            plan(SCAN1, "dve", o + 5, "gate1", c)
            plan(SCAN1, "pe", o + 6, "out1_T", c)
            plan(SCAN1, "dve", o + 8, "residual1", c)

        AHEAD = {"dve": 0, "act": DR - 1, "pool": -1, "pe": -2, "sp": 2 * SHI}
        beside = {}
        for step, stage, engine, piece, args in sorted(PLAN, key=lambda p: p[0]):
            n = step + AHEAD[engine]
            n = min(max(n, -1), S0 - 1 if stage == IN1 else STEPS - 1)
            beside.setdefault((engine, n), []).append((stage, piece, args))

        def pieces(engine, n):
            return beside.get((engine, n), [])

        SIGNALS = {
            ("dve", "stats"): lambda pos: [(s_stats, 2)],
            ("dve", "route_max"): lambda f: [(s_route, 3)],
            ("dve", "route_first"): lambda f: [(s_route, 3 + 5)],
            ("dve", "route_second"): lambda f: [(s_route, N_ROUTE[f] - 11)],
            ("dve", "hw0"): lambda c, e: [(s_hw, 1)],
            ("dve", "shared"): lambda c: [(s_sh, 1)],
            ("dve", "scale"): lambda f, c: [(s_ffn, 1)],
            ("dve", "step0"): lambda c, m: [(s_dt, 1)],
            ("dve", "step1"): lambda c: [(s_dt, 1)],
            ("dve", "y_sum0"): lambda i: [(s_y1, 1)],
            ("dve", "y_sum1"): lambda c: [(s_cy, 1), (s_y1, 1)],
            ("dve", "residual0"): lambda c: [(s_xr0, 1)],
            ("dve", "gate1"): lambda c: [(s_o1, 1)],
            ("dve", "residual1"): lambda c: [(s_xr2, 1)],
            ("dve", SCAN0): lambda: [(s_u, S0), (s_scan, S0), (s_carry, S0 // SHI // NC)],
            ("dve", SCAN1): lambda: [(s_u, S1), (s_scan, S1), (s_carry, S1 // SHI // NC)],
            ("pool", "rstd"): lambda pos: [(s_rstd, 4)],
            ("pool", "w_gate"): lambda: [(s_wg, 1)],
            ("pool", "dtx0"): lambda c, m: [(s_dtx, 1)],
            ("pool", "dtx1"): lambda c: [(s_dtx, 1)],
            ("pool", "y_gated"): lambda i: [(s_y2, 1)],
            ("pool", "hw1"): lambda c, e: [(s_hw1, 1)],
            ("pool", "hws"): lambda c: [(s_hws, 1)],
            ("pool", "moe_sum"): lambda f, c: [(s_xo if f else s_xr1, 1)],
            ("pool", SCAN0): lambda: [(s_hc, S0)],
            ("pool", SCAN1): lambda: [],
            ("act", "norm"): lambda pos, c: [(s_xn, 1)],
            ("act", "hT"): lambda pos, c: [(s_hT, 1)],
            ("act", "silu0"): lambda what, c, m: [(s_in_act, 1)],
            ("act", "silu1"): lambda what, c: [(s_in_act, 1)],
            ("act", "xdbl0"): lambda c: [(s_xdbl_act, 1)],
            ("act", "xdbl1"): lambda c: [(s_xdbl_act, 1)],
            ("act", "cmat"): lambda c: [(s_cmat, 1)],
            ("act", "relu_abs0"): lambda c, m: [(s_pre, 2)],
            ("act", "relu_abs1"): lambda c: [(s_pre, 2)],
            ("act", "soft"): lambda lay: [(s_soft, 2)],
            ("act", "ex"): lambda f: [(s_ex, 1)] + ([(s_sg, 1)] if f == 0 else []),
            ("act", "combT"): lambda f, c: [(s_combT_act, 1)],
            ("act", "silu_h"): lambda c, e: [(s_h1a, 1)],
            ("act", SCAN0): lambda: [(s_da, S0)],
            ("act", SCAN1): lambda: [(s_da, S1)],
            ("pe", "xnT"): lambda pos, c: [(s_xnT, 1)],
            ("pe", "in0"): lambda what, c, m: [(s_in, 1)],
            ("pe", "in1"): lambda what, c: [(s_in, 1)],
            ("pe", "xdbl0"): lambda c: [(s_xdbl, 1)],
            ("pe", "xdbl1"): lambda c: [(s_xdbl, 1)],
            ("pe", "cmat"): lambda c: [(s_cpe, 1)],
            ("pe", "dtpre0"): lambda c, m: [(s_dtpre, 1)],
            ("pe", "dtpre1"): lambda c: [(s_dtpre, 1)],
            ("pe", "lg"): lambda f: [(s_lg, 1)],
            ("pe", "combT"): lambda f, c: [(s_combT, 1)],
            ("pe", "h1"): lambda c, e: [(s_h1, 1)],
            ("pe", "second0"): lambda c, e: [(s_hwu, 1)],
            ("pe", "second1"): lambda c, e: [(s_hwu, 1)],
            ("pe", "bias1"): lambda c: [],
            ("pe", "out0"): lambda c: [(s_out0, 1)],
            ("pe", "out1"): lambda c: [(s_out1, 1)],
            ("pe", "out1_T"): lambda c: [(s_o1T, 1)],
            ("pe", SCAN0): lambda: [(s_dtxrep, S0 // SHI), (s_hsum, S0)],
            ("pe", SCAN1): lambda: [(s_dtxrep, S1 // SHI), (s_hsum, S1)],
            ("sp", "load_x"): lambda: [(s_x, 16)],
            ("sp", "keep_x"): lambda c: [(s_keep[c], 16)],
            ("sp", "rows"): lambda lay: [(s_rows[lay], 16)],
            ("sp", "fill_b"): lambda lay, c: [(s_brep[lay][c], 16 * SLO)],
            ("sp", "fill_c"): lambda: [(s_crep, 16 * SLO)],
            ("sp", "comb_store"): lambda f, c: [(s_comb_row[f][c], 16)],
            ("sp", "comb_rep"): lambda n: [(s_crow[n % 3], 16)],
            ("sp", "gate_load"): lambda g: [(s_gate[g], 16)],
            ("sp", "store"): lambda c: [(s_store[c], 16)],
            ("sp", SCAN0): lambda: [(s_dtrep[i], S0 // SHI // 2 * SLO * 16) for i in range(2)],
            ("sp", SCAN1): lambda: [(s_dtrep[i], S1 // SHI // 2 * SLO * 16) for i in range(2)],
        }
        given = [SIGNALS[engine, piece](*args) for _, _, engine, piece, args in PLAN]
        given += [SIGNALS[engine, stage]() for engine in AHEAD for stage in (SCAN0, SCAN1)]
        for s, n in sum(given, []):
            per[s.name] += n

        def stand_in(eng, t, so_far, engine, piece, args):
            for s, n in SIGNALS[engine, piece](*args):
                eng.wait_ge(s, at(s, t, so_far.get(s.name, 0)))
                eng.sem_inc(s, n)

        def add_up(so_far, engine, piece, args):
            for s, n in SIGNALS[engine, piece](*args):
                so_far[s.name] = so_far.get(s.name, 0) + n

        def seq_slice(b):
            return slice(b, b + 1) if isinstance(b, int) else bass.ds(b, 1)

        PASSES = [(t, {st for st in LAG if 0 <= t - LAG[st] < NB}) for t in range(NB + max(LAG.values()))]
        HEAD = [p for p in PASSES if p[0] < max(LAG.values())]
        TAIL = [p for p in PASSES if p[0] >= NB]
        FULL = set(LAG)

        def passes(eng, one_pass):
            for t, have in HEAD:
                one_pass(t, have)
            with eng.Fori(max(LAG.values()), NB) as t:
                one_pass(t, FULL)
            for t, have in TAIL:
                one_pass(t, have)

        def bank_use(piece, args):
            if piece == "xnT":
                return ("norm",) + args, s_hT, NC * args[0] + args[1] + 1
            if piece in ("in1", "in0"):
                idx = (IN_1 if piece == "in1" else IN_0)[args]
                return ("in", idx), s_in_act, idx + 1
            if piece in ("xdbl1", "xdbl0"):
                idx = args[0] + (0 if piece == "xdbl1" else NC)
                return ("xdbl", idx), s_xdbl_act, idx + 1
            if piece == "cmat":
                return ("cmat", args[0]), s_cmat, args[0] + 1
            if piece in ("dtpre1", "dtpre0"):
                idx = args[0] if piece == "dtpre1" else NC + args[0] * H0 + args[1]
                return ("dtpre", idx), s_pre, 2 * (idx + 1)
            if piece == "lg":
                return ("lg",) + args, s_route, N_ROUTE[0] + 1 if args[0] else 3
            if piece == "combT":
                return ("combT",) + args, s_combT_act, NC * args[0] + args[1] + 1
            if piece == "h1":
                c, e = args
                freed = (s_hw, NE * c + e + 1) if e < NE else (s_h1a, EXP0 * (c + 1)) if e == NE else (s_sh, c + 1)
                return (("h1", c, e),) + freed
            if piece == "second0" and args[1] == 0:
                return ("acc", 0, args[0]), s_ffn, args[0] + 1
            if piece == "bias1":
                return ("acc", 1, args[0]), s_ffn, NC + args[0] + 1
            if piece == "out0":
                return ("out0", args[0]), s_xr0, args[0] + 1
            if piece == "out1":
                return ("out1", args[0]), s_o1, args[0] + 1
            if piece == "out1_T":
                return ("o1T", args[0]), s_xr2, args[0] + 1
            return None

        uses = []
        last = {}
        for n in range(-1, STEPS):
            for _, piece, args in pieces("pe", n):
                if bank_use(piece, args):
                    uses.append(bank_use(piece, args))
                elif piece == "second0" and args[1] == NE:
                    last["acc", 0, args[0]] = len(uses)
                elif piece == "second1" and args[1] == NE - 1:
                    last["acc", 1, args[0]] = len(uses)

        bank = {}
        holder = [None] * MB
        order = [-1] * MB
        before = {}
        for n, (name, _, _) in enumerate(uses):
            free = [i for i in range(MB) if holder[i] is None or n >= last.get(uses[holder[i]][0], -1)]
            i = min(free, key=lambda k: order[k])
            bank[name], before[name] = i, holder[i]
            holder[i], order[i] = n, last.get(name, n)

        def claim(pe, t, name):
            if before[name] is not None:
                _, s, n = uses[before[name]]
                pe.wait_ge(s, at(s, t, n))
            else:
                _, s, n = uses[holder[bank[name]]]
                if not isinstance(t, int) or t:
                    pe.wait_ge(s, at(s, t - 1, n))
            return mm[:, bank[name], :]

        def bank_of(name):
            return mm[:, bank[name], :]
        block = ctx.enter_context(nc.Block())

        loads = [
            (w_in0[:], w["w_in0"]), (conv0_bc, w["conv0"].partition_broadcast(P)), (conv_b0[:], w["conv_b0"]),
            (w_x0[:], w["w_x0"]), (w_dt0[:], w["w_dt0"]), (b_dt0[:], w["b_dt0"]), (a_log0[:], w["a_log0"]),
            (d0[:], w["d0"]), (w_out0[:], w["w_out0"]), (router[:], w["router"]), (w1[:], w["w1"]),
            (w2[:], w["w2"]), (w_in1[:], w["w_in1"]), (conv1_bc, w["conv1"].partition_broadcast(P)),
            (w_x1dt[:], w["w_x1dt"]), (w_x1b[:], w["w_x1b"]), (w_x1c[:], w["w_x1c"]), (w_dt1[:], w["w_dt1"]),
            (w_c1[:], w["w_c1"]), (b_dt1[:], w["b_dt1"]), (a_log1[:], w["a_log1"]), (d1[:], w["d1"]),
            (w_out1[:], w["w_out1"]), (gate_w1[:], w["gate_w1"]), (gate_b1[:], w["gate_b1"].partition_broadcast(P)),
            (w_e1[:], w["w_e1"]), (b_e1[:], w["b_e1"]), (c_t[:], w["c_t"]), (w_mod, w["w_mod"]),
        ]
        N_LOAD = 16 * len(loads)

        @block.sync
        def _(sp_):
            for dst, src in loads:
                sp_.dma_start(dst, src).then_inc(s_load, 16)

            sp_.wait_ge(s_setup, N_SETUP)
            sp_.dma_start(gates_dram.rearrange("g b d -> (g b d)").unsqueeze(0),
                          gates[0:1, :, :, :].rearrange("o g b d -> o (g b d)")).then_inc(s_gstore, 16)
            sp_.wait_ge(s_gstore, 16)

            def value(v):
                return v if isinstance(v, int) else sp_.compute_val(v)

            def wait_all(*pairs):
                pairs = [(s, value(v)) for s, v in pairs]
                for s, v in pairs:
                    sp_.wait_ge(s, v)

            def rep_dt(t, j):
                lay1 = j >= KS0
                jj = j - KS0 if lay1 else j
                kn = KPH if lay1 else H0 * KPH
                c, k = jj // kn, jj % kn
                m, kk = k // KPH, k % KPH
                src = dt1 if lay1 else dt[:, m, :]
                wait_all((s_dt, at(s_dt, t, c + 1) if lay1 else at(s_dt, t - 1, NC + c * H0 + m + 1)),
                         (s_da, at(s_da, t, SHI * max(j - 1, 0))))
                for a in range(SLO):
                    sp_.dma_start(dt_rep[R * a:R * a + R, j % 2, :],
                                  src[R * kk:R * kk + R, CH * c:CH * c + CH]).then_inc(s_dtrep[j % 2], 16)

            def rep_rows(dst, rows, row0, s_done, cols):
                for a in range(SLO):
                    sp_.dma_start(dst[R * a:R * a + R],
                                  rows[row0 + SHI * a:row0 + SHI * a + SHI, cols].partition_broadcast(R)
                                  ).then_inc(s_done, 16)

            def gate_load(t, g):
                s, n = ((s_wg, 0), (s_ffn, 0), (s_ffn, 0))[g]
                wait_all((s, at(s, t, n)))
                stage = (SCAN0, MOE0, MOE1)[g]
                dst = gate_b[:, g - 1:g, :] if g else gate_a[:]
                sp_.dma_start(dst, gates_dram[g, seq_slice(t - LAG[stage]), :].partition_broadcast(P)
                              ).then_inc(s_gate[g], 16)

            def fill_b(t, lay, c):
                cols = slice(CH * c, CH * c + CH)
                if lay:
                    wait_all((s_rows[1], at(s_rows[1], t, 16)), (s_u, at(s_u, t, S0 // NC * (c + 1))))
                    rep_rows(b_rep[:, c, :, :], rows1_dram, 0, s_brep[1][c], cols)
                elif c == 0:
                    wait_all((s_rows[0], at(s_rows[0], t, 16)), (s_u, at(s_u, t, S0 + S1 // NC)))
                    rep_rows(b_rep[:, c, :, :], rows0_dram, 1, s_brep[0][c], cols)
                else:
                    wait_all((s_rows[0], at(s_rows[0], t, 0)), (s_u, at(s_u, t, 0)))
                    rep_rows(b_rep[:, c, :, :], rows0_dram, 1, s_brep[0][c], cols)

            def fill_c(t):
                wait_all((s_rows[0], at(s_rows[0], t, 16)), (s_hc, at(s_hc, t, S0)))
                rep_rows(c_rep, rows0_dram, 1 + NS, s_crep, slice(0, T))

            def rows(t, lay):
                if lay:
                    wait_all((s_xdbl_act, at(s_xdbl_act, t, NC)), (s_brep[1][0], at(s_brep[1][0], t, 0)),
                             (s_brep[1][1], at(s_brep[1][1], t, 0)))
                    sp_.dma_start(rows1_dram, xdbl[0:NS, :]).then_inc(s_rows[1], 16)
                else:
                    wait_all((s_xdbl_act, at(s_xdbl_act, t, 2 * NC)), (s_brep[0][0], at(s_brep[0][0], t, 0)),
                             (s_brep[0][1], at(s_brep[0][1], t, 16 * SLO)), (s_crep, at(s_crep, t, 0)))
                    sp_.dma_start(rows0_dram, xdbl[:]).then_inc(s_rows[0], 16)

            def comb_store(t, f, c):
                cols = slice(CH * c, CH * c + CH)
                k = NC * f + c + 1
                wait_all((s_combT_act, at(s_combT_act, t, k)), (s_hw1, at(s_hw1, t, 0)))
                dst, src = (comb1_dram, combT[0:NE, cols]) if f else (comb0_dram, combT[:, cols])
                sp_.dma_start(dst[:, cols], src).then_inc(s_comb_row[f][c], 16)

            def comb_rep_row(t, n):
                old = n - 3
                if old < 0:
                    used, v = s_hw1, 0
                elif old >= NC * EXP0:
                    used, v = s_hw1, old - NC * EXP0 + 1
                elif old % EXP0 == NE:
                    used, v = s_hws, old // EXP0 + 1
                else:
                    used, v = s_hw, old // EXP0 * NE + old % EXP0 + 1
                f = n >= NC * EXP0
                c, e = divmod(n - NC * EXP0, NE) if f else divmod(n, EXP0)
                src = (comb1_dram if f else comb0_dram)[e:e + 1, CH * c:CH * c + CH]
                wait_all((used, at(used, t, v)), (s_comb_row[f][c], at(s_comb_row[f][c], t, 16)))
                sp_.dma_start(comb_rep[:, n % 3:n % 3 + 1, :], src.partition_broadcast(P)).then_inc(s_crow[n % 3], 16)

            def tiles(dram, b, c):
                v = dram[seq_slice(b), :, :].rearrange("o (i p) d -> (o p) i d", p=P)
                return v if c is None else v[:, TPC * c:TPC * c + TPC, :]

            def keep_x(t, c):
                wait_all((s_xr1, at(s_xr1, t, c + 1)), (s_x, at(s_x, t, 0)))
                v = slice(TPC * c, TPC * c + TPC)
                sp_.dma_start(xr0[:, v, :], xa[:, v, :]).then_inc(s_keep[c], 16)

            def load_x(t):
                wait_all((s_keep[0], at(s_keep[0], t, 16)), (s_keep[1], at(s_keep[1], t, 16)), (s_xn, at(s_xn, t, 0)))
                sp_.dma_start(xa[:], tiles(x_in, t, None)).then_inc(s_x, 16)

            def store(t, c):
                wait_all((s_xo, at(s_xo, t, c + 1)))
                sp_.dma_start(tiles(out, t - LAG[MOE1], c), xr2[:, TPC * c:TPC * c + TPC, :]).then_inc(s_store[c], 16)

            do = {"gate_load": gate_load, "fill_b": fill_b, "fill_c": fill_c, "rows": rows, "comb_store": comb_store,
                  "comb_rep": comb_rep_row, "keep_x": keep_x, "load_x": load_x, "store": store}

            def one_pass(t, have):
                so_far = {}

                for n in range(-1, STEPS):
                    stage = SCAN0 if n < S0 else SCAN1
                    if n in (0, S0):
                        if stage not in have:
                            stand_in(sp_, t, so_far, "sp", stage, ())
                        add_up(so_far, "sp", stage, ())
                    if n >= 0 and n % SHI == 0 and stage in have:
                        rep_dt(t, n // SHI)
                    for of, piece, args in pieces("sp", n):
                        if of in have:
                            do[piece](t, *args)
                        else:
                            stand_in(sp_, t, so_far, "sp", piece, args)
                        add_up(so_far, "sp", piece, args)

            passes(sp_, one_pass)
            for c in range(NC):
                sp_.wait_ge(s_store[c], at(s_store[c], len(PASSES), 0))
        @block.gpsimd
        def _(pool):
            for s in counted:
                pool.sem_inc(s, 1)
            pool.memset(ident[:], 0.0).then_inc(s_const, 1)
            pool.memset(rep[:], 0.0).then_inc(s_const, 1)
            pool.memset(state_sum[:], 0.0).then_inc(s_const, 1)
            pool.memset(eps8[:], EPS).then_inc(s_const, 1)
            pool.memset(neg_half[:], -0.5).then_inc(s_const, 1)
            pool.memset(neg_one[:], -1.0).then_inc(s_const, 1)
            pool.memset(hTa[:], 0.0).then_inc(s_const, 1)
            pool.memset(hTb[:], 0.0).then_inc(s_const, 1)
            for e in range(NE):
                pool.memset(rev[:, e:e + 1], float(NE - e)).then_inc(s_const, 1)
            n = 8 + NE
            pool.wait_ge(s_const, n)
            pool.affine_select(out=ident[:], in_=ident[:], compare_op=ALU.not_equal, fill=1.0, base=0,
                               pattern=[[-1, P]], channel_multiplier=1).then_inc(s_const, 1)
            n += 1
            for k in range(KPH):
                v = rep[:, k, :].rearrange("p (a r) -> p a r", a=SLO)
                pool.affine_select(out=v, in_=v, compare_op=ALU.not_equal, fill=1.0, base=-R * k,
                                   pattern=[[0, SLO], [-1, R]], channel_multiplier=1).then_inc(s_const, 1)
            n += KPH
            for a in range(SLO):
                pool.wait_ge(s_const, n)
                pool.affine_select(out=state_sum[:], in_=state_sum[:], compare_op=ALU.not_equal, fill=1.0,
                                   base=-R * a, pattern=[[-1, R]], channel_multiplier=1).then_inc(s_const, 1)
                n += 1
            pool.wait_ge(s_load, N_LOAD)
            for k in range(TAPS0):
                pool.tensor_tensor(w_conv0[:, k, :], w_in0[:, 0:DI], conv0_bc[:, k, :], ALU.mult).then_inc(s_const, 1)
            for k in range(TAPS1):
                pool.tensor_tensor(w_conv1[:, k, :], w_in1[:, 0:D], conv1_bc[:, k, :], ALU.mult).then_inc(s_const, 1)

            def w_gate(t):
                pool.wait_ge(s_gate[0], at(s_gate[0], t, 16))
                pool.wait_ge(s_out0, at(s_out0, t, 0))
                for m in range(H0):
                    ins = pool.tensor_tensor(w_out0g[:, m:m + 1, :], w_out0[:, m:m + 1, :], gate_a[:], ALU.mult)
                ins.then_inc(s_wg, 1)

            def rstd_(t, pos):
                pool.wait_ge(s_stats, at(s_stats, t, 2 * pos + 2))
                pool.wait_ge(s_xn, at(s_xn, t, NC * pos))
                pool.tensor_tensor(var_eps[:], mean_var[:, :, 1], eps8[:], ALU.add).then_inc(s_rstd, 1)
                pool.wait_ge(s_rstd, at(s_rstd, t, 4 * pos + 1))
                pool.tensor_tensor(rstd[:], var_eps[:], neg_half[:], ALU.pow).then_inc(s_rstd, 1)
                pool.wait_ge(s_rstd, at(s_rstd, t, 4 * pos + 2))
                pool.tensor_tensor(shift[:], mean_var[:, :, 0], rstd[:], ALU.mult).then_inc(s_rstd, 1)
                pool.wait_ge(s_rstd, at(s_rstd, t, 4 * pos + 3))
                pool.tensor_tensor(shift[:], shift[:], neg_one[:], ALU.mult).then_inc(s_rstd, 1)

            def dtx_0(t, c, m):
                i = NC + c * H0 + m
                v = slice(CH * c, CH * c + CH)
                pool.wait_ge(s_dt, at(s_dt, t, i + 1))
                pool.wait_ge(s_in_act, at(s_in_act, t, IN_0["xs", c, m] + 1))
                pool.tensor_tensor(dtx[:, m, v], dt[:, m, v], xs[:, m, v], ALU.mult).then_inc(s_dtx, 1)

            def dtx_1(t, c):
                v = slice(CH * c, CH * c + CH)
                pool.wait_ge(s_dt, at(s_dt, t, c + 1))
                pool.wait_ge(s_in_act, at(s_in_act, t, IN_1["xs", c] + 1))
                pool.tensor_tensor(dtx1[:, v], dt1[:, v], xs1[:, v], ALU.mult).then_inc(s_dtx, 1)

            def y_gated(t, i):
                c, m = i // H0, i % H0
                pool.wait_ge(s_y1, at(s_y1, t, i + 1))
                pool.wait_ge(s_out0, at(s_out0, t, c))
                pool.wait_ge(s_o1T, at(s_o1T, t, 0))
                pool.tensor_tensor(y2[:, m, :], y1[:], zs[:, m, CH * c:CH * c + CH], ALU.mult).then_inc(s_y2, 1)

            def hws(t, c):
                n = c * EXP0 + NE
                pool.wait_ge(s_crow[n % 3], at(s_crow[n % 3], t, 16 * (n // 3 + 1)))
                pool.wait_ge(s_sh, at(s_sh, t, c + 1))
                pool.wait_ge(s_hwu, at(s_hwu, t, n - 1))
                pool.tensor_tensor(hw[:, NE % 2, :], shared[:], comb_rep[:, n % 3, :], ALU.mult).then_inc(s_hws, 1)

            def hw1(t, c, e):
                n = NC * EXP0 + NE * c + e
                pool.wait_ge(s_crow[n % 3], at(s_crow[n % 3], t, 16 * (n // 3 + 1)))
                pool.wait_ge(s_hwu, at(s_hwu, t, n - (e > 0)))
                pool.tensor_tensor(hw[:, e % 2, :], comb_rep[:, n % 3, :], hTb[:, 3 + CH * c:3 + CH * c + CH],
                                   ALU.mult).then_inc(s_hw1, 1)

            def moe_sum(t, f, c):
                pool.wait_ge(s_ffn, at(s_ffn, t, NC * f + c + 1))
                v = slice(TPC * c, TPC * c + TPC)
                if f == 0:
                    pool.wait_ge(s_xr2, at(s_xr2, t, 0))
                    pool.tensor_tensor(xr1[:, v, :], xr0[:, v, :], ffn[:], ALU.add).then_inc(s_xr1, 1)
                else:
                    pool.tensor_tensor(xr2[:, v, :], xr2[:, v, :], ffn[:], ALU.add).then_inc(s_xo, 1)

            do = {"w_gate": w_gate, "rstd": rstd_, "dtx0": dtx_0, "dtx1": dtx_1, "y_gated": y_gated, "hws": hws, "hw1": hw1,
                  "moe_sum": moe_sum}

            def one_pass(t, have):
                so_far = {}
                if SCAN0 not in have:
                    stand_in(pool, t, so_far, "pool", SCAN0, ())
                else:
                    pool.wait_ge(s_crep, at(s_crep, t, 0))
                for n in range(-1, STEPS):
                    if 0 <= n < S0 and SCAN0 in have:
                        c, i = n // (H0 * KPH * SHI), n % SHI
                        pool.wait_ge(s_scan, at(s_scan, t, n + 1))
                        pool.wait_ge(s_hsum, at(s_hsum, t, n - CR + 1) if n >= CR else at(s_hsum, t, 0))
                        pool.tensor_tensor(hc[:, n % CR, :], h[:, n % HR, :], c_rep[:, i, CH * c:CH * c + CH],
                                           ALU.mult).then_inc(s_hc, 1)
                    for of, piece, args in pieces("pool", n):
                        if of in have:
                            do[piece](t, *args)
                        else:
                            stand_in(pool, t, so_far, "pool", piece, args)
                        add_up(so_far, "pool", piece, args)

            pool.wait_ge(s_setup, N_SETUP)
            passes(pool, one_pass)
        @block.scalar
        def _(act):
            act.wait_ge(s_load, N_LOAD)
            act.activation(silu_c[:], c_t[:], ACT.Silu).then_inc(s_setup_act, 1)
            act.activation(neg_a0[:], a_log0[:], ACT.Exp).then_inc(s_setup_act, 1)
            act.activation(neg_a1[:], a_log1[:], ACT.Exp).then_inc(s_setup_act, 1)
            act.wait_ge(s_setup, N_SETUP)
            act.wait_ge(s_const, N_CONST)

            def norm(t, pos, c):
                src = {N_MOE0: xr0, N_MOE1: xr2, N_IN1: xr1, N_IN0: xa}[pos]
                act.wait_ge(s_rstd, at(s_rstd, t, 4 * pos + 4))
                act.wait_ge(s_xnT, at(s_xnT, t, NC * pos))
                for i in range(TPC * c, TPC * c + TPC):
                    ins = act.activation(xn[:, i, :], src[:, i, :], ACT.Identity, bias=shift[:, i:i + 1],
                                         scale=rstd[:, i:i + 1])
                ins.then_inc(s_xn, 1)

            def hT_(t, pos, c):
                lay, j, stage = NORM_MODS[pos]
                seq = seq_slice(t - LAG[stage])
                used, n = {N_MOE0: (s_in, 0), N_MOE1: (s_hw1, 0), N_IN1: (s_h1, NC * (NE + 2)), N_IN0: (s_in, len(IN_1))}[pos]
                there, free = at(s_xnT, t, NC * pos + c + 1), at(used, t, n)
                if not isinstance(t, int):
                    there, free = act.compute_val(there), act.compute_val(free)
                act.wait_ge(s_setup, N_SETUP)
                act.wait_ge(s_xnT, there)
                act.wait_ge(used, free)
                dst = hTb if pos == N_MOE1 else hTa
                act.activation(dst[:, 3 + CH * c:3 + CH * c + CH], bank_of(("norm", pos, c)), ACT.Identity,
                               bias=mods[:, lay, j, seq], scale=mods[:, lay, j + 1, seq]).then_inc(s_hT, 1)

            def silu0(t, what, c, m):
                idx = IN_0[what, c, m]
                i = c * H0 + m
                act.wait_ge(s_in, at(s_in, t, idx + 1))
                if what == "xs":
                    act.wait_ge(s_y1, at(s_y1, t, i + 1))
                else:
                    act.wait_ge(s_y2, at(s_y2, t, i + 1))
                dst = (xs if what == "xs" else zs)[:, m, CH * c:CH * c + CH]
                act.activation(dst, bank_of(("in", idx)), ACT.Silu, bias=conv_b0[:, m:m + 1] if what == "xs" else 0.0
                               ).then_inc(s_in_act, 1)

            def silu1(t, what, c):
                idx = IN_1[what, c]
                act.wait_ge(s_in, at(s_in, t, idx + 1))
                if what == "xs":
                    act.wait_ge(s_y1, at(s_y1, t, 0))
                else:
                    act.wait_ge(s_o1, at(s_o1, t, 0))
                dst = (xs1 if what == "xs" else zs1)[:, CH * c:CH * c + CH]
                act.activation(dst, bank_of(("in", idx)), ACT.Silu).then_inc(s_in_act, 1)

            def xdbl_0(t, c):
                act.wait_ge(s_xdbl, at(s_xdbl, t, NC + c + 1))
                act.wait_ge(s_rows[1], at(s_rows[1], t, 16))
                act.copy(xdbl[:, CH * c:CH * c + CH], bank_of(("xdbl", NC + c))[0:1 + 2 * NS, :]).then_inc(s_xdbl_act, 1)

            def xdbl_1(t, c):
                act.wait_ge(s_xdbl, at(s_xdbl, t, c + 1))
                act.wait_ge(s_rows[0], at(s_rows[0], t, 0))
                act.wait_ge(s_dtpre, at(s_dtpre, t, 0))
                act.copy(xdbl[0:NS, CH * c:CH * c + CH], bank_of(("xdbl", c))[0:NS, :]).then_inc(s_xdbl_act, 1)

            def cmat(t, c):
                act.wait_ge(s_cpe, at(s_cpe, t, c + 1))
                act.wait_ge(s_cy, at(s_cy, t, 0))
                act.copy(c_mat[:, CH * c:CH * c + CH], bank_of(("cmat", c))).then_inc(s_cmat, 1)

            def relu_abs(t, i, relu_to, abs_to, bias):
                act.wait_ge(s_dtpre, at(s_dtpre, t, i + 1))
                v = bank_of(("dtpre", i))
                act.activation(relu_to, v, ACT.Relu, bias=bias).then_inc(s_pre, 1)
                act.activation(abs_to, v, ACT.Abs, bias=bias).then_inc(s_pre, 1)

            def relu_abs0(t, c, m):
                act.wait_ge(s_dtxrep, at(s_dtxrep, t, KS0))
                for s in s_dtrep:
                    act.wait_ge(s, at(s, t, KS0 // 2 * SLO * 16))
                v = slice(CH * c, CH * c + CH)
                relu_abs(t, NC + c * H0 + m, dtx[:, m, v], dt[:, m, v], b_dt0[:, m:m + 1])

            def relu_abs1(t, c):
                act.wait_ge(s_dtxrep, at(s_dtxrep, t, 0))
                for s in s_dtrep:
                    act.wait_ge(s, at(s, t, 0))
                v = slice(CH * c, CH * c + CH)
                relu_abs(t, c, dtx1[:, v], dt1[:, v], b_dt1[:, 0:1])

            def soft(t, lay):
                v = dt1[:] if lay else dt[:]
                base = 0 if lay else 2
                act.wait_ge(s_pre, at(s_pre, t, 2 * NC if lay else 2 * (NC + NC * H0)))
                act.activation(v, v, ACT.Exp, scale=-1.0).then_inc(s_soft, 1)
                act.wait_ge(s_soft, at(s_soft, t, base + 1))
                act.activation(v, v, ACT.Ln, bias=1.0).then_inc(s_soft, 1)

            def ex_(t, f):
                act.wait_ge(s_route, at(s_route, t, N_ROUTE[0] * f + (3 if f else 2)))
                act.activation(ex[:], lg[:], ACT.Exp).then_inc(s_ex, 1)
                if f == 0:
                    act.wait_ge(s_route, at(s_route, t, 3))
                    act.activation(sg[:], sg[:], ACT.Exp, scale=-1.0).then_inc(s_sg, 1)

            def combT_(t, f, c):
                act.wait_ge(s_combT, at(s_combT, t, NC * f + c + 1))
                if f == 0:
                    act.wait_ge(s_hwu, at(s_hwu, t, 0))
                else:
                    for s in s_comb_row[0]:
                        act.wait_ge(s, at(s, t, 16))
                k = NE if f else NE + 1
                act.copy(combT[0:k, CH * c:CH * c + CH], bank_of(("combT", f, c))[0:k, :]).then_inc(s_combT_act, 1)

            def silu_h(t, c, e):
                act.wait_ge(s_h1, at(s_h1, t, c * (NE + 2) + e + 1))
                v = bank_of(("h1", c, e))
                if e == NE:
                    act.wait_ge(s_sh, at(s_sh, t, c))
                act.activation(v if e < NE else gate_act[:], v, ACT.Silu).then_inc(s_h1a, 1)

            do = {"norm": norm, "hT": hT_, "silu0": silu0, "silu1": silu1, "xdbl0": xdbl_0, "xdbl1": xdbl_1,
                  "cmat": cmat, "relu_abs0": relu_abs0, "relu_abs1": relu_abs1, "soft": soft, "ex": ex_,
                  "combT": combT_, "silu_h": silu_h}

            def one_pass(t, have):
                so_far = {}
                for n in range(-1, STEPS):
                    stage, neg_a = (SCAN0, neg_a0) if n < S0 else (SCAN1, neg_a1)
                    if n in (0, S0):
                        if stage not in have:
                            stand_in(act, t, so_far, "act", stage, ())
                        add_up(so_far, "act", stage, ())
                    if n >= 0 and stage in have:
                        kn = KPH if n >= S0 else H0 * KPH
                        j, i = n // SHI, n % SHI
                        k = (j - (KS0 if n >= S0 else 0)) % kn
                        if i == 0:
                            act.wait_ge(s_dtrep[j % 2], at(s_dtrep[j % 2], t, (j // 2 + 1) * SLO * 16))
                        act.wait_ge(s_scan, at(s_scan, t, max(n - DR + 1, 0)))
                        act.activation(da[:, n % DR, :], dt_rep[:, j % 2, :], ACT.Exp, scale=neg_a[:, k, i:i + 1]
                                       ).then_inc(s_da, 1)
                    for of, piece, args in pieces("act", n):
                        if of in have:
                            do[piece](t, *args)
                        else:
                            stand_in(act, t, so_far, "act", piece, args)
                        add_up(so_far, "act", piece, args)

            passes(act, one_pass)
        @block.vector
        def _(dve):
            dve.wait_ge(s_setup_act, 3)
            dve.wait_ge(s_const, N_CONST)
            dve.tensor_scalar(neg_a0[:], neg_a0[:], -1.0, None, ALU.mult).then_inc(s_setup, 1)
            dve.tensor_scalar(neg_a1[:], neg_a1[:], -1.0, None, ALU.mult).then_inc(s_setup, 1)
            n = 2
            dve.wait_ge(s_setup_pe, 3)
            for lay in range(2):
                v = mods[:, lay, :, :].rearrange("p j b -> p (j b)")
                dve.tensor_copy(v, mm[:, lay, 0:6 * NB]).then_inc(s_setup, 1)
            dve.tensor_copy(w_dtx1[:], mm[:, 2, 0:D]).then_inc(s_setup, 1)
            dve.tensor_copy(w_cx1[:], mm[:, 2, D:2 * D]).then_inc(s_setup, 1)
            n += 4
            dve.wait_ge(s_setup, n)
            for lay in range(2):
                for j in (1, 4):
                    dve.tensor_scalar(mods[:, lay, j, :], mods[:, lay, j, :], 1.0, None, ALU.add).then_inc(s_setup, 1)
                    n += 1

            def gated(v, tmp):
                nonlocal n
                dve.wait_ge(s_setup, n)
                dve.tensor_scalar(tmp, v, 0.0, 2.0, ALU.is_ge, ALU.mult).then_inc(s_setup, 1)
                dve.wait_ge(s_setup, n + 1)
                dve.scalar_tensor_tensor(out=v, in0=tmp, scalar=-1.0, in1=v, op0=ALU.add, op1=ALU.mult).then_inc(s_setup, 1)
                dve.wait_ge(s_setup, n + 2)
                dve.tensor_scalar(v, v, GATE_MIN, None, ALU.max).then_inc(s_setup, 1)
                dve.wait_ge(s_setup, n + 3)
                dve.scalar_tensor_tensor(out=v, in0=tmp, scalar=-1.0, in1=v, op0=ALU.add, op1=ALU.mult).then_inc(s_setup, 1)
                n += 4

            gated(mods[:, 1, 2, :], gate_tmp[:, 0:NB])
            for g in range(3):
                for q in range(2):
                    dve.wait_ge(s_setup_pe, 4 + 2 * g + q)
                    dve.tensor_copy(gates[:, g, NB // 2 * q:NB // 2 * q + NB // 2, :].rearrange("p b d -> p (b d)"),
                                    mm[:, q, :]).then_inc(s_setup, 1)
                    n += 1
            for g in range(3):
                gated(gates[:, g, :, :].rearrange("p b d -> p (b d)"), gate_tmp)
            assert n == N_SETUP

            def stats_(t, pos):
                src = {N_MOE0: xr0, N_MOE1: xr2, N_IN1: xr1, N_IN0: xa}[pos]
                s_src, n_src = {N_MOE0: (s_xr0, 0), N_MOE1: (s_xr2, 0), N_IN1: (s_xr1, NC), N_IN0: (s_x, 16)}[pos]
                dve.wait_ge(s_src, at(s_src, t, n_src))
                dve.wait_ge(s_xn, at(s_xn, t, NC * pos))
                for i in range(TILES):
                    ins = dve.bn_stats(stats[:, i, :], src[:, i, :])
                ins.then_inc(s_stats, 1)
                stats_there = at(s_stats, t, 2 * pos + 1)
                if not isinstance(t, int):
                    stats_there = dve.compute_val(stats_there)
                dve.wait_ge(s_setup, N_SETUP)
                dve.wait_ge(s_stats, stats_there)
                for i in range(TILES):
                    ins = dve.bn_aggr(mean_var[:, i, :], stats[:, i, :])
                ins.then_inc(s_stats, 1)

            def step0(t, c, m):
                v = slice(CH * c, CH * c + CH)
                dve.wait_ge(s_soft, at(s_soft, t, 4))
                dve.tensor_tensor(dt[:, m, v], dt[:, m, v], dtx[:, m, v], ALU.add).then_inc(s_dt, 1)

            def step1(t, c):
                v = slice(CH * c, CH * c + CH)
                dve.wait_ge(s_soft, at(s_soft, t, 2))
                dve.scalar_tensor_tensor(out=dt1[:, v], in0=dt1[:, v], scalar=EPS, in1=dtx1[:, v], op0=ALU.add,
                                         op1=ALU.add).then_inc(s_dt, 1)

            def hw0(t, c, e):
                n = c * EXP0 + e
                dve.wait_ge(s_h1a, at(s_h1a, t, n + 1))
                dve.wait_ge(s_crow[n % 3], at(s_crow[n % 3], t, 16 * (n // 3 + 1)))
                dve.wait_ge(s_hwu, at(s_hwu, t, n - (e > 0)))
                dve.tensor_tensor(hw[:, e % 2, :], bank_of(("h1", c, e)), comb_rep[:, n % 3, :], ALU.mult
                                  ).then_inc(s_hw, 1)

            def shared_(t, c):
                dve.wait_ge(s_h1, at(s_h1, t, (NE + 2) * (c + 1)))
                dve.wait_ge(s_h1a, at(s_h1a, t, EXP0 * (c + 1)))
                dve.wait_ge(s_hws, at(s_hws, t, c))
                dve.tensor_tensor(shared[:], bank_of(("h1", c, NE + 1)), gate_act[:], ALU.mult).then_inc(s_sh, 1)

            def scale(t, f, c):
                dve.wait_ge(s_hwu, at(s_hwu, t, NC * EXP0 + NE * (c + 1) if f else EXP0 * (c + 1)))
                dve.wait_ge(s_gate[1 + f], at(s_gate[1 + f], t, 16))
                dve.wait_ge(s_xr1, at(s_xr1, t, NC if f else c))
                dve.wait_ge(s_xo, at(s_xo, t, c if f else 0))
                dve.tensor_tensor(ffn[:], bank_of(("acc", f, c)).rearrange("p (i d) -> p i d", i=TPC),
                                  gate_b[:, f:f + 1, :].to_broadcast([P, TPC, D]), ALU.mult).then_inc(s_ffn, 1)

            def y_sum0(t, i):
                c, m = i // H0, i % H0
                dve.wait_ge(s_hsum, at(s_hsum, t, HALF * (i + 1)))
                dve.wait_ge(s_y2, at(s_y2, t, i))
                dve.wait_ge(s_out1, at(s_out1, t, 0))
                dve.scalar_tensor_tensor(out=y1[:], in0=xs[:, m, CH * c:CH * c + CH], scalar=d0[:, m:m + 1],
                                         in1=ysum[:], op0=ALU.mult, op1=ALU.add).then_inc(s_y1, 1)

            def residual0(t, c):
                dve.wait_ge(s_out0, at(s_out0, t, c + 1))
                dve.wait_ge(s_keep[c], at(s_keep[c], t, 16))
                v = slice(TPC * c, TPC * c + TPC)
                dve.tensor_tensor(xr0[:, v, :], xr0[:, v, :],
                                  bank_of(("out0", c)).rearrange("p (i d) -> p i d", i=TPC), ALU.add
                                  ).then_inc(s_xr0, 1)

            def y_sum1(t, c):
                dve.wait_ge(s_hsum, at(s_hsum, t, S0 + HALF * (c + 1)))
                dve.wait_ge(s_cmat, at(s_cmat, t, c + 1))
                dve.tensor_tensor(ysum[:], ysum[:], c_mat[:, CH * c:CH * c + CH], ALU.mult).then_inc(s_cy, 1)
                dve.wait_ge(s_cy, at(s_cy, t, c + 1))
                dve.wait_ge(s_out1, at(s_out1, t, c))
                dve.wait_ge(s_y2, at(s_y2, t, NC * H0))
                dve.scalar_tensor_tensor(out=y1[:], in0=xs1[:, CH * c:CH * c + CH], scalar=d1[:, 0:1],
                                         in1=ysum[:], op0=ALU.mult, op1=ALU.add).then_inc(s_y1, 1)

            def gate1(t, c):
                dve.wait_ge(s_out1, at(s_out1, t, c + 1))
                dve.wait_ge(s_out0, at(s_out0, t, NC))
                dve.wait_ge(s_o1T, at(s_o1T, t, c))
                dve.scalar_tensor_tensor(out=y2[:, 0, :], in0=bank_of(("out1", c)),
                                         scalar=mods[:, 1, 2, seq_slice(t - LAG[SCAN1])],
                                         in1=zs1[:, CH * c:CH * c + CH], op0=ALU.mult, op1=ALU.mult
                                         ).then_inc(s_o1, 1)

            def residual1(t, c):
                dve.wait_ge(s_o1T, at(s_o1T, t, c + 1))
                dve.wait_ge(s_store[c], at(s_store[c], t, 16))
                v = slice(TPC * c, TPC * c + TPC)
                dve.tensor_tensor(xr2[:, v, :], xr1[:, v, :], bank_of(("o1T", c)).rearrange("p (i d) -> p i d", i=TPC),
                                  ALU.add).then_inc(s_xr2, 1)

            route_step = [0]

            def done(ins):
                ins.then_inc(s_route, 1)
                route_step[0] += 1

            def need(t):
                dve.wait_ge(s_route, at(s_route, t, route_step[0]))

            def bc(v):
                return v.unsqueeze(2).to_broadcast([P, TILES, NE])

            def route_max(t, f):
                route_step[0] = N_ROUTE[0] * f
                width = NE if f else NE + 1
                v = bank_of(("lg", f))[:, 0:TILES * width].rearrange("p (i e) -> p i e", i=TILES)
                dve.wait_ge(s_lg, at(s_lg, t, f + 1))
                need(t)
                if f == 0:
                    done(dve.tensor_reduce(mx[:], v[:, :, 0:NE], AX.X, ALU.max))
                    need(t)
                    done(dve.tensor_tensor(lg[:], v[:, :, 0:NE], bc(mx[:]), ALU.subtract))
                    done(dve.tensor_copy(sg[:], v[:, :, NE]))
                else:
                    done(dve.tensor_tensor(lg[:], v, gate_b1[:].unsqueeze(1).to_broadcast([P, TILES, NE]), ALU.add))
                    need(t)
                    done(dve.tensor_reduce(mx[:], lg[:], AX.X, ALU.max))
                    need(t)
                    done(dve.tensor_tensor(lg[:], lg[:], bc(mx[:]), ALU.subtract))

            def largest(t, dst):
                need(t)
                done(dve.tensor_reduce(mx[:], ex[:], AX.X, ALU.max))
                need(t)
                done(dve.tensor_tensor(key[:], ex[:], bc(mx[:]), ALU.is_equal))
                need(t)
                done(dve.tensor_tensor(key[:], key[:], rev[:].unsqueeze(1).to_broadcast([P, TILES, NE]), ALU.mult))
                need(t)
                done(dve.tensor_reduce(mx[:], key[:], AX.X, ALU.max))
                need(t)
                done(dve.tensor_tensor(dst[:], key[:], bc(mx[:]), ALU.is_equal))

            def route_first(t, f):
                route_step[0] = N_ROUTE[0] * f + 3
                need(t)
                dve.wait_ge(s_ex, at(s_ex, t, f + 1))
                done(dve.tensor_reduce(mx[:], ex[:], AX.X, ALU.add))
                need(t)
                done(dve.reciprocal(mx[:], mx[:]))
                need(t)
                done(dve.tensor_tensor(pr[:], ex[:], bc(mx[:]), ALU.mult))
                largest(t, pick1)

            def route_second(t, f):
                route_step[0] = N_ROUTE[0] * f + 11
                comb = comb1 if f else comb0
                need(t)
                done(dve.scalar_tensor_tensor(out=ex[:], in0=pick1[:], scalar=-4.0, in1=ex[:], op0=ALU.mult, op1=ALU.add))
                largest(t, pick2)
                need(t)
                done(dve.tensor_tensor(pick1[:], pick1[:], pick2[:], ALU.add))
                need(t)
                dve.wait_ge(s_combT, at(s_combT, t, 0))
                done(dve.tensor_tensor(comb[:, :, 0:NE], pick1[:], pr[:], ALU.mult))
                if f == 0:
                    dve.wait_ge(s_sg, at(s_sg, t, 1))
                    done(dve.tensor_scalar(sg[:], sg[:], 1.0, None, ALU.add))
                    need(t)
                    done(dve.reciprocal(comb[:, :, NE], sg[:]))
                assert route_step[0] == sum(N_ROUTE[:f + 1]), route_step

            do = {"stats": stats_, "step0": step0, "step1": step1, "hw0": hw0, "shared": shared_,
                  "scale": scale, "y_sum0": y_sum0, "residual0": residual0, "y_sum1": y_sum1, "gate1": gate1,
                  "residual1": residual1, "route_max": route_max, "route_first": route_first,
                  "route_second": route_second}

            def product(t, n):
                j, i = n // SHI, n % SHI
                c = (n - S0) // HALF if n >= S0 else n // (H0 * HALF)
                if i == 0:
                    dve.wait_ge(s_dtxrep, at(s_dtxrep, t, j + 1))
                    if n in (0, S0 // NC):
                        dve.wait_ge(s_brep[0][c], at(s_brep[0][c], t, 16 * SLO * c))
                    elif n in (S0, S0 + HALF):
                        dve.wait_ge(s_brep[1][c], at(s_brep[1][c], t, 16 * SLO))
                dve.wait_ge(s_scan, at(s_scan, t, max(n - 1, 0)))
                dve.tensor_tensor(u[:, n % 2, :], dtx_rep[:, j % 2, :], b_rep[:, c, i, :], ALU.mult).then_inc(s_u, 1)

            def scan(t, n):
                lay1 = n >= S0
                c = (n - S0) // HALF if lay1 else n // (H0 * HALF)
                j, i = n // SHI, n % SHI
                k = (j - (KS0 if lay1 else 0)) % (KPH if lay1 else H0 * KPH)
                dve.wait_ge(s_u, at(s_u, t, n + 1))
                dve.wait_ge(s_da, at(s_da, t, n + 1))
                dve.wait_ge(s_hc, at(s_hc, t, min(max(n - HR + 1, 0), S0)))
                dve.wait_ge(s_hsum, at(s_hsum, t, n - HR + 1 if lay1 else 0))
                first = 0 if n < S0 else S0
                if c == 0:
                    ends = (S0 // NC // SHI if lay1 else 0) + (n - first) // SHI
                else:
                    ends = S0 // NC // SHI + (HALF // SHI if lay1 else 0)
                dve.wait_ge(s_carry, at(s_carry, t, ends))
                dve.tensor_tensor_scan(h[:, n % HR, :], da[:, n % DR, :], u[:, n % 2, :],
                                       0.0 if c == 0 else carry[:, k, i:i + 1], ALU.mult, ALU.add
                                       ).then_inc(s_scan, 1)
                if c == 0 and i == SHI - 1:
                    dve.wait_ge(s_scan, at(s_scan, t, n + 1))
                    dve.tensor_copy(carry[:, k, :], h[:, :, CH - 1]).then_inc(s_carry, 1)

            def one_pass(t, have):
                so_far = {}
                for n in range(-1, STEPS):
                    stage = SCAN0 if n < S0 else SCAN1
                    if n in (0, S0):
                        if stage in have:
                            product(t, n)
                        else:
                            stand_in(dve, t, so_far, "dve", stage, ())
                        add_up(so_far, "dve", stage, ())
                    if n >= 0 and stage in have:
                        if n + 1 not in (S0, STEPS):
                            product(t, n + 1)
                        scan(t, n)
                    for of, piece, args in pieces("dve", n):
                        if of in have:
                            do[piece](t, *args)
                        else:
                            stand_in(dve, t, so_far, "dve", piece, args)
                        add_up(so_far, "dve", piece, args)

            passes(dve, one_pass)
        @block.tensor
        def _(pe):
            pe.wait_ge(s_load, N_LOAD)
            pe.wait_ge(s_setup_act, 1)
            for lay in range(2):
                for j in range(6):
                    ins = pe.matmul(mm[:, lay, NB * j:NB * j + NB], w_mod[:, lay, D * j:D * j + D], silu_c[:, lay, :],
                                    start=True, stop=True)
                ins.then_inc(s_setup_pe, 1)
            pe.matmul(mm[:, 2, 0:D], w_x1dt[:], w_dt1[:], start=True, stop=True)
            pe.matmul(mm[:, 2, D:2 * D], w_x1c[:], w_c1[:], start=True, stop=True).then_inc(s_setup_pe, 1)
            for g, (lay, j) in enumerate(((0, 2), (0, 5), (1, 5))):
                for q in range(2):
                    pe.wait_ge(s_setup, N_MODS + 2 * (g - 1) + q + 1 if g else N_COPIED)
                    for i in range(NB // 2):
                        bb = NB // 2 * q + i
                        ins = pe.matmul(mm[:, q, D * i:D * i + D], silu_c[:, lay, bb:bb + 1].to_broadcast([P, P]),
                                        w_mod[:, lay, D * j:D * j + D], start=True, stop=True)
                    ins.then_inc(s_setup_pe, 1)
            pe.wait_ge(s_setup, N_SETUP)
            pe.wait_ge(s_const, N_CONST)

            def xnT(t, pos, c):
                pe.wait_ge(s_xn, at(s_xn, t, NC * pos + c + 1))
                v = claim(pe, t, ("norm", pos, c))
                for i in range(TPC):
                    ins = pe.transpose(v[:, P * i:P * i + P], xn[:, TPC * c + i, :], ident[:])
                ins.then_inc(s_xnT, 1)

            def conv(v, w_taps, taps, first, c, m):
                for k in range(taps):
                    o = 3 + CH * c + k - first
                    ins = pe.matmul(v, w_taps[:, k, P * m:P * m + P], hTa[:, o:o + CH], start=(k == 0), stop=(k == taps - 1))
                return ins

            def in0(t, what, c, m):
                pe.wait_ge(s_hT, at(s_hT, t, NC * N_IN0 + NC))
                v = claim(pe, t, ("in", IN_0[what, c, m]))
                if what == "xs":
                    ins = conv(v, w_conv0, TAPS0, TAPS0 - 1, c, m)
                else:
                    ins = pe.matmul(v, w_in0[:, DI + P * m:DI + P * m + P], hTa[:, 3 + CH * c:3 + CH * c + CH],
                                    start=True, stop=True)
                ins.then_inc(s_in, 1)

            def in1(t, what, c):
                pe.wait_ge(s_hT, at(s_hT, t, NC * N_IN1 + NC))
                v = claim(pe, t, ("in", IN_1[what, c]))
                if what == "xs":
                    ins = conv(v, w_conv1, TAPS1, TAPS1 // 2, c, 0)
                else:
                    ins = pe.matmul(v, w_in1[:, D:2 * D], hTa[:, 3 + CH * c:3 + CH * c + CH], start=True, stop=True)
                ins.then_inc(s_in, 1)

            def xdbl_0(t, c):
                pe.wait_ge(s_in_act, at(s_in_act, t, IN_0["xs", c, H0 - 1] + 1))
                v = claim(pe, t, ("xdbl", NC + c))
                for m in range(H0):
                    ins = pe.matmul(v[0:1 + 2 * NS, :], w_x0[:, m, :], xs[:, m, CH * c:CH * c + CH],
                                    start=(m == 0), stop=(m == H0 - 1))
                ins.then_inc(s_xdbl, 1)

            def xdbl_1(t, c):
                pe.wait_ge(s_in_act, at(s_in_act, t, IN_1["xs", c] + 1))
                v = claim(pe, t, ("xdbl", c))
                pe.matmul(v[0:NS, :], w_x1b[:], xs1[:, CH * c:CH * c + CH], start=True, stop=True).then_inc(s_xdbl, 1)

            def cmat(t, c):
                v = claim(pe, t, ("cmat", c))
                pe.matmul(v, w_cx1[:], xs1[:, CH * c:CH * c + CH], start=True, stop=True).then_inc(s_cpe, 1)

            def dtpre0(t, c, m):
                pe.wait_ge(s_xdbl_act, at(s_xdbl_act, t, NC + c + 1))
                v = claim(pe, t, ("dtpre", NC + c * H0 + m))
                pe.matmul(v, w_dt0[0:1, P * m:P * m + P], xdbl[0:1, CH * c:CH * c + CH],
                          start=True, stop=True).then_inc(s_dtpre, 1)

            def dtpre1(t, c):
                v = claim(pe, t, ("dtpre", c))
                pe.matmul(v, w_dtx1[:], xs1[:, CH * c:CH * c + CH], start=True, stop=True).then_inc(s_dtpre, 1)

            def lg_(t, f):
                hT, wr, width = (hTb, gate_w1, NE) if f else (hTa, router, NE + 1)
                pe.wait_ge(s_hT, at(s_hT, t, NC * (N_MOE1 if f else N_MOE0) + NC))
                v = claim(pe, t, ("lg", f))
                for i in range(TILES):
                    ins = pe.matmul(v[:, width * i:width * (i + 1)], hT[:, 3 + P * i:3 + P * i + P], wr[:],
                                    start=True, stop=True)
                ins.then_inc(s_lg, 1)

            def combT_(t, f, c):
                comb, width = (comb1, NE) if f else (comb0, NE + 1)
                pe.wait_ge(s_route, at(s_route, t, sum(N_ROUTE[:f + 1])))
                v = claim(pe, t, ("combT", f, c))
                for i in range(TPC):
                    ins = pe.transpose(v[0:width, P * i:P * i + P], comb[:, TPC * c + i, 0:width], ident[:])
                ins.then_inc(s_combT, 1)

            def h1_(t, c, e):
                v = claim(pe, t, ("h1", c, e))
                pe.matmul(v, w1[:, e, :], hTa[:, 3 + CH * c:3 + CH * c + CH], start=True, stop=True).then_inc(s_h1, 1)

            def second0(t, c, e):
                acc = claim(pe, t, ("acc", 0, c)) if e == 0 else bank_of(("acc", 0, c))
                if e < NE:
                    pe.wait_ge(s_hw, at(s_hw, t, NE * c + e + 1))
                else:
                    pe.wait_ge(s_hws, at(s_hws, t, c + 1))
                for i in range(TPC):
                    ins = pe.matmul(acc[:, D * i:D * i + D], hw[:, e % 2, P * i:P * i + P], w2[:, e, :],
                                    start=(e == 0 and i == 0), stop=(e == NE), skip_group_check=True)
                ins.then_inc(s_hwu, 1)

            def bias1(t, c):
                acc = claim(pe, t, ("acc", 1, c))
                pe.wait_ge(s_combT_act, at(s_combT_act, t, NC + c + 1))
                for i in range(TPC):
                    pe.matmul(acc[:, D * i:D * i + D], combT[0:NE, CH * c + P * i:CH * c + P * i + P], b_e1[:],
                              start=(i == 0), stop=False, skip_group_check=True)

            def second1(t, c, e):
                acc = bank_of(("acc", 1, c))
                pe.wait_ge(s_hw1, at(s_hw1, t, NE * c + e + 1))
                for i in range(TPC):
                    ins = pe.matmul(acc[:, D * i:D * i + D], hw[:, e % 2, P * i:P * i + P], w_e1[:, e, :],
                                    start=False, stop=(e == NE - 1), skip_group_check=True)
                ins.then_inc(s_hwu, 1)

            def out0(t, c):
                pe.wait_ge(s_wg, at(s_wg, t, 1))
                pe.wait_ge(s_y2, at(s_y2, t, H0 * (c + 1)))
                v = claim(pe, t, ("out0", c))
                for i in range(TPC):
                    for m in range(H0):
                        ins = pe.matmul(v[:, D * i:D * i + D], y2[:, m, P * i:P * i + P], w_out0g[:, m, :],
                                        start=(m == 0), stop=(m == H0 - 1))
                ins.then_inc(s_out0, 1)

            def out1(t, c):
                pe.wait_ge(s_y1, at(s_y1, t, NC * H0 + c + 1))
                v = claim(pe, t, ("out1", c))
                pe.matmul(v, w_out1[:], y1[:], start=True, stop=True).then_inc(s_out1, 1)

            def out1_T(t, c):
                pe.wait_ge(s_o1, at(s_o1, t, c + 1))
                v = claim(pe, t, ("o1T", c))
                for i in range(TPC):
                    ins = pe.transpose(v[:, D * i:D * i + D], y2[:, 0, P * i:P * i + P], ident[:])
                ins.then_inc(s_o1T, 1)

            do = {"xnT": xnT, "in0": in0, "in1": in1, "xdbl0": xdbl_0, "xdbl1": xdbl_1, "cmat": cmat, "dtpre0": dtpre0,
                  "dtpre1": dtpre1, "lg": lg_, "combT": combT_, "h1": h1_, "second0": second0, "bias1": bias1,
                  "second1": second1, "out0": out0, "out1": out1, "out1_T": out1_T}

            def replicate(t, j):
                lay1 = j >= KS0
                kn = KPH if lay1 else H0 * KPH
                c, k = (j - (KS0 if lay1 else 0)) // kn, (j - (KS0 if lay1 else 0)) % kn
                m = k // KPH
                pe.wait_ge(s_dtx, at(s_dtx, t, c + 1) if lay1 else at(s_dtx, t - 1, NC + c * H0 + m + 1))
                pe.wait_ge(s_u, at(s_u, t, SHI * max(j - 1, 0)))
                src = dtx1 if lay1 else dtx[:, m, :]
                pe.matmul(dtx_rep[:, j % 2, :], rep[:, k % KPH, :], src[:, CH * c:CH * c + CH],
                          start=True, stop=True).then_inc(s_dtxrep, 1)

            def state_sums(t, n):
                j, i = n // SHI, n % SHI
                kk, half = j % KPH, j // KPH
                if n < S0:
                    pe.wait_ge(s_hc, at(s_hc, t, n + 1))
                    src = hc[:, n % CR, :]
                else:
                    pe.wait_ge(s_scan, at(s_scan, t, n + 1))
                    src = h[:, n % HR, :]
                if kk == 0 and i == 0:
                    pe.wait_ge(s_y1, at(s_y1, t, half))
                pe.matmul(ysum[R * kk:R * kk + R, :], state_sum[:], src, start=(i == 0), stop=(i == SHI - 1)
                          ).then_inc(s_hsum, 1)

            def one_pass(t, have):
                so_far = {}
                for n in range(-1, STEPS):
                    stage = SCAN0 if n < S0 else SCAN1
                    if n in (0, S0):
                        if stage in have:
                            replicate(t, n // SHI)
                        else:
                            stand_in(pe, t, so_far, "pe", stage, ())
                        add_up(so_far, "pe", stage, ())
                    if n >= 0 and stage in have:
                        if n % SHI == 0 and n + SHI not in (S0, STEPS):
                            replicate(t, n // SHI + 1)
                        state_sums(t, n)
                    for of, piece, args in pieces("pe", n):
                        if of in have:
                            do[piece](t, *args)
                        else:
                            if bank_use(piece, args):
                                claim(pe, t, bank_use(piece, args)[0])
                            stand_in(pe, t, so_far, "pe", piece, args)
                        add_up(so_far, "pe", piece, args)

            passes(pe, one_pass)


_NAMES = ["w_in0", "conv0", "conv_b0", "w_x0", "w_dt0", "b_dt0", "a_log0", "d0", "w_out0", "router", "w1", "w2", "w_in1",
          "conv1", "w_x1dt", "w_x1b", "w_x1c", "w_dt1", "w_c1", "b_dt1", "a_log1", "d1", "w_out1", "gate_w1", "gate_b1",
          "w_e1", "b_e1", "c_t", "w_mod"]


def kernel(**inputs):
    import numpy as _np
    import concourse.bacc as _bacc
    from concourse.bass_utils import run_bass_kernel_spmd as _run

    g = {k: _np.asarray(v) for k, v in inputs.items()}

    def halves(a):
        return a.reshape((H0, P) + a.shape[1:]).swapaxes(0, 1)

    def blocks(a):
        return a.reshape(-1, R, SLO, SHI).transpose(2, 1, 0, 3).reshape(P, -1, SHI)

    wx1 = g["L1_attn_W_x"]
    sgu = g["L0_ffn_shared_gate_up"].reshape(D, 2, P)
    laid = {
        "w_in0": g["L0_attn_W_in"],
        "conv0": g["L0_attn_conv_w"].reshape(DI, TAPS0).T,
        "conv_b0": g["L0_attn_conv_b"].reshape(H0, P).T,
        "w_x0": halves(g["L0_attn_W_x"]),
        "w_dt0": g["L0_attn_W_dt"],
        "b_dt0": g["L0_attn_b_dt"].reshape(H0, P).T,
        "a_log0": blocks(g["L0_attn_A_log"]),
        "d0": g["L0_attn_D_param"].reshape(H0, P).T,
        "w_out0": halves(g["L0_attn_W_out"]),
        "router": _np.concatenate([g["L0_ffn_router_w"], g["L0_ffn_shared_gate_w"]], axis=1),
        "w1": _np.concatenate([g["L0_ffn_w1"].transpose(1, 0, 2), sgu], axis=1),
        "w2": _np.concatenate([g["L0_ffn_w2"].transpose(1, 0, 2), g["L0_ffn_shared_down"][:, None, :]], axis=1),
        "w_in1": g["L1_attn_W_in"].T,
        "conv1": g["L1_attn_conv_w"].T,
        "w_x1dt": wx1[:R1],
        "w_x1b": wx1[R1:R1 + NS].T,
        "w_x1c": wx1[R1 + NS:],
        "w_dt1": g["L1_attn_W_dt"].T,
        "w_c1": g["L1_attn_W_C"].T,
        "b_dt1": g["L1_attn_b_dt"].reshape(P, 1),
        "a_log1": blocks(g["L1_attn_A_log"]),
        "d1": g["L1_attn_D_param"].reshape(P, 1),
        "w_out1": g["L1_attn_W_out"].T,
        "gate_w1": g["L1_ffn_gate_w"].T,
        "gate_b1": g["L1_ffn_gate_b"],
        "w_e1": g["L1_ffn_expert_w"].transpose(2, 0, 1),
        "b_e1": g["L1_ffn_expert_b"],
        "c_t": _np.stack([g["L0_c"].T, g["L1_c"].T], axis=1),
        "w_mod": _np.stack([g["L0_wmod"], g["L1_wmod"]], axis=1),
    }
    nc = _bacc.Bacc("TRN2", target_bir_lowering=False, num_devices=1)
    arrays, w = {}, {}
    for name in _NAMES:
        a = _np.ascontiguousarray(laid[name])
        arrays[f"in_{name}"] = a
        w[name] = nc.dram_tensor(f"in_{name}", a.shape, mybir.dt.from_np(a.dtype), kind="ExternalInput").ap()
    x = _np.ascontiguousarray(g["L0_attn_x"])
    arrays["in_x"] = x
    x_ap = nc.dram_tensor("in_x", x.shape, F32, kind="ExternalInput").ap()
    out = nc.dram_tensor("out_0", (NB, T, D), F32, kind="ExternalOutput").ap()
    rows0 = nc.dram_tensor("rows0", (1 + 2 * NS, T), F32, kind="Internal").ap()
    rows1 = nc.dram_tensor("rows1", (NS, T), F32, kind="Internal").ap()
    gates = nc.dram_tensor("gate_rows", (3, NB, D), F32, kind="Internal").ap()
    comb0 = nc.dram_tensor("comb_rows0", (NE + 1, T), F32, kind="Internal").ap()
    comb1 = nc.dram_tensor("comb_rows1", (NE, T), F32, kind="Internal").ap()
    adaln_blocks(nc, x_ap, w, rows0, rows1, comb0, comb1, gates, out)
    r = _run(nc, [arrays], core_ids=[0])
    return r.results[0]["out_0"]
```

```python
from contextlib import ExitStack

import concourse.bass as bass
from concourse import mybir

F32 = mybir.dt.float32
ALU = mybir.AluOpType
ACT = mybir.ActivationFunctionType
AX = mybir.AxisListType

P = 128
NB = 8
T = 1024
D = 128
DI = 256
NS = 16
NE = 8
R1 = 64
TILES = T // P
CH = 512
NC = T // CH
TPC = CH // P
H0 = DI // P
SHI = 4
SLO = NS // SHI
R = P // SLO
KPH = P // R
TAPS0 = 4
TAPS1 = 3
GATE_MIN = 0.25
EPS = 1e-5
MB = 3
HALF = KPH * SHI
S0 = KPH * H0 * NC * SHI
S1 = KPH * NC * SHI
KS0 = S0 // SHI
KS1 = S1 // SHI
HR = 4
CR = 3
DR = 5


def adaln_blocks(nc, x_in, w, rows0_dram, rows1_dram, comb0_dram, comb1_dram, gates_dram, out):
    with ExitStack() as ctx:
        def sb(name, shape):
            return ctx.enter_context(nc.sbuf_tensor(name, shape, F32))

        def ps(name, shape):
            return ctx.enter_context(nc.psum_tensor(name, shape, F32))

        per = {}
        counted = []

        def sem(name, per_pass=True):
            s = ctx.enter_context(nc.semaphore(name))
            per[s.name] = 0
            if per_pass:
                counted.append(s)
            return s

        def at(s, t, n):
            return t * per[s.name] + n + 1

        w_z0 = sb("w_z0", [P, DI])
        conv_b0 = sb("conv_b0", [P, H0])
        w_x0 = sb("w_x0", [P, H0, 1 + 2 * NS])
        w_dt0 = sb("w_dt0", [1, DI])
        b_dt0 = sb("b_dt0", [P, H0])
        d0 = sb("d0", [P, H0])
        w_out0 = sb("w_out0", [P, H0, D])
        router = sb("router", [P, NE + 1])
        w1 = sb("w1", [P, NE + 2, P])
        w2 = sb("w2", [P, NE + 1, D])
        w_z1 = sb("w_z1", [P, D])
        w_x1b = sb("w_x1b", [P, NS])
        b_dt1 = sb("b_dt1", [P, 1])
        d1 = sb("d1", [P, 1])
        w_out1 = sb("w_out1", [P, D])
        gate_w1 = sb("gate_w1", [P, NE])
        gate_b1 = sb("gate_b1", [P, NE])
        w_e1 = sb("w_e1", [P, NE, D])
        b_e1 = sb("b_e1", [NE, D])
        c_t = sb("c_t", [P, 2, NB])

        ident = sb("ident", [P, P])
        rep = sb("rep", [P, KPH, P])
        state_sum = sb("state_sum", [P, R])
        rev = sb("rev", [P, NE])
        w_conv0 = sb("w_conv0", [P, TAPS0, DI])
        w_conv1 = sb("w_conv1", [P, TAPS1, D])
        neg_a0 = sb("neg_a0", [P, H0 * KPH, SHI])
        neg_a1 = sb("neg_a1", [P, KPH, SHI])
        w_dtx1 = sb("w_dtx1", [P, D])
        w_cx1 = sb("w_cx1", [P, D])
        silu_c = sb("silu_c", [P, 2, NB])
        mods = sb("mods", [P, 2, 6, NB])
        gate_a = sb("gate_a", [P, 1, D])
        gate_b = sb("gate_b", [P, 2, D])
        eps8 = sb("eps8", [P, TILES])
        neg_half = sb("neg_half", [P, TILES])
        neg_one = sb("neg_one", [P, TILES])

        xa = sb("xa", [P, TILES, D])
        xr0 = sb("xr0", [P, TILES, D])
        xr1 = sb("xr1", [P, TILES, D])
        xr2 = sb("xr2", [P, TILES, D])
        stats = sb("stats", [P, TILES, 6])
        mean_var = sb("mean_var", [P, TILES, 2])
        var_eps = sb("var_eps", [P, TILES])
        rstd = sb("rstd", [P, TILES])
        shift = sb("shift", [P, TILES])
        xn = sb("xn", [P, TILES, D])
        hTa = sb("hTa", [P, T + 4])
        hTb = sb("hTb", [P, T + 4])
        hTc = sb("hTc", [P, T + 4])
        xs = sb("xs", [P, H0, T])
        zs = sb("zs", [P, H0, T])
        xs1 = sb("xs1", [P, T])
        zs1 = sb("zs1", [P, T])
        conv0_bc = zs[:, 0, :].rearrange("p (k d) -> p k d", k=TAPS0)
        conv1_bc = zs[:, 1, 0:TAPS1 * D].rearrange("p (k d) -> p k d", k=TAPS1)
        xdbl = sb("xdbl", [1 + 2 * NS, T])
        dt = sb("dt", [P, H0, T])
        dtx = sb("dtx", [P, H0, T])
        dt1 = sb("dt1", [P, T])
        dtx1 = sb("dtx1", [P, T])
        gate_tmp = dtx[:, 0, :]
        b_rep = sb("b_rep", [P, NC, SHI, CH])
        c_rep = sb("c_rep", [P, SHI, T])
        w_mod = b_rep[:].rearrange("p c s t -> p (c s t)")[:, 0:2 * 6 * D].rearrange("p (l d) -> p l d", l=2)
        low_rank = b_rep[:].rearrange("p c s t -> p (c s t)")[:, 2 * 6 * D:2 * 6 * D + 4 * D]
        w_x1dt, w_dt1 = low_rank[0:R1, 0:D], low_rank[0:R1, D:2 * D]
        w_x1c, w_c1 = low_rank[0:NS, 2 * D:3 * D], low_rank[0:NS, 3 * D:4 * D]
        w_x_in = b_rep[:].rearrange("p c s t -> p (c s t)")[:, 2 * 6 * D + 4 * D:2 * 6 * D + 4 * D + DI + D]
        w_x_in0, w_x_in1 = w_x_in[:, 0:DI], w_x_in[:, DI:DI + D]
        gates = c_rep[:].rearrange("p s t -> p (s t)")[:, 0:3 * NB * D].rearrange("p (g b d) -> p g b d", g=3, b=NB)
        dt_rep = sb("dt_rep", [P, 2, CH])
        carry = sb("carry", [P, H0 * KPH, SHI])
        da = sb("da", [P, DR, CH])
        h = sb("h", [P, HR, CH])
        hc = sb("hc", [P, CR, CH])
        y1 = sb("y1", [P, CH])
        y2 = sb("y2", [P, H0, CH])
        w_out0g = sb("w_out0g", [P, H0, D])
        c_mat = sb("c_mat", [P, T])
        mx = sb("mx", [P, TILES])
        lg = sb("lg", [P, TILES, NE])
        ex = sb("ex", [P, TILES, NE])
        sg = sb("sg", [P, TILES])
        pr = sb("pr", [P, TILES, NE])
        key = sb("key", [P, TILES, NE])
        pick1 = sb("pick1", [P, TILES, NE])
        pick2 = sb("pick2", [P, TILES, NE])
        comb0 = sb("comb0", [P, TILES, NE + 1])
        comb1 = sb("comb1", [P, TILES, NE])
        combT = sb("combT", [NE + 1, T])
        comb_rep = sb("comb_rep", [P, 3, CH])
        hw = sb("hw", [P, 2, CH])
        gate_act = sb("gate_act", [P, CH])
        shared = sb("shared", [P, CH])
        ffn = sb("ffn", [P, TPC, D])

        u = ps("u", [P, 2, CH])
        dtx_rep = ps("dtx_rep", [P, 2, CH])
        ysum = ps("ysum", [P, CH])
        mm = ps("mm", [P, MB, CH])

        s_load = sem("s_load", False)
        s_const = sem("s_const", False)
        s_setup_pe = sem("s_setup_pe", False)
        s_setup_act = sem("s_setup_act", False)
        s_setup = sem("s_setup", False)
        s_gstore = sem("s_gstore", False)
        s_x = sem("s_x")
        s_again = [sem(f"s_again{c}") for c in range(NC)]
        s_stats = sem("s_stats")
        s_rstd = sem("s_rstd")
        s_xn = sem("s_xn")
        s_xnT = sem("s_xnT")
        s_hT = sem("s_hT")
        s_in = sem("s_in")
        s_in_act = sem("s_in_act")
        s_xdbl = sem("s_xdbl")
        s_xdbl_act = sem("s_xdbl_act")
        s_cpe = sem("s_cpe")
        s_cmat = sem("s_cmat")
        s_dtpre = sem("s_dtpre")
        s_pre = sem("s_pre")
        s_soft = sem("s_soft")
        s_dt = sem("s_dt")
        s_dtx = sem("s_dtx")
        s_brep = [[sem(f"s_brep{lay}{c}") for c in range(NC)] for lay in range(2)]
        s_crep = sem("s_crep")
        s_rows0 = [sem(f"s_rows0{c}") for c in range(NC)]
        s_rows1 = sem("s_rows1")
        s_comb_row = [[sem(f"s_comb_row{f}{c}") for c in range(NC)] for f in range(2)]
        s_gate = [sem(f"s_gate{g}") for g in range(3)]
        s_dtrep = [sem(f"s_dtrep{i}") for i in range(2)]
        s_dtxrep = sem("s_dtxrep")
        s_da = sem("s_da")
        s_u = sem("s_u")
        s_scan = sem("s_scan")
        s_carry = sem("s_carry")
        s_hc = sem("s_hc")
        s_hsum = sem("s_hsum")
        s_y1 = sem("s_y1")
        s_y2 = sem("s_y2")
        s_wg = sem("s_wg")
        s_out0 = sem("s_out0")
        s_xr0 = sem("s_xr0")
        s_cy = sem("s_cy")
        s_out1 = sem("s_out1")
        s_o1 = sem("s_o1")
        s_o1T = sem("s_o1T")
        s_xr2 = sem("s_xr2")
        s_lg = sem("s_lg")
        s_route = sem("s_route")
        s_ex = sem("s_ex")
        s_sg = sem("s_sg")
        s_combT = sem("s_combT")
        s_combT_act = sem("s_combT_act")
        s_crow = [sem(f"s_crow{i}") for i in range(3)]
        s_h1 = sem("s_h1")
        s_h1a = sem("s_h1a")
        s_sh = sem("s_sh")
        s_hw = sem("s_hw")
        s_hws = sem("s_hws")
        s_hwu = sem("s_hwu")
        s_hw1 = sem("s_hw1")
        s_ffn = sem("s_ffn")
        s_xr1 = sem("s_xr1")
        s_xo = sem("s_xo")
        s_store = [sem(f"s_store{c}") for c in range(NC)]
        N_CONST = 9 + NE + 1 + KPH + SLO + TAPS0 + TAPS1
        N_COPIED = 6
        N_MODS = N_COPIED + 4 + 4
        N_SETUP = N_MODS + 3 * 2 + 3 * 4
        IN0, SCAN0, ROUTE0, MOE0, IN1, SCAN1, TAIL1, MOE1 = \
            "in0", "scan0", "route0", "moe0", "in1", "scan1", "tail1", "moe1"
        LAG = {IN0: 0, SCAN0: 1, ROUTE0: 1, MOE0: 2, IN1: 2, SCAN1: 2, TAIL1: 3, MOE1: 3}
        STEPS = S0 + S1
        N_MOE1, N_IN0, N_IN1, N_MOE0 = range(4)
        NORM_MODS = {N_MOE0: (0, 3, ROUTE0), N_MOE1: (1, 3, MOE1), N_IN1: (1, 0, IN1), N_IN0: (0, 0, IN0)}
        IN_1 = {("xs", c): 2 * H0 + c for c in range(NC)} | {("zs", c): 2 * H0 + NC + c for c in range(NC)}
        IN_0 = {(what, c, m): c * (2 * H0 + 2 * NC) + H0 * k + m
                for c in range(NC) for k, what in enumerate(("xs", "zs")) for m in range(H0)}
        XDBL_1 = {c: 1 + c for c in range(NC)}
        XDBL_0 = {0: 0, 1: 1 + NC}
        DTPRE_1 = {c: H0 + c for c in range(NC)}
        DTPRE_0 = {(c, m): c * (H0 + NC) + m for c in range(NC) for m in range(H0)}
        N_ROUTE = (21, 19)
        ROUTE_FIRST = (N_ROUTE[1], 0)
        ROUTE_ORDER = (1, 0)
        EXP0 = NE + 1
        END1 = {NC - 1: 0} | {c: c + 1 for c in range(NC - 1)}
        Y0 = 1

        PLAN = []

        def plan(stage, engine, step, piece, *args):
            PLAN.append((step, stage, engine, piece, args))

        def plan_norm(stage, pos, steps, apart=0):
            plan(stage, "dve", steps[0], "stats", pos)
            plan(stage, "pool", steps[1], "rstd", pos)
            for c in range(NC):
                plan(stage, "act", steps[2], "norm", pos, c)
                plan(stage, "pe", steps[3] + apart * c, "xnT", pos, c)
                plan(stage, "act", steps[4] + apart * c, "hT", pos, c)

        def plan_router(stage, f, steps, apart=0):
            plan(stage, "pe", steps[0], "lg", f)
            plan(stage, "dve", steps[1], "route_max", f)
            plan(stage, "act", steps[2], "ex", f)
            plan(stage, "dve", steps[3], "route_first", f)
            plan(stage, "dve", steps[4], "route_second", f)
            for c in range(NC):
                plan(stage, "pe", steps[5] + apart * c, "combT", f, c)
                plan(stage, "act", steps[6] + apart * c, "combT", f, c)
                plan(stage, "sp", steps[6] + apart * c, "comb_store", f, c)

        def plan_end1(stage, c, steps):
            plan(stage, "dve", steps[0], "y_sum1", c)
            plan(stage, "pe", steps[1], "out1", c)
            plan(stage, "dve", steps[2], "gate1", c)
            plan(stage, "pe", steps[3], "out1_T", c)
            plan(stage, "dve", steps[4], "residual1", c)

        plan_end1(TAIL1, NC - 1, (-1, 0, 1, 2, 3))
        for c in range(NC - 1):
            o = S0 + HALF * (c + 1)
            plan_end1(SCAN1, c, (o + 2, o + 5, o + 7, o + 9, o + 11))

        plan(SCAN0, "sp", 0, "gate_load", 0)
        plan(SCAN0, "sp", 0, "fill_b", 0, 1)
        plan(MOE0, "sp", 0, "gate_load", 1)
        plan(MOE1, "sp", 0, "gate_load", 2)
        plan(SCAN0, "pool", 4, "w_gate")

        def pair_step(k):
            return 4 * k + 2 * (k >= 3)

        for c in range(NC):
            for p in range((NE + 2) // 2):
                s = pair_step(c * (NE + 2) // 2 + p)
                for e in (2 * p, 2 * p + 1):
                    plan(MOE0, "pe", s, "h1", c, e)
                    if e < EXP0:
                        plan(MOE0, "act", s + 1, "silu_h", c, e)
                    if e < NE:
                        plan(MOE0, "dve", s + 3, "hw0", c, e)
                        plan(MOE0, "pe", s + 4, "second0", c, e)
                    if e < EXP0:
                        n = c * EXP0 + e - 3
                        cc, ee = n // EXP0, n % EXP0
                        r = 0 if n < 0 else pair_step(cc * (NE + 2) // 2 + ee // 2) + 3 + (ee == NE)
                        plan(MOE0, "sp", r, "comb_rep", c * EXP0 + e)
            plan(MOE0, "dve", s + 3, "shared", c)
            plan(MOE0, "pool", s + 4, "hws", c)
            plan(MOE0, "pe", s + 5, "second0", c, NE)
            plan(MOE0, "dve", s + 7, "scale", 0, c)
            plan(MOE0, "pool", s + 8, "moe_sum", 0, c)
            plan(SCAN0, "sp", s + 8, "load_again", c)

        plan_norm(MOE1, N_MOE1, (5, 7, 9, 12, 13))
        plan_router(MOE1, 1, (20, 21, 24, 26, 28, 40, 40), 1)

        plan_norm(IN1, N_IN1, (47, 48, 49, 50, 51), 1)
        for c in range(NC):
            plan(IN1, "pe", 53 + c, "in1", "xs", c)
            plan(IN1, "act", 55, "silu1", "xs", c)
        for c in range(NC):
            plan(IN1, "pe", 56, "dtpre1", c)
            plan(IN1, "act", 57, "relu_abs1", c)
        for c in range(NC):
            plan(IN1, "pe", 58, "xdbl1", c)
            plan(IN1, "act", 58, "xdbl1", c)
        plan(IN1, "act", 58, "soft1")
        for c in range(NC):
            plan(IN1, "dve", 62, "step1", c)
            plan(IN1, "pool", 63, "dtx1", c)
        for c in range(NC):
            plan(SCAN1, "pe", 66, "in1", "zs", c)
            plan(SCAN1, "act", 66, "silu1", "zs", c)
        for c in range(NC):
            plan(SCAN1, "pe", 68, "cmat", c)
            plan(SCAN1, "act", 68, "cmat", c)
        plan(IN1, "sp", 55, "rows1")
        plan(IN1, "sp", 55, "fill_b", 1, 0)
        plan(SCAN1, "sp", S0, "fill_b", 1, 1)

        plan(IN0, "sp", 2, "load_x")
        plan_norm(IN0, N_IN0, (30, 31, 33, 42, 43))
        IN0_STEPS = ({"xs": 45, "xs_act": 48, "zs": 49, "zs_act": 50, "xdbl": 49, "dtpre": (51, 52), "soft": 71},
                     {"xs": 70, "xs_act": 74, "zs": 75, "zs_act": 76, "xdbl": 79, "dtpre": (81, 81), "soft": 82})
        for c, at_step in enumerate(IN0_STEPS):
            for m in range(H0):
                plan(IN0, "pe", at_step["xs"] + m, "in0", "xs", c, m)
                plan(IN0, "act", at_step["xs_act"], "silu0", "xs", c, m)
            for m in range(H0):
                plan(IN0, "pe", at_step["zs"], "in0", "zs", c, m)
                plan(IN0, "act", at_step["zs_act"], "silu0", "zs", c, m)
            plan(IN0, "pe", at_step["xdbl"], "xdbl0", c)
            plan(IN0, "act", at_step["xdbl"] + 1, "xdbl0", c)
            plan(IN0, "sp", at_step["xdbl"] + 1, "rows0", c)
            for m in range(H0):
                plan(IN0, "pe", at_step["dtpre"][m], "dtpre0", c, m)
                plan(IN0, "act", at_step["dtpre"][m] + 1, "relu_abs0", c, m)
            plan(IN0, "act", at_step["soft"], "soft0", c)
            for m in range(H0):
                plan(IN0, "dve", at_step["soft"] + 3 + m, "step0", c, m)
                plan(IN0, "pool", at_step["soft"] + 4 + m, "dtx0", c, m)
        plan(IN0, "sp", S0 + 17, "fill_c")
        plan(IN0, "sp", S0 + HALF + 4, "fill_b", 0, 0)

        for c in range(NC):
            s = S0 + 12 * c
            plan(MOE1, "pe", s + 1, "bias1", c)
            for e in range(NE):
                r = s + 1 + (5 * e) // 4
                plan(MOE1, "pool", r, "hw1", c, e)
                plan(MOE1, "pe", r + 1, "second1", c, e)
                plan(MOE1, "sp", r - 4 if c or e > 2 else s - 2, "comb_rep", NC * EXP0 + c * NE + e)
            plan(MOE1, "dve", s + 12, "scale", 1, c)
            plan(MOE1, "pool", s + 13, "moe_sum", 1, c)
            plan(MOE1, "sp", s + 13, "store", c)

        plan_norm(ROUTE0, N_MOE0, (79, 80, 81, 83, 84))
        plan_router(ROUTE0, 0, (86, 87, 88, 89, 90, 92, 92))

        for i in range(NC * H0):
            plan(SCAN0, "dve", HALF * (i + 1) + 2, "y_sum0", i)
            plan(SCAN0, "pool", HALF * (i + 1) + 3, "y_gated", i)
        for c, o in enumerate((44, 77)):
            plan(SCAN0, "pe", o, "out0", c)
            plan(SCAN0, "dve", o + 1, "residual0", c)

        AHEAD = {"dve": 0, "act": DR - 1, "pool": -1, "pe": -2, "sp": 2 * SHI}
        beside = {}
        for step, stage, engine, piece, args in sorted(PLAN, key=lambda p: p[0]):
            n = step + AHEAD[engine]
            n = min(max(n, -1), S0 - 1 if stage == IN1 else STEPS - 1)
            beside.setdefault((engine, n), []).append((stage, piece, args))

        def pieces(engine, n):
            return beside.get((engine, n), [])

        SIGNALS = {
            ("dve", "stats"): lambda pos: [(s_stats, 2)],
            ("dve", "route_max"): lambda f: [(s_route, 3)],
            ("dve", "route_first"): lambda f: [(s_route, 3 + 5)],
            ("dve", "route_second"): lambda f: [(s_route, N_ROUTE[f] - 11)],
            ("dve", "hw0"): lambda c, e: [(s_hw, 1)],
            ("dve", "shared"): lambda c: [(s_sh, 1)],
            ("dve", "scale"): lambda f, c: [(s_ffn, 1)],
            ("dve", "step0"): lambda c, m: [(s_dt, 1)],
            ("dve", "step1"): lambda c: [(s_dt, 1)],
            ("dve", "y_sum0"): lambda i: [(s_y1, 1)],
            ("dve", "y_sum1"): lambda c: [(s_cy, 1), (s_y1, 1)],
            ("dve", "residual0"): lambda c: [(s_xr0, 1)],
            ("dve", "gate1"): lambda c: [(s_o1, 1)],
            ("dve", "residual1"): lambda c: [(s_xr2, 1)],
            ("dve", SCAN0): lambda: [(s_u, S0), (s_scan, S0), (s_carry, S0 // SHI // NC)],
            ("dve", SCAN1): lambda: [(s_u, S1), (s_scan, S1), (s_carry, S1 // SHI // NC)],
            ("pool", "rstd"): lambda pos: [(s_rstd, 4)],
            ("pool", "w_gate"): lambda: [(s_wg, 1)],
            ("pool", "dtx0"): lambda c, m: [(s_dtx, 1)],
            ("pool", "dtx1"): lambda c: [(s_dtx, 1)],
            ("pool", "y_gated"): lambda i: [(s_y2, 1)],
            ("pool", "hw1"): lambda c, e: [(s_hw1, 1)],
            ("pool", "hws"): lambda c: [(s_hws, 1)],
            ("pool", "moe_sum"): lambda f, c: [(s_xo if f else s_xr1, 1)],
            ("pool", SCAN0): lambda: [(s_hc, S0)],
            ("pool", SCAN1): lambda: [],
            ("act", "norm"): lambda pos, c: [(s_xn, 1)],
            ("act", "hT"): lambda pos, c: [(s_hT, 1)],
            ("act", "silu0"): lambda what, c, m: [(s_in_act, 1)],
            ("act", "silu1"): lambda what, c: [(s_in_act, 1)],
            ("act", "xdbl0"): lambda c: [(s_xdbl_act, 1)],
            ("act", "xdbl1"): lambda c: [(s_xdbl_act, 1)],
            ("act", "cmat"): lambda c: [(s_cmat, 1)],
            ("act", "relu_abs0"): lambda c, m: [(s_pre, 2)],
            ("act", "relu_abs1"): lambda c: [(s_pre, 2)],
            ("act", "soft0"): lambda c: [(s_soft, 2)],
            ("act", "soft1"): lambda: [(s_soft, 2)],
            ("act", "ex"): lambda f: [(s_ex, 1)] + ([(s_sg, 1)] if f == 0 else []),
            ("act", "combT"): lambda f, c: [(s_combT_act, 1)],
            ("act", "silu_h"): lambda c, e: [(s_h1a, 1)],
            ("act", SCAN0): lambda: [(s_da, S0)],
            ("act", SCAN1): lambda: [(s_da, S1)],
            ("pe", "xnT"): lambda pos, c: [(s_xnT, 1)],
            ("pe", "in0"): lambda what, c, m: [(s_in, 1)],
            ("pe", "in1"): lambda what, c: [(s_in, 1)],
            ("pe", "xdbl0"): lambda c: [(s_xdbl, 1)],
            ("pe", "xdbl1"): lambda c: [(s_xdbl, 1)],
            ("pe", "cmat"): lambda c: [(s_cpe, 1)],
            ("pe", "dtpre0"): lambda c, m: [(s_dtpre, 1)],
            ("pe", "dtpre1"): lambda c: [(s_dtpre, 1)],
            ("pe", "lg"): lambda f: [(s_lg, 1)],
            ("pe", "combT"): lambda f, c: [(s_combT, 1)],
            ("pe", "h1"): lambda c, e: [(s_h1, 1)],
            ("pe", "second0"): lambda c, e: [(s_hwu, 1)],
            ("pe", "second1"): lambda c, e: [(s_hwu, 1)],
            ("pe", "bias1"): lambda c: [],
            ("pe", "out0"): lambda c: [(s_out0, 1)],
            ("pe", "out1"): lambda c: [(s_out1, 1)],
            ("pe", "out1_T"): lambda c: [(s_o1T, 1)],
            ("pe", SCAN0): lambda: [(s_dtxrep, S0 // SHI), (s_hsum, S0)],
            ("pe", SCAN1): lambda: [(s_dtxrep, S1 // SHI), (s_hsum, S1)],
            ("sp", "load_x"): lambda: [(s_x, 16)],
            ("sp", "load_again"): lambda c: [(s_again[c], 16)],
            ("sp", "rows0"): lambda c: [(s_rows0[c], 16)],
            ("sp", "rows1"): lambda: [(s_rows1, 16)],
            ("sp", "fill_b"): lambda lay, c: [(s_brep[lay][c], 16 * SLO)],
            ("sp", "fill_c"): lambda: [(s_crep, 16 * SLO)],
            ("sp", "comb_store"): lambda f, c: [(s_comb_row[f][c], 16)],
            ("sp", "comb_rep"): lambda n: [(s_crow[n % 3], 16)],
            ("sp", "gate_load"): lambda g: [(s_gate[g], 16)],
            ("sp", "store"): lambda c: [(s_store[c], 16)],
            ("sp", SCAN0): lambda: [(s_dtrep[i], S0 // SHI // 2 * SLO * 16) for i in range(2)],
            ("sp", SCAN1): lambda: [(s_dtrep[i], S1 // SHI // 2 * SLO * 16) for i in range(2)],
        }
        given = [SIGNALS[engine, piece](*args) for _, _, engine, piece, args in PLAN]
        given += [SIGNALS[engine, stage]() for engine in AHEAD for stage in (SCAN0, SCAN1)]
        for s, n in sum(given, []):
            per[s.name] += n

        def stand_in(eng, t, so_far, engine, piece, args):
            for s, n in SIGNALS[engine, piece](*args):
                eng.wait_ge(s, at(s, t, so_far.get(s.name, 0)))
                eng.sem_inc(s, n)

        def add_up(so_far, engine, piece, args):
            for s, n in SIGNALS[engine, piece](*args):
                so_far[s.name] = so_far.get(s.name, 0) + n

        def seq_slice(b):
            return slice(b, b + 1) if isinstance(b, int) else bass.ds(b, 1)

        PASSES = [(t, {st for st in LAG if 0 <= t - LAG[st] < NB}) for t in range(NB + max(LAG.values()))]
        HEAD = [p for p in PASSES if p[0] < max(LAG.values())]
        TAIL = [p for p in PASSES if p[0] >= NB]
        FULL = set(LAG)

        def passes(eng, one_pass):
            for t, have in HEAD:
                one_pass(t, have)
            with eng.Fori(max(LAG.values()), NB) as t:
                one_pass(t, FULL)
            for t, have in TAIL:
                one_pass(t, have)

        def bank_use(piece, args):
            if piece == "xnT":
                return ("norm",) + args, s_hT, NC * args[0] + args[1] + 1
            if piece in ("in1", "in0"):
                idx = (IN_1 if piece == "in1" else IN_0)[args]
                return ("in", idx), s_in_act, idx + 1
            if piece in ("xdbl1", "xdbl0"):
                idx = (XDBL_1 if piece == "xdbl1" else XDBL_0)[args[0]]
                return ("xdbl", idx), s_xdbl_act, idx + 1
            if piece == "cmat":
                return ("cmat", args[0]), s_cmat, args[0] + 1
            if piece in ("dtpre1", "dtpre0"):
                idx = DTPRE_1[args[0]] if piece == "dtpre1" else DTPRE_0[args]
                return ("dtpre", idx), s_pre, 2 * (idx + 1)
            if piece == "lg":
                return ("lg",) + args, s_route, ROUTE_FIRST[args[0]] + (1 if args[0] else 3)
            if piece == "combT":
                return ("combT",) + args, s_combT_act, NC * ROUTE_ORDER[args[0]] + args[1] + 1
            if piece == "h1":
                c, e = args
                freed = (s_hw, NE * c + e + 1) if e < NE else (s_h1a, EXP0 * (c + 1)) if e == NE else (s_sh, c + 1)
                return (("h1", c, e),) + freed
            if piece == "second0" and args[1] == 0:
                return ("acc", 0, args[0]), s_ffn, args[0] + 1
            if piece == "bias1":
                return ("acc", 1, args[0]), s_ffn, NC + args[0] + 1
            if piece == "out0":
                return ("out0", args[0]), s_xr0, args[0] + 1
            if piece == "out1":
                return ("out1", args[0]), s_o1, END1[args[0]] + 1
            if piece == "out1_T":
                return ("o1T", args[0]), s_xr2, END1[args[0]] + 1
            return None

        uses = []
        last = {}
        for n in range(-1, STEPS):
            for _, piece, args in pieces("pe", n):
                if bank_use(piece, args):
                    uses.append(bank_use(piece, args))
                elif piece == "second0" and args[1] == NE:
                    last["acc", 0, args[0]] = len(uses)
                elif piece == "second1" and args[1] == NE - 1:
                    last["acc", 1, args[0]] = len(uses)

        bank = {}
        holder = [None] * MB
        order = [-1] * MB
        before = {}
        for n, (name, _, _) in enumerate(uses):
            free = [i for i in range(MB) if holder[i] is None or n >= last.get(uses[holder[i]][0], -1)]
            i = min(free, key=lambda k: order[k])
            bank[name], before[name] = i, holder[i]
            holder[i], order[i] = n, last.get(name, n)

        def claim(pe, t, name):
            if before[name] is not None:
                _, s, n = uses[before[name]]
                pe.wait_ge(s, at(s, t, n))
            else:
                _, s, n = uses[holder[bank[name]]]
                if not isinstance(t, int) or t:
                    pe.wait_ge(s, at(s, t - 1, n))
            return mm[:, bank[name], :]

        def bank_of(name):
            return mm[:, bank[name], :]
        block = ctx.enter_context(nc.Block())

        loads = [
            (w_x_in0, w["w_in0"][:, 0:DI]), (w_z0[:], w["w_in0"][:, DI:2 * DI]), (conv0_bc, w["conv0"].partition_broadcast(P)), (conv_b0[:], w["conv_b0"]),
            (w_x0[:], w["w_x0"]), (w_dt0[:], w["w_dt0"]), (b_dt0[:], w["b_dt0"]), (neg_a0[:], w["a_log0"]),
            (d0[:], w["d0"]), (w_out0[:], w["w_out0"]), (router[:], w["router"]), (w1[:], w["w1"]),
            (w2[:], w["w2"]), (w_x_in1, w["w_in1"][:, 0:D]), (w_z1[:], w["w_in1"][:, D:2 * D]), (conv1_bc, w["conv1"].partition_broadcast(P)),
            (w_x1dt, w["w_x1dt"]), (w_x1b[:], w["w_x1b"]), (w_x1c, w["w_x1c"]), (w_dt1, w["w_dt1"]),
            (w_c1, w["w_c1"]), (b_dt1[:], w["b_dt1"]), (neg_a1[:], w["a_log1"]), (d1[:], w["d1"]),
            (w_out1[:], w["w_out1"]), (gate_w1[:], w["gate_w1"]), (gate_b1[:], w["gate_b1"].partition_broadcast(P)),
            (w_e1[:], w["w_e1"]), (b_e1[:], w["b_e1"]), (c_t[:], w["c_t"]), (w_mod, w["w_mod"]),
        ]
        N_LOAD = 16 * len(loads)

        @block.sync
        def _(sp_):
            for dst, src in loads:
                sp_.dma_start(dst, src).then_inc(s_load, 16)

            sp_.wait_ge(s_setup, N_SETUP)
            sp_.dma_start(gates_dram.rearrange("g b d -> (g b d)").unsqueeze(0),
                          gates[0:1, :, :, :].rearrange("o g b d -> o (g b d)")).then_inc(s_gstore, 16)
            sp_.wait_ge(s_gstore, 16)

            def value(v):
                return v if isinstance(v, int) else sp_.compute_val(v)

            def wait_all(*pairs):
                pairs = [(s, value(v)) for s, v in pairs]
                for s, v in pairs:
                    sp_.wait_ge(s, v)

            def rep_dt(t, j):
                lay1 = j >= KS0
                jj = j - KS0 if lay1 else j
                kn = KPH if lay1 else H0 * KPH
                c, k = jj // kn, jj % kn
                m, kk = k // KPH, k % KPH
                src = dt1 if lay1 else dt[:, m, :]
                wait_all((s_dt, at(s_dt, t, c + 1) if lay1 else at(s_dt, t - 1, NC + c * H0 + m + 1)),
                         (s_da, at(s_da, t, SHI * max(j - 1, 0))))
                for a in range(SLO):
                    sp_.dma_start(dt_rep[R * a:R * a + R, j % 2, :],
                                  src[R * kk:R * kk + R, CH * c:CH * c + CH]).then_inc(s_dtrep[j % 2], 16)

            def rep_rows(dst, rows, row0, s_done, cols):
                for a in range(SLO):
                    sp_.dma_start(dst[R * a:R * a + R],
                                  rows[row0 + SHI * a:row0 + SHI * a + SHI, cols].partition_broadcast(R)
                                  ).then_inc(s_done, 16)

            def gate_load(t, g):
                s, n = ((s_wg, 0), (s_ffn, 0), (s_ffn, 0))[g]
                wait_all((s, at(s, t, n)))
                stage = (SCAN0, MOE0, MOE1)[g]
                dst = gate_b[:, g - 1:g, :] if g else gate_a[:]
                sp_.dma_start(dst, gates_dram[g, seq_slice(t - LAG[stage]), :].partition_broadcast(P)
                              ).then_inc(s_gate[g], 16)

            def fill_b(t, lay, c):
                cols = slice(CH * c, CH * c + CH)
                if lay:
                    wait_all((s_rows1, at(s_rows1, t, 16)), (s_u, at(s_u, t, S0 // NC * (c + 1))))
                    rep_rows(b_rep[:, c, :, :], rows1_dram, 0, s_brep[1][c], cols)
                elif c == 0:
                    wait_all((s_rows0[0], at(s_rows0[0], t, 16)), (s_u, at(s_u, t, S0 + S1 // NC)))
                    rep_rows(b_rep[:, c, :, :], rows0_dram, 1, s_brep[0][c], cols)
                else:
                    wait_all((s_rows0[c], at(s_rows0[c], t, 0)), (s_u, at(s_u, t, 0)))
                    rep_rows(b_rep[:, c, :, :], rows0_dram, 1, s_brep[0][c], cols)

            def fill_c(t):
                wait_all((s_rows0[0], at(s_rows0[0], t, 16)), (s_rows0[1], at(s_rows0[1], t, 16)),
                         (s_hc, at(s_hc, t, S0)))
                rep_rows(c_rep, rows0_dram, 1 + NS, s_crep, slice(0, T))

            def rows0(t, c):
                wait_all((s_xdbl_act, at(s_xdbl_act, t, XDBL_0[c] + 1)), (s_crep, at(s_crep, t, 0)),
                         (s_brep[0][c], at(s_brep[0][c], t, 16 * SLO if c else 0)))
                cols = slice(CH * c, CH * c + CH)
                sp_.dma_start(rows0_dram[:, cols], xdbl[:, cols]).then_inc(s_rows0[c], 16)

            def rows1(t):
                wait_all((s_xdbl_act, at(s_xdbl_act, t, XDBL_1[NC - 1] + 1)), (s_brep[1][0], at(s_brep[1][0], t, 0)),
                         (s_brep[1][1], at(s_brep[1][1], t, 0)))
                sp_.dma_start(rows1_dram, xdbl[0:NS, :]).then_inc(s_rows1, 16)

            def comb_store(t, f, c):
                cols = slice(CH * c, CH * c + CH)
                k = NC * ROUTE_ORDER[f] + c + 1
                wait_all((s_combT_act, at(s_combT_act, t, k)), (s_hw1, at(s_hw1, t, 0)) if f else (s_hws, at(s_hws, t, NC)))
                dst, src = (comb1_dram, combT[0:NE, cols]) if f else (comb0_dram, combT[:, cols])
                sp_.dma_start(dst[:, cols], src).then_inc(s_comb_row[f][c], 16)

            def comb_rep_row(t, n):
                old = n - 3
                if old < 0:
                    used, v = s_hw1, 0
                elif old >= NC * EXP0:
                    used, v = s_hw1, old - NC * EXP0 + 1
                elif old % EXP0 == NE:
                    used, v = s_hws, old // EXP0 + 1
                else:
                    used, v = s_hw, old // EXP0 * NE + old % EXP0 + 1
                f = n >= NC * EXP0
                c, e = divmod(n - NC * EXP0, NE) if f else divmod(n, EXP0)
                src = (comb1_dram if f else comb0_dram)[e:e + 1, CH * c:CH * c + CH]
                wait_all((used, at(used, t, v)), (s_comb_row[f][c], at(s_comb_row[f][c], t, 16 if f else 0)))
                sp_.dma_start(comb_rep[:, n % 3:n % 3 + 1, :], src.partition_broadcast(P)).then_inc(s_crow[n % 3], 16)

            def tiles(dram, b, c):
                v = dram[seq_slice(b), :, :].rearrange("o (i p) d -> (o p) i d", p=P)
                return v if c is None else v[:, TPC * c:TPC * c + TPC, :]

            def load_again(t, c):
                wait_all((s_xr1, at(s_xr1, t, c + 1)))
                sp_.dma_start(xr0[:, TPC * c:TPC * c + TPC, :], tiles(x_in, t - LAG[SCAN0], c)).then_inc(s_again[c], 16)

            def load_x(t):
                wait_all((s_xn, at(s_xn, t, 0)))
                sp_.dma_start(xa[:], tiles(x_in, t, None)).then_inc(s_x, 16)

            def store(t, c):
                wait_all((s_xo, at(s_xo, t, c + 1)))
                sp_.dma_start(tiles(out, t - LAG[MOE1], c), xr2[:, TPC * c:TPC * c + TPC, :]).then_inc(s_store[c], 16)

            do = {"gate_load": gate_load, "fill_b": fill_b, "fill_c": fill_c, "rows0": rows0, "rows1": rows1, "comb_store": comb_store,
                  "comb_rep": comb_rep_row, "load_again": load_again, "load_x": load_x, "store": store}

            def one_pass(t, have):
                so_far = {}

                for n in range(-1, STEPS):
                    stage = SCAN0 if n < S0 else SCAN1
                    if n in (0, S0):
                        if stage not in have:
                            stand_in(sp_, t, so_far, "sp", stage, ())
                        add_up(so_far, "sp", stage, ())
                    if n >= 0 and n % SHI == 0 and stage in have:
                        rep_dt(t, n // SHI)
                    for of, piece, args in pieces("sp", n):
                        if of in have:
                            do[piece](t, *args)
                        else:
                            stand_in(sp_, t, so_far, "sp", piece, args)
                        add_up(so_far, "sp", piece, args)

            passes(sp_, one_pass)
            for c in range(NC):
                sp_.wait_ge(s_store[c], at(s_store[c], len(PASSES), 0))
        @block.gpsimd
        def _(pool):
            for s in counted:
                pool.sem_inc(s, 1)
            pool.memset(ident[:], 0.0).then_inc(s_const, 1)
            pool.memset(rep[:], 0.0).then_inc(s_const, 1)
            pool.memset(state_sum[:], 0.0).then_inc(s_const, 1)
            pool.memset(eps8[:], EPS).then_inc(s_const, 1)
            pool.memset(neg_half[:], -0.5).then_inc(s_const, 1)
            pool.memset(neg_one[:], -1.0).then_inc(s_const, 1)
            pool.memset(hTa[:], 0.0).then_inc(s_const, 1)
            pool.memset(hTb[:], 0.0).then_inc(s_const, 1)
            pool.memset(hTc[:], 0.0).then_inc(s_const, 1)
            for e in range(NE):
                pool.memset(rev[:, e:e + 1], float(NE - e)).then_inc(s_const, 1)
            n = 9 + NE
            pool.wait_ge(s_const, n)
            pool.affine_select(out=ident[:], in_=ident[:], compare_op=ALU.not_equal, fill=1.0, base=0,
                               pattern=[[-1, P]], channel_multiplier=1).then_inc(s_const, 1)
            n += 1
            for k in range(KPH):
                v = rep[:, k, :].rearrange("p (a r) -> p a r", a=SLO)
                pool.affine_select(out=v, in_=v, compare_op=ALU.not_equal, fill=1.0, base=-R * k,
                                   pattern=[[0, SLO], [-1, R]], channel_multiplier=1).then_inc(s_const, 1)
            n += KPH
            for a in range(SLO):
                pool.wait_ge(s_const, n)
                pool.affine_select(out=state_sum[:], in_=state_sum[:], compare_op=ALU.not_equal, fill=1.0,
                                   base=-R * a, pattern=[[-1, R]], channel_multiplier=1).then_inc(s_const, 1)
                n += 1
            pool.wait_ge(s_load, N_LOAD)
            for k in range(TAPS0):
                pool.tensor_tensor(w_conv0[:, k, :], w_x_in0, conv0_bc[:, k, :], ALU.mult).then_inc(s_const, 1)
            for k in range(TAPS1):
                pool.tensor_tensor(w_conv1[:, k, :], w_x_in1, conv1_bc[:, k, :], ALU.mult).then_inc(s_const, 1)

            def w_gate(t):
                pool.wait_ge(s_gate[0], at(s_gate[0], t, 16))
                pool.wait_ge(s_out0, at(s_out0, t, 0))
                for m in range(H0):
                    ins = pool.tensor_tensor(w_out0g[:, m:m + 1, :], w_out0[:, m:m + 1, :], gate_a[:], ALU.mult)
                ins.then_inc(s_wg, 1)

            def rstd_(t, pos):
                pool.wait_ge(s_stats, at(s_stats, t, 2 * pos + 2))
                pool.wait_ge(s_xn, at(s_xn, t, NC * pos))
                pool.tensor_tensor(var_eps[:], mean_var[:, :, 1], eps8[:], ALU.add).then_inc(s_rstd, 1)
                pool.wait_ge(s_rstd, at(s_rstd, t, 4 * pos + 1))
                pool.tensor_tensor(rstd[:], var_eps[:], neg_half[:], ALU.pow).then_inc(s_rstd, 1)
                pool.wait_ge(s_rstd, at(s_rstd, t, 4 * pos + 2))
                pool.tensor_tensor(shift[:], mean_var[:, :, 0], rstd[:], ALU.mult).then_inc(s_rstd, 1)
                pool.wait_ge(s_rstd, at(s_rstd, t, 4 * pos + 3))
                pool.tensor_tensor(shift[:], shift[:], neg_one[:], ALU.mult).then_inc(s_rstd, 1)

            def dtx_0(t, c, m):
                i = NC + c * H0 + m
                v = slice(CH * c, CH * c + CH)
                pool.wait_ge(s_dt, at(s_dt, t, i + 1))
                pool.wait_ge(s_in_act, at(s_in_act, t, IN_0["xs", c, m] + 1))
                pool.tensor_tensor(dtx[:, m, v], dt[:, m, v], xs[:, m, v], ALU.mult).then_inc(s_dtx, 1)

            def dtx_1(t, c):
                v = slice(CH * c, CH * c + CH)
                pool.wait_ge(s_dt, at(s_dt, t, c + 1))
                pool.wait_ge(s_in_act, at(s_in_act, t, IN_1["xs", c] + 1))
                pool.tensor_tensor(dtx1[:, v], dt1[:, v], xs1[:, v], ALU.mult).then_inc(s_dtx, 1)

            def y_gated(t, i):
                c, m = i // H0, i % H0
                pool.wait_ge(s_y1, at(s_y1, t, Y0 + i + 1))
                pool.wait_ge(s_out0, at(s_out0, t, c))
                pool.wait_ge(s_o1T, at(s_o1T, t, 1))
                pool.tensor_tensor(y2[:, m, :], y1[:], zs[:, m, CH * c:CH * c + CH], ALU.mult).then_inc(s_y2, 1)

            def hws(t, c):
                n = c * EXP0 + NE
                pool.wait_ge(s_crow[n % 3], at(s_crow[n % 3], t, 16 * (n // 3 + 1)))
                pool.wait_ge(s_sh, at(s_sh, t, c + 1))
                pool.wait_ge(s_hwu, at(s_hwu, t, n - 1))
                pool.tensor_tensor(hw[:, NE % 2, :], shared[:], comb_rep[:, n % 3, :], ALU.mult).then_inc(s_hws, 1)

            def hw1(t, c, e):
                n = NC * EXP0 + NE * c + e
                pool.wait_ge(s_crow[n % 3], at(s_crow[n % 3], t, 16 * (n // 3 + 1)))
                pool.wait_ge(s_hwu, at(s_hwu, t, n - (e > 0)))
                pool.tensor_tensor(hw[:, e % 2, :], comb_rep[:, n % 3, :], hTb[:, 3 + CH * c:3 + CH * c + CH],
                                   ALU.mult).then_inc(s_hw1, 1)

            def moe_sum(t, f, c):
                pool.wait_ge(s_ffn, at(s_ffn, t, NC * f + c + 1))
                v = slice(TPC * c, TPC * c + TPC)
                if f == 0:
                    pool.wait_ge(s_xr2, at(s_xr2, t, 1))
                    pool.tensor_tensor(xr1[:, v, :], xr0[:, v, :], ffn[:], ALU.add).then_inc(s_xr1, 1)
                else:
                    pool.tensor_tensor(xr2[:, v, :], xr2[:, v, :], ffn[:], ALU.add).then_inc(s_xo, 1)

            do = {"w_gate": w_gate, "rstd": rstd_, "dtx0": dtx_0, "dtx1": dtx_1, "y_gated": y_gated, "hws": hws, "hw1": hw1,
                  "moe_sum": moe_sum}

            def one_pass(t, have):
                so_far = {}
                if SCAN0 not in have:
                    stand_in(pool, t, so_far, "pool", SCAN0, ())
                else:
                    pool.wait_ge(s_crep, at(s_crep, t, 0))
                for n in range(-1, STEPS):
                    if 0 <= n < S0 and SCAN0 in have:
                        c, i = n // (H0 * KPH * SHI), n % SHI
                        pool.wait_ge(s_scan, at(s_scan, t, n + 1))
                        pool.wait_ge(s_hsum, at(s_hsum, t, n - CR + 1) if n >= CR else at(s_hsum, t, 0))
                        pool.tensor_tensor(hc[:, n % CR, :], h[:, n % HR, :], c_rep[:, i, CH * c:CH * c + CH],
                                           ALU.mult).then_inc(s_hc, 1)
                    for of, piece, args in pieces("pool", n):
                        if of in have:
                            do[piece](t, *args)
                        else:
                            stand_in(pool, t, so_far, "pool", piece, args)
                        add_up(so_far, "pool", piece, args)

            pool.wait_ge(s_setup, N_SETUP)
            passes(pool, one_pass)
        @block.scalar
        def _(act):
            act.wait_ge(s_load, N_LOAD)
            act.activation(silu_c[:], c_t[:], ACT.Silu).then_inc(s_setup_act, 1)
            act.activation(neg_a0[:], neg_a0[:], ACT.Exp).then_inc(s_setup_act, 1)
            act.activation(neg_a1[:], neg_a1[:], ACT.Exp).then_inc(s_setup_act, 1)
            act.wait_ge(s_setup, N_SETUP)
            act.wait_ge(s_const, N_CONST)

            def norm(t, pos, c):
                src = {N_MOE0: xr0, N_MOE1: xr2, N_IN1: xr1, N_IN0: xa}[pos]
                act.wait_ge(s_rstd, at(s_rstd, t, 4 * pos + 4))
                act.wait_ge(s_xnT, at(s_xnT, t, NC * pos))
                for i in range(TPC * c, TPC * c + TPC):
                    ins = act.activation(xn[:, i, :], src[:, i, :], ACT.Identity, bias=shift[:, i:i + 1],
                                         scale=rstd[:, i:i + 1])
                ins.then_inc(s_xn, 1)

            def hT_(t, pos, c):
                lay, j, stage = NORM_MODS[pos]
                seq = seq_slice(t - LAG[stage])
                used, n = {N_MOE0: (s_in, IN_1["zs", NC - 1] + 1), N_MOE1: (s_hw1, 0), N_IN1: (s_h1, NC * (NE + 2)),
                           N_IN0: (s_in, 0)}[pos]
                there, free = at(s_xnT, t, NC * pos + c + 1), at(used, t, n)
                if not isinstance(t, int):
                    there, free = act.compute_val(there), act.compute_val(free)
                act.wait_ge(s_setup, N_SETUP)
                act.wait_ge(s_xnT, there)
                act.wait_ge(used, free)
                dst = {N_IN0: hTa, N_MOE1: hTb, N_IN1: hTc, N_MOE0: hTc}[pos]
                act.activation(dst[:, 3 + CH * c:3 + CH * c + CH], bank_of(("norm", pos, c)), ACT.Identity,
                               bias=mods[:, lay, j, seq], scale=mods[:, lay, j + 1, seq]).then_inc(s_hT, 1)

            def silu0(t, what, c, m):
                idx = IN_0[what, c, m]
                i = c * H0 + m
                act.wait_ge(s_in, at(s_in, t, idx + 1))
                if what == "xs":
                    act.wait_ge(s_y1, at(s_y1, t, Y0 + i + 1))
                else:
                    act.wait_ge(s_y2, at(s_y2, t, i + 1))
                dst = (xs if what == "xs" else zs)[:, m, CH * c:CH * c + CH]
                act.activation(dst, bank_of(("in", idx)), ACT.Silu, bias=conv_b0[:, m:m + 1] if what == "xs" else 0.0
                               ).then_inc(s_in_act, 1)

            def silu1(t, what, c):
                idx = IN_1[what, c]
                act.wait_ge(s_in, at(s_in, t, idx + 1))
                if what == "xs":
                    act.wait_ge(s_cpe, at(s_cpe, t, 0))
                    act.wait_ge(s_y1, at(s_y1, t, 1))
                else:
                    act.wait_ge(s_o1, at(s_o1, t, 1))
                dst = (xs1 if what == "xs" else zs1)[:, CH * c:CH * c + CH]
                act.activation(dst, bank_of(("in", idx)), ACT.Silu).then_inc(s_in_act, 1)

            def xdbl_0(t, c):
                act.wait_ge(s_xdbl, at(s_xdbl, t, XDBL_0[c] + 1))
                act.wait_ge(s_rows1, at(s_rows1, t, 16 if c else 0))
                act.copy(xdbl[:, CH * c:CH * c + CH], bank_of(("xdbl", XDBL_0[c]))[0:1 + 2 * NS, :]).then_inc(s_xdbl_act, 1)

            def xdbl_1(t, c):
                act.wait_ge(s_xdbl, at(s_xdbl, t, XDBL_1[c] + 1))
                act.wait_ge(s_rows0[c], at(s_rows0[c], t, 0 if c else 16))
                act.wait_ge(s_dtpre, at(s_dtpre, t, DTPRE_0[0, H0 - 1] + 1))
                act.copy(xdbl[0:NS, CH * c:CH * c + CH], bank_of(("xdbl", XDBL_1[c]))[0:NS, :]).then_inc(s_xdbl_act, 1)

            def cmat(t, c):
                act.wait_ge(s_cpe, at(s_cpe, t, c + 1))
                act.wait_ge(s_cy, at(s_cy, t, 1))
                act.copy(c_mat[:, CH * c:CH * c + CH], bank_of(("cmat", c))).then_inc(s_cmat, 1)

            def relu_abs(t, i, relu_to, abs_to, bias):
                act.wait_ge(s_dtpre, at(s_dtpre, t, i + 1))
                v = bank_of(("dtpre", i))
                act.activation(relu_to, v, ACT.Relu, bias=bias).then_inc(s_pre, 1)
                act.activation(abs_to, v, ACT.Abs, bias=bias).then_inc(s_pre, 1)

            def relu_abs0(t, c, m):
                act.wait_ge(s_dtxrep, at(s_dtxrep, t, KS0 // NC * (c + 1)))
                for s in s_dtrep:
                    act.wait_ge(s, at(s, t, KS0 // NC * (c + 1) // 2 * SLO * 16))
                v = slice(CH * c, CH * c + CH)
                relu_abs(t, DTPRE_0[c, m], dtx[:, m, v], dt[:, m, v], b_dt0[:, m:m + 1])

            def relu_abs1(t, c):
                act.wait_ge(s_dtxrep, at(s_dtxrep, t, 0))
                for s in s_dtrep:
                    act.wait_ge(s, at(s, t, 0))
                v = slice(CH * c, CH * c + CH)
                relu_abs(t, DTPRE_1[c], dtx1[:, v], dt1[:, v], b_dt1[:, 0:1])

            def soft(t, v, last, before):
                act.wait_ge(s_pre, at(s_pre, t, 2 * (last + 1)))
                act.activation(v, v, ACT.Exp, scale=-1.0).then_inc(s_soft, 1)
                act.wait_ge(s_soft, at(s_soft, t, before + 1))
                act.activation(v, v, ACT.Ln, bias=1.0).then_inc(s_soft, 1)

            def soft0(t, c):
                soft(t, dt[:, :, CH * c:CH * c + CH], DTPRE_0[c, H0 - 1], 2 + 2 * c)

            def soft1(t):
                soft(t, dt1[:], DTPRE_1[NC - 1], 0)

            def ex_(t, f):
                act.wait_ge(s_route, at(s_route, t, ROUTE_FIRST[f] + (3 if f else 2)))
                act.activation(ex[:], lg[:], ACT.Exp).then_inc(s_ex, 1)
                if f == 0:
                    act.wait_ge(s_route, at(s_route, t, ROUTE_FIRST[0] + 3))
                    act.activation(sg[:], sg[:], ACT.Exp, scale=-1.0).then_inc(s_sg, 1)

            def combT_(t, f, c):
                act.wait_ge(s_combT, at(s_combT, t, NC * ROUTE_ORDER[f] + c + 1))
                for s in s_comb_row[1 - f]:
                    act.wait_ge(s, at(s, t, 0 if f else 16))
                act.wait_ge(s_hwu, at(s_hwu, t, 0 if f else NC * EXP0 + NE * (NC - 1) + 1))
                k = NE if f else NE + 1
                act.copy(combT[0:k, CH * c:CH * c + CH], bank_of(("combT", f, c))[0:k, :]).then_inc(s_combT_act, 1)

            def silu_h(t, c, e):
                act.wait_ge(s_h1, at(s_h1, t, c * (NE + 2) + e + 1))
                v = bank_of(("h1", c, e))
                if e == NE:
                    act.wait_ge(s_sh, at(s_sh, t, c))
                act.activation(v if e < NE else gate_act[:], v, ACT.Silu).then_inc(s_h1a, 1)

            do = {"norm": norm, "hT": hT_, "silu0": silu0, "silu1": silu1, "xdbl0": xdbl_0, "xdbl1": xdbl_1,
                  "cmat": cmat, "relu_abs0": relu_abs0, "relu_abs1": relu_abs1, "soft0": soft0, "soft1": soft1, "ex": ex_,
                  "combT": combT_, "silu_h": silu_h}

            def one_pass(t, have):
                so_far = {}
                for n in range(-1, STEPS):
                    stage, neg_a = (SCAN0, neg_a0) if n < S0 else (SCAN1, neg_a1)
                    if n in (0, S0):
                        if stage not in have:
                            stand_in(act, t, so_far, "act", stage, ())
                        add_up(so_far, "act", stage, ())
                    if n >= 0 and stage in have:
                        kn = KPH if n >= S0 else H0 * KPH
                        j, i = n // SHI, n % SHI
                        k = (j - (KS0 if n >= S0 else 0)) % kn
                        if i == 0:
                            act.wait_ge(s_dtrep[j % 2], at(s_dtrep[j % 2], t, (j // 2 + 1) * SLO * 16))
                        act.wait_ge(s_scan, at(s_scan, t, max(n - DR + 1, 0)))
                        act.activation(da[:, n % DR, :], dt_rep[:, j % 2, :], ACT.Exp, scale=neg_a[:, k, i:i + 1]
                                       ).then_inc(s_da, 1)
                    for of, piece, args in pieces("act", n):
                        if of in have:
                            do[piece](t, *args)
                        else:
                            stand_in(act, t, so_far, "act", piece, args)
                        add_up(so_far, "act", piece, args)

            passes(act, one_pass)
        @block.vector
        def _(dve):
            dve.wait_ge(s_setup_act, 3)
            dve.wait_ge(s_const, N_CONST)
            dve.tensor_scalar(neg_a0[:], neg_a0[:], -1.0, None, ALU.mult).then_inc(s_setup, 1)
            dve.tensor_scalar(neg_a1[:], neg_a1[:], -1.0, None, ALU.mult).then_inc(s_setup, 1)
            n = 2
            dve.wait_ge(s_setup_pe, 3)
            for lay in range(2):
                v = mods[:, lay, :, :].rearrange("p j b -> p (j b)")
                dve.tensor_copy(v, mm[:, lay, 0:6 * NB]).then_inc(s_setup, 1)
            dve.tensor_copy(w_dtx1[:], mm[:, 2, 0:D]).then_inc(s_setup, 1)
            dve.tensor_copy(w_cx1[:], mm[:, 2, D:2 * D]).then_inc(s_setup, 1)
            n += 4
            dve.wait_ge(s_setup, n)
            for lay in range(2):
                for j in (1, 4):
                    dve.tensor_scalar(mods[:, lay, j, :], mods[:, lay, j, :], 1.0, None, ALU.add).then_inc(s_setup, 1)
                    n += 1

            def gated(v, tmp):
                nonlocal n
                dve.wait_ge(s_setup, n)
                dve.tensor_scalar(tmp, v, 0.0, 2.0, ALU.is_ge, ALU.mult).then_inc(s_setup, 1)
                dve.wait_ge(s_setup, n + 1)
                dve.scalar_tensor_tensor(out=v, in0=tmp, scalar=-1.0, in1=v, op0=ALU.add, op1=ALU.mult).then_inc(s_setup, 1)
                dve.wait_ge(s_setup, n + 2)
                dve.tensor_scalar(v, v, GATE_MIN, None, ALU.max).then_inc(s_setup, 1)
                dve.wait_ge(s_setup, n + 3)
                dve.scalar_tensor_tensor(out=v, in0=tmp, scalar=-1.0, in1=v, op0=ALU.add, op1=ALU.mult).then_inc(s_setup, 1)
                n += 4

            gated(mods[:, 1, 2, :], gate_tmp[:, 0:NB])
            for g in range(3):
                for q in range(2):
                    dve.wait_ge(s_setup_pe, 4 + 2 * g + q)
                    dve.tensor_copy(gates[:, g, NB // 2 * q:NB // 2 * q + NB // 2, :].rearrange("p b d -> p (b d)"),
                                    mm[:, q, :]).then_inc(s_setup, 1)
                    n += 1
            for g in range(3):
                gated(gates[:, g, :, :].rearrange("p b d -> p (b d)"), gate_tmp)
            assert n == N_SETUP

            def stats_(t, pos):
                src = {N_MOE0: xr0, N_MOE1: xr2, N_IN1: xr1, N_IN0: xa}[pos]
                s_src, n_src = {N_MOE0: (s_xr0, NC), N_MOE1: (s_xr2, 1), N_IN1: (s_xr1, NC), N_IN0: (s_x, 16)}[pos]
                dve.wait_ge(s_src, at(s_src, t, n_src))
                dve.wait_ge(s_xn, at(s_xn, t, NC * pos))
                for i in range(TILES):
                    ins = dve.bn_stats(stats[:, i, :], src[:, i, :])
                ins.then_inc(s_stats, 1)
                stats_there = at(s_stats, t, 2 * pos + 1)
                if not isinstance(t, int):
                    stats_there = dve.compute_val(stats_there)
                dve.wait_ge(s_setup, N_SETUP)
                dve.wait_ge(s_stats, stats_there)
                for i in range(TILES):
                    ins = dve.bn_aggr(mean_var[:, i, :], stats[:, i, :])
                ins.then_inc(s_stats, 1)

            def step0(t, c, m):
                v = slice(CH * c, CH * c + CH)
                dve.wait_ge(s_soft, at(s_soft, t, 4 + 2 * c))
                dve.tensor_tensor(dt[:, m, v], dt[:, m, v], dtx[:, m, v], ALU.add).then_inc(s_dt, 1)

            def step1(t, c):
                v = slice(CH * c, CH * c + CH)
                dve.wait_ge(s_soft, at(s_soft, t, 2))
                dve.scalar_tensor_tensor(out=dt1[:, v], in0=dt1[:, v], scalar=EPS, in1=dtx1[:, v], op0=ALU.add,
                                         op1=ALU.add).then_inc(s_dt, 1)

            def hw0(t, c, e):
                n = c * EXP0 + e
                dve.wait_ge(s_h1a, at(s_h1a, t, n + 1))
                dve.wait_ge(s_crow[n % 3], at(s_crow[n % 3], t, 16 * (n // 3 + 1)))
                dve.wait_ge(s_hwu, at(s_hwu, t, n - (e > 0)))
                dve.tensor_tensor(hw[:, e % 2, :], bank_of(("h1", c, e)), comb_rep[:, n % 3, :], ALU.mult
                                  ).then_inc(s_hw, 1)

            def shared_(t, c):
                dve.wait_ge(s_h1, at(s_h1, t, (NE + 2) * (c + 1)))
                dve.wait_ge(s_h1a, at(s_h1a, t, EXP0 * (c + 1)))
                dve.wait_ge(s_hws, at(s_hws, t, c))
                dve.tensor_tensor(shared[:], bank_of(("h1", c, NE + 1)), gate_act[:], ALU.mult).then_inc(s_sh, 1)

            def scale(t, f, c):
                dve.wait_ge(s_hwu, at(s_hwu, t, NC * EXP0 + NE * (c + 1) if f else EXP0 * (c + 1)))
                dve.wait_ge(s_gate[1 + f], at(s_gate[1 + f], t, 16))
                dve.wait_ge(s_xr1, at(s_xr1, t, NC if f else c))
                dve.wait_ge(s_xo, at(s_xo, t, c if f else 0))
                dve.tensor_tensor(ffn[:], bank_of(("acc", f, c)).rearrange("p (i d) -> p i d", i=TPC),
                                  gate_b[:, f:f + 1, :].to_broadcast([P, TPC, D]), ALU.mult).then_inc(s_ffn, 1)

            def y_sum0(t, i):
                c, m = i // H0, i % H0
                dve.wait_ge(s_hsum, at(s_hsum, t, HALF * (i + 1)))
                dve.wait_ge(s_y2, at(s_y2, t, i))
                dve.wait_ge(s_out1, at(s_out1, t, 1))
                dve.scalar_tensor_tensor(out=y1[:], in0=xs[:, m, CH * c:CH * c + CH], scalar=d0[:, m:m + 1],
                                         in1=ysum[:], op0=ALU.mult, op1=ALU.add).then_inc(s_y1, 1)

            def residual0(t, c):
                dve.wait_ge(s_out0, at(s_out0, t, c + 1))
                dve.wait_ge(s_again[c], at(s_again[c], t, 16))
                v = slice(TPC * c, TPC * c + TPC)
                dve.tensor_tensor(xr0[:, v, :], xr0[:, v, :],
                                  bank_of(("out0", c)).rearrange("p (i d) -> p i d", i=TPC), ALU.add
                                  ).then_inc(s_xr0, 1)

            def y_sum1(t, c):
                tail, k = c == NC - 1, END1[c]
                dve.wait_ge(s_hsum, at(s_hsum, t, 0 if tail else S0 + HALF * (c + 1)))
                dve.wait_ge(s_cmat, at(s_cmat, t, 0 if tail else c + 1))
                dve.tensor_tensor(ysum[:], ysum[:], c_mat[:, CH * c:CH * c + CH], ALU.mult).then_inc(s_cy, 1)
                dve.wait_ge(s_cy, at(s_cy, t, k + 1))
                dve.wait_ge(s_out1, at(s_out1, t, k))
                dve.wait_ge(s_y2, at(s_y2, t, 0 if tail else NC * H0))
                dve.scalar_tensor_tensor(out=y1[:], in0=xs1[:, CH * c:CH * c + CH], scalar=d1[:, 0:1],
                                         in1=ysum[:], op0=ALU.mult, op1=ALU.add).then_inc(s_y1, 1)

            def gate1(t, c):
                tail, k = c == NC - 1, END1[c]
                dve.wait_ge(s_out1, at(s_out1, t, k + 1))
                dve.wait_ge(s_out0, at(s_out0, t, 0 if tail else NC))
                dve.wait_ge(s_o1T, at(s_o1T, t, k))
                dve.scalar_tensor_tensor(out=y2[:, 0, :], in0=bank_of(("out1", c)),
                                         scalar=mods[:, 1, 2, seq_slice(t - LAG[TAIL1 if tail else SCAN1])],
                                         in1=zs1[:, CH * c:CH * c + CH], op0=ALU.mult, op1=ALU.mult
                                         ).then_inc(s_o1, 1)

            def residual1(t, c):
                tail, k = c == NC - 1, END1[c]
                dve.wait_ge(s_o1T, at(s_o1T, t, k + 1))
                dve.wait_ge(s_store[c], at(s_store[c], t, 0 if tail else 16))
                v = slice(TPC * c, TPC * c + TPC)
                dve.tensor_tensor(xr2[:, v, :], xr1[:, v, :], bank_of(("o1T", c)).rearrange("p (i d) -> p i d", i=TPC),
                                  ALU.add).then_inc(s_xr2, 1)

            route_step = [0]

            def done(ins):
                ins.then_inc(s_route, 1)
                route_step[0] += 1

            def need(t):
                dve.wait_ge(s_route, at(s_route, t, route_step[0]))

            def bc(v):
                return v.unsqueeze(2).to_broadcast([P, TILES, NE])

            def route_max(t, f):
                route_step[0] = ROUTE_FIRST[f]
                width = NE if f else NE + 1
                v = bank_of(("lg", f))[:, 0:TILES * width].rearrange("p (i e) -> p i e", i=TILES)
                dve.wait_ge(s_lg, at(s_lg, t, ROUTE_ORDER[f] + 1))
                need(t)
                if f == 0:
                    done(dve.tensor_reduce(mx[:], v[:, :, 0:NE], AX.X, ALU.max))
                    need(t)
                    done(dve.tensor_tensor(lg[:], v[:, :, 0:NE], bc(mx[:]), ALU.subtract))
                    done(dve.tensor_copy(sg[:], v[:, :, NE]))
                else:
                    done(dve.tensor_tensor(lg[:], v, gate_b1[:].unsqueeze(1).to_broadcast([P, TILES, NE]), ALU.add))
                    need(t)
                    done(dve.tensor_reduce(mx[:], lg[:], AX.X, ALU.max))
                    need(t)
                    done(dve.tensor_tensor(lg[:], lg[:], bc(mx[:]), ALU.subtract))

            def largest(t, dst):
                need(t)
                done(dve.tensor_reduce(mx[:], ex[:], AX.X, ALU.max))
                need(t)
                done(dve.tensor_tensor(key[:], ex[:], bc(mx[:]), ALU.is_equal))
                need(t)
                done(dve.tensor_tensor(key[:], key[:], rev[:].unsqueeze(1).to_broadcast([P, TILES, NE]), ALU.mult))
                need(t)
                done(dve.tensor_reduce(mx[:], key[:], AX.X, ALU.max))
                need(t)
                done(dve.tensor_tensor(dst[:], key[:], bc(mx[:]), ALU.is_equal))

            def route_first(t, f):
                route_step[0] = ROUTE_FIRST[f] + 3
                need(t)
                dve.wait_ge(s_ex, at(s_ex, t, ROUTE_ORDER[f] + 1))
                done(dve.tensor_reduce(mx[:], ex[:], AX.X, ALU.add))
                need(t)
                done(dve.reciprocal(mx[:], mx[:]))
                need(t)
                done(dve.tensor_tensor(pr[:], ex[:], bc(mx[:]), ALU.mult))
                largest(t, pick1)

            def route_second(t, f):
                route_step[0] = ROUTE_FIRST[f] + 11
                comb = comb1 if f else comb0
                need(t)
                done(dve.scalar_tensor_tensor(out=ex[:], in0=pick1[:], scalar=-4.0, in1=ex[:], op0=ALU.mult, op1=ALU.add))
                largest(t, pick2)
                need(t)
                done(dve.tensor_tensor(pick1[:], pick1[:], pick2[:], ALU.add))
                need(t)
                dve.wait_ge(s_combT, at(s_combT, t, 0))
                done(dve.tensor_tensor(comb[:, :, 0:NE], pick1[:], pr[:], ALU.mult))
                if f == 0:
                    dve.wait_ge(s_sg, at(s_sg, t, 1))
                    done(dve.tensor_scalar(sg[:], sg[:], 1.0, None, ALU.add))
                    need(t)
                    done(dve.reciprocal(comb[:, :, NE], sg[:]))
                assert route_step[0] == ROUTE_FIRST[f] + N_ROUTE[f], route_step

            do = {"stats": stats_, "step0": step0, "step1": step1, "hw0": hw0, "shared": shared_,
                  "scale": scale, "y_sum0": y_sum0, "residual0": residual0, "y_sum1": y_sum1, "gate1": gate1,
                  "residual1": residual1, "route_max": route_max, "route_first": route_first,
                  "route_second": route_second}

            def product(t, n):
                j, i = n // SHI, n % SHI
                c = (n - S0) // HALF if n >= S0 else n // (H0 * HALF)
                if i == 0:
                    dve.wait_ge(s_dtxrep, at(s_dtxrep, t, j + 1))
                    if n in (0, S0 // NC):
                        dve.wait_ge(s_brep[0][c], at(s_brep[0][c], t, 16 * SLO * c))
                    elif n in (S0, S0 + HALF):
                        dve.wait_ge(s_brep[1][c], at(s_brep[1][c], t, 16 * SLO))
                dve.wait_ge(s_scan, at(s_scan, t, max(n - 1, 0)))
                dve.tensor_tensor(u[:, n % 2, :], dtx_rep[:, j % 2, :], b_rep[:, c, i, :], ALU.mult).then_inc(s_u, 1)

            def scan(t, n):
                lay1 = n >= S0
                c = (n - S0) // HALF if lay1 else n // (H0 * HALF)
                j, i = n // SHI, n % SHI
                k = (j - (KS0 if lay1 else 0)) % (KPH if lay1 else H0 * KPH)
                dve.wait_ge(s_u, at(s_u, t, n + 1))
                dve.wait_ge(s_da, at(s_da, t, n + 1))
                dve.wait_ge(s_hc, at(s_hc, t, min(max(n - HR + 1, 0), S0)))
                dve.wait_ge(s_hsum, at(s_hsum, t, n - HR + 1 if lay1 else 0))
                first = 0 if n < S0 else S0
                if c == 0:
                    ends = (S0 // NC // SHI if lay1 else 0) + (n - first) // SHI
                else:
                    ends = S0 // NC // SHI + (HALF // SHI if lay1 else 0)
                dve.wait_ge(s_carry, at(s_carry, t, ends))
                dve.tensor_tensor_scan(h[:, n % HR, :], da[:, n % DR, :], u[:, n % 2, :],
                                       0.0 if c == 0 else carry[:, k, i:i + 1], ALU.mult, ALU.add
                                       ).then_inc(s_scan, 1)
                if c == 0 and i == SHI - 1:
                    dve.wait_ge(s_scan, at(s_scan, t, n + 1))
                    dve.tensor_copy(carry[:, k, :], h[:, :, CH - 1]).then_inc(s_carry, 1)

            def one_pass(t, have):
                so_far = {}
                if SCAN0 in have:
                    product(t, 0)
                for n in range(-1, STEPS):
                    stage = SCAN0 if n < S0 else SCAN1
                    if n in (0, S0):
                        if stage in have and n:
                            product(t, n)
                        elif stage not in have:
                            stand_in(dve, t, so_far, "dve", stage, ())
                        add_up(so_far, "dve", stage, ())
                    if n >= 0 and stage in have:
                        if n + 1 not in (S0, STEPS):
                            product(t, n + 1)
                        scan(t, n)
                    for of, piece, args in pieces("dve", n):
                        if of in have:
                            do[piece](t, *args)
                        else:
                            stand_in(dve, t, so_far, "dve", piece, args)
                        add_up(so_far, "dve", piece, args)

            passes(dve, one_pass)
        @block.tensor
        def _(pe):
            pe.wait_ge(s_load, N_LOAD)
            pe.wait_ge(s_setup_act, 1)
            for lay in range(2):
                for j in range(6):
                    ins = pe.matmul(mm[:, lay, NB * j:NB * j + NB], w_mod[:, lay, D * j:D * j + D], silu_c[:, lay, :],
                                    start=True, stop=True)
                ins.then_inc(s_setup_pe, 1)
            pe.matmul(mm[:, 2, 0:D], w_x1dt, w_dt1, start=True, stop=True)
            pe.matmul(mm[:, 2, D:2 * D], w_x1c, w_c1, start=True, stop=True).then_inc(s_setup_pe, 1)
            for g, (lay, j) in enumerate(((0, 2), (0, 5), (1, 5))):
                for q in range(2):
                    pe.wait_ge(s_setup, N_MODS + 2 * (g - 1) + q + 1 if g else N_COPIED)
                    for i in range(NB // 2):
                        bb = NB // 2 * q + i
                        ins = pe.matmul(mm[:, q, D * i:D * i + D], silu_c[:, lay, bb:bb + 1].to_broadcast([P, P]),
                                        w_mod[:, lay, D * j:D * j + D], start=True, stop=True)
                    ins.then_inc(s_setup_pe, 1)
            pe.wait_ge(s_setup, N_SETUP)
            pe.wait_ge(s_const, N_CONST)

            def xnT(t, pos, c):
                pe.wait_ge(s_xn, at(s_xn, t, NC * pos + c + 1))
                v = claim(pe, t, ("norm", pos, c))
                for i in range(TPC):
                    ins = pe.transpose(v[:, P * i:P * i + P], xn[:, TPC * c + i, :], ident[:])
                ins.then_inc(s_xnT, 1)

            def conv(v, w_taps, taps, first, c, m, hT):
                for k in range(taps):
                    o = 3 + CH * c + k - first
                    ins = pe.matmul(v, w_taps[:, k, P * m:P * m + P], hT[:, o:o + CH], start=(k == 0), stop=(k == taps - 1))
                return ins

            def in0(t, what, c, m):
                pe.wait_ge(s_hT, at(s_hT, t, NC * N_IN0 + NC))
                v = claim(pe, t, ("in", IN_0[what, c, m]))
                if what == "xs":
                    ins = conv(v, w_conv0, TAPS0, TAPS0 - 1, c, m, hTa)
                else:
                    ins = pe.matmul(v, w_z0[:, P * m:P * m + P], hTa[:, 3 + CH * c:3 + CH * c + CH],
                                    start=True, stop=True)
                ins.then_inc(s_in, 1)

            def in1(t, what, c):
                pe.wait_ge(s_hT, at(s_hT, t, NC * N_IN1 + NC))
                v = claim(pe, t, ("in", IN_1[what, c]))
                if what == "xs":
                    ins = conv(v, w_conv1, TAPS1, TAPS1 // 2, c, 0, hTc)
                else:
                    ins = pe.matmul(v, w_z1[:], hTc[:, 3 + CH * c:3 + CH * c + CH], start=True, stop=True)
                ins.then_inc(s_in, 1)

            def xdbl_0(t, c):
                pe.wait_ge(s_in_act, at(s_in_act, t, IN_0["xs", c, H0 - 1] + 1))
                v = claim(pe, t, ("xdbl", XDBL_0[c]))
                for m in range(H0):
                    ins = pe.matmul(v[0:1 + 2 * NS, :], w_x0[:, m, :], xs[:, m, CH * c:CH * c + CH],
                                    start=(m == 0), stop=(m == H0 - 1))
                ins.then_inc(s_xdbl, 1)

            def xdbl_1(t, c):
                pe.wait_ge(s_in_act, at(s_in_act, t, IN_1["xs", c] + 1))
                v = claim(pe, t, ("xdbl", XDBL_1[c]))
                pe.matmul(v[0:NS, :], w_x1b[:], xs1[:, CH * c:CH * c + CH], start=True, stop=True).then_inc(s_xdbl, 1)

            def cmat(t, c):
                v = claim(pe, t, ("cmat", c))
                pe.matmul(v, w_cx1[:], xs1[:, CH * c:CH * c + CH], start=True, stop=True).then_inc(s_cpe, 1)

            def dtpre0(t, c, m):
                pe.wait_ge(s_xdbl_act, at(s_xdbl_act, t, XDBL_0[c] + 1))
                v = claim(pe, t, ("dtpre", DTPRE_0[c, m]))
                pe.matmul(v, w_dt0[0:1, P * m:P * m + P], xdbl[0:1, CH * c:CH * c + CH],
                          start=True, stop=True).then_inc(s_dtpre, 1)

            def dtpre1(t, c):
                pe.wait_ge(s_in_act, at(s_in_act, t, IN_1["xs", c] + 1))
                v = claim(pe, t, ("dtpre", DTPRE_1[c]))
                pe.matmul(v, w_dtx1[:], xs1[:, CH * c:CH * c + CH], start=True, stop=True).then_inc(s_dtpre, 1)

            def lg_(t, f):
                hT, wr, width = (hTb, gate_w1, NE) if f else (hTc, router, NE + 1)
                pe.wait_ge(s_hT, at(s_hT, t, NC * (N_MOE1 if f else N_MOE0) + NC))
                v = claim(pe, t, ("lg", f))
                for i in range(TILES):
                    ins = pe.matmul(v[:, width * i:width * (i + 1)], hT[:, 3 + P * i:3 + P * i + P], wr[:],
                                    start=True, stop=True)
                ins.then_inc(s_lg, 1)

            def combT_(t, f, c):
                comb, width = (comb1, NE) if f else (comb0, NE + 1)
                pe.wait_ge(s_route, at(s_route, t, ROUTE_FIRST[f] + N_ROUTE[f]))
                v = claim(pe, t, ("combT", f, c))
                for i in range(TPC):
                    ins = pe.transpose(v[0:width, P * i:P * i + P], comb[:, TPC * c + i, 0:width], ident[:])
                ins.then_inc(s_combT, 1)

            def h1_(t, c, e):
                v = claim(pe, t, ("h1", c, e))
                pe.matmul(v, w1[:, e, :], hTc[:, 3 + CH * c:3 + CH * c + CH], start=True, stop=True).then_inc(s_h1, 1)

            def second0(t, c, e):
                acc = claim(pe, t, ("acc", 0, c)) if e == 0 else bank_of(("acc", 0, c))
                if e < NE:
                    pe.wait_ge(s_hw, at(s_hw, t, NE * c + e + 1))
                else:
                    pe.wait_ge(s_hws, at(s_hws, t, c + 1))
                for i in range(TPC):
                    ins = pe.matmul(acc[:, D * i:D * i + D], hw[:, e % 2, P * i:P * i + P], w2[:, e, :],
                                    start=(e == 0 and i == 0), stop=(e == NE), skip_group_check=True)
                ins.then_inc(s_hwu, 1)

            def bias1(t, c):
                acc = claim(pe, t, ("acc", 1, c))
                pe.wait_ge(s_combT_act, at(s_combT_act, t, c + 1))
                for i in range(TPC):
                    pe.matmul(acc[:, D * i:D * i + D], combT[0:NE, CH * c + P * i:CH * c + P * i + P], b_e1[:],
                              start=(i == 0), stop=False, skip_group_check=True)

            def second1(t, c, e):
                acc = bank_of(("acc", 1, c))
                pe.wait_ge(s_hw1, at(s_hw1, t, NE * c + e + 1))
                for i in range(TPC):
                    ins = pe.matmul(acc[:, D * i:D * i + D], hw[:, e % 2, P * i:P * i + P], w_e1[:, e, :],
                                    start=False, stop=(e == NE - 1), skip_group_check=True)
                ins.then_inc(s_hwu, 1)

            def out0(t, c):
                pe.wait_ge(s_wg, at(s_wg, t, 1))
                pe.wait_ge(s_y2, at(s_y2, t, H0 * (c + 1)))
                v = claim(pe, t, ("out0", c))
                for i in range(TPC):
                    for m in range(H0):
                        ins = pe.matmul(v[:, D * i:D * i + D], y2[:, m, P * i:P * i + P], w_out0g[:, m, :],
                                        start=(m == 0), stop=(m == H0 - 1))
                ins.then_inc(s_out0, 1)

            def out1(t, c):
                pe.wait_ge(s_y1, at(s_y1, t, 1 if c == NC - 1 else Y0 + NC * H0 + c + 1))
                v = claim(pe, t, ("out1", c))
                pe.matmul(v, w_out1[:], y1[:], start=True, stop=True).then_inc(s_out1, 1)

            def out1_T(t, c):
                pe.wait_ge(s_o1, at(s_o1, t, END1[c] + 1))
                v = claim(pe, t, ("o1T", c))
                for i in range(TPC):
                    ins = pe.transpose(v[:, D * i:D * i + D], y2[:, 0, P * i:P * i + P], ident[:])
                ins.then_inc(s_o1T, 1)

            do = {"xnT": xnT, "in0": in0, "in1": in1, "xdbl0": xdbl_0, "xdbl1": xdbl_1, "cmat": cmat, "dtpre0": dtpre0,
                  "dtpre1": dtpre1, "lg": lg_, "combT": combT_, "h1": h1_, "second0": second0, "bias1": bias1,
                  "second1": second1, "out0": out0, "out1": out1, "out1_T": out1_T}

            def replicate(t, j):
                lay1 = j >= KS0
                kn = KPH if lay1 else H0 * KPH
                c, k = (j - (KS0 if lay1 else 0)) // kn, (j - (KS0 if lay1 else 0)) % kn
                m = k // KPH
                pe.wait_ge(s_dtx, at(s_dtx, t, c + 1) if lay1 else at(s_dtx, t - 1, NC + c * H0 + m + 1))
                pe.wait_ge(s_u, at(s_u, t, SHI * max(j - 1, 0)))
                src = dtx1 if lay1 else dtx[:, m, :]
                pe.matmul(dtx_rep[:, j % 2, :], rep[:, k % KPH, :], src[:, CH * c:CH * c + CH],
                          start=True, stop=True).then_inc(s_dtxrep, 1)

            def state_sums(t, n):
                j, i = n // SHI, n % SHI
                kk, half = j % KPH, j // KPH
                if n < S0:
                    pe.wait_ge(s_hc, at(s_hc, t, n + 1))
                    src = hc[:, n % CR, :]
                else:
                    pe.wait_ge(s_scan, at(s_scan, t, n + 1))
                    src = h[:, n % HR, :]
                if kk == 0 and i == 0:
                    pe.wait_ge(s_y1, at(s_y1, t, half + 1))
                pe.matmul(ysum[R * kk:R * kk + R, :], state_sum[:], src, start=(i == 0), stop=(i == SHI - 1)
                          ).then_inc(s_hsum, 1)

            def run_pieces(t, have, so_far, n):
                for of, piece, args in pieces("pe", n):
                    if of in have:
                        do[piece](t, *args)
                    else:
                        if bank_use(piece, args):
                            claim(pe, t, bank_use(piece, args)[0])
                        stand_in(pe, t, so_far, "pe", piece, args)
                    add_up(so_far, "pe", piece, args)

            def one_pass(t, have):
                so_far = {}
                if SCAN0 in have:
                    replicate(t, 0)
                    replicate(t, 1)
                for n in range(-1, STEPS):
                    stage = SCAN0 if n < S0 else SCAN1
                    if n in (0, S0):
                        if stage in have and n:
                            replicate(t, n // SHI)
                            replicate(t, n // SHI + 1)
                        elif stage not in have:
                            stand_in(pe, t, so_far, "pe", stage, ())
                        add_up(so_far, "pe", stage, ())
                    early = n % HALF == 0
                    if early:
                        run_pieces(t, have, so_far, n)
                    if n >= 0 and stage in have:
                        state_sums(t, n)
                        if n % SHI == SHI // 2 and n // SHI + 2 not in (KS0, KS0 + 1, KS0 + KS1, KS0 + KS1 + 1):
                            replicate(t, n // SHI + 2)
                    if not early:
                        run_pieces(t, have, so_far, n)

            passes(pe, one_pass)


_NAMES = ["w_in0", "conv0", "conv_b0", "w_x0", "w_dt0", "b_dt0", "a_log0", "d0", "w_out0", "router", "w1", "w2", "w_in1",
          "conv1", "w_x1dt", "w_x1b", "w_x1c", "w_dt1", "w_c1", "b_dt1", "a_log1", "d1", "w_out1", "gate_w1", "gate_b1",
          "w_e1", "b_e1", "c_t", "w_mod"]


def kernel(**inputs):
    import numpy as _np
    import concourse.bacc as _bacc
    from concourse.bass_utils import run_bass_kernel_spmd as _run

    g = {k: _np.asarray(v) for k, v in inputs.items()}

    def halves(a):
        return a.reshape((H0, P) + a.shape[1:]).swapaxes(0, 1)

    def blocks(a):
        return a.reshape(-1, R, SLO, SHI).transpose(2, 1, 0, 3).reshape(P, -1, SHI)

    wx1 = g["L1_attn_W_x"]
    sgu = g["L0_ffn_shared_gate_up"].reshape(D, 2, P)
    laid = {
        "w_in0": g["L0_attn_W_in"],
        "conv0": g["L0_attn_conv_w"].reshape(DI, TAPS0).T,
        "conv_b0": g["L0_attn_conv_b"].reshape(H0, P).T,
        "w_x0": halves(g["L0_attn_W_x"]),
        "w_dt0": g["L0_attn_W_dt"],
        "b_dt0": g["L0_attn_b_dt"].reshape(H0, P).T,
        "a_log0": blocks(g["L0_attn_A_log"]),
        "d0": g["L0_attn_D_param"].reshape(H0, P).T,
        "w_out0": halves(g["L0_attn_W_out"]),
        "router": _np.concatenate([g["L0_ffn_router_w"], g["L0_ffn_shared_gate_w"]], axis=1),
        "w1": _np.concatenate([g["L0_ffn_w1"].transpose(1, 0, 2), sgu], axis=1),
        "w2": _np.concatenate([g["L0_ffn_w2"].transpose(1, 0, 2), g["L0_ffn_shared_down"][:, None, :]], axis=1),
        "w_in1": g["L1_attn_W_in"].T,
        "conv1": g["L1_attn_conv_w"].T,
        "w_x1dt": wx1[:R1],
        "w_x1b": wx1[R1:R1 + NS].T,
        "w_x1c": wx1[R1 + NS:],
        "w_dt1": g["L1_attn_W_dt"].T,
        "w_c1": g["L1_attn_W_C"].T,
        "b_dt1": g["L1_attn_b_dt"].reshape(P, 1),
        "a_log1": blocks(g["L1_attn_A_log"]),
        "d1": g["L1_attn_D_param"].reshape(P, 1),
        "w_out1": g["L1_attn_W_out"].T,
        "gate_w1": g["L1_ffn_gate_w"].T,
        "gate_b1": g["L1_ffn_gate_b"],
        "w_e1": g["L1_ffn_expert_w"].transpose(2, 0, 1),
        "b_e1": g["L1_ffn_expert_b"],
        "c_t": _np.stack([g["L0_c"].T, g["L1_c"].T], axis=1),
        "w_mod": _np.stack([g["L0_wmod"], g["L1_wmod"]], axis=1),
    }
    nc = _bacc.Bacc("TRN2", target_bir_lowering=False, num_devices=1)
    arrays, w = {}, {}
    for name in _NAMES:
        a = _np.ascontiguousarray(laid[name])
        arrays[f"in_{name}"] = a
        w[name] = nc.dram_tensor(f"in_{name}", a.shape, mybir.dt.from_np(a.dtype), kind="ExternalInput").ap()
    x = _np.ascontiguousarray(g["L0_attn_x"])
    arrays["in_x"] = x
    x_ap = nc.dram_tensor("in_x", x.shape, F32, kind="ExternalInput").ap()
    out = nc.dram_tensor("out_0", (NB, T, D), F32, kind="ExternalOutput").ap()
    rows0 = nc.dram_tensor("rows0", (1 + 2 * NS, T), F32, kind="Internal").ap()
    rows1 = nc.dram_tensor("rows1", (NS, T), F32, kind="Internal").ap()
    gates = nc.dram_tensor("gate_rows", (3, NB, D), F32, kind="Internal").ap()
    comb0 = nc.dram_tensor("comb_rows0", (NE + 1, T), F32, kind="Internal").ap()
    comb1 = nc.dram_tensor("comb_rows1", (NE, T), F32, kind="Internal").ap()
    adaln_blocks(nc, x_ap, w, rows0, rows1, comb0, comb1, gates, out)
    r = _run(nc, [arrays], core_ids=[0])
    return r.results[0]["out_0"]
```
